# Optimizing a Trainium2 kernel written in Bass

```python
import numpy as np
import jax
import jax.numpy as jnp

def _softmax(x, axis=-1):
    return jax.nn.softmax(x, axis=axis)

def _gelu(x):
    return jax.nn.gelu(x, approximate=True)

def _silu(x):
    return jax.nn.silu(x)

def _sigmoid(x):
    return jax.nn.sigmoid(x)

def _layernorm(x, axis=-1, eps=1e-05):
    m = jnp.mean(x, axis=axis, keepdims=True)
    v = jnp.var(x, axis=axis, keepdims=True)
    return (x - m) / jnp.sqrt(v + eps)

def _scatter_add(tgt, idx, src, axis=0):
    return tgt.at[idx].add(src)

def _segment_sum(src, seg, n):
    return jax.ops.segment_sum(src, seg, n)
kernel_name = 'mk_sandwich_d1_jaxref_r8_0bfde9'

def setup_inputs(seed: int=0):
    np.random.seed(seed)
    _w = jnp.asarray

    def _L0_attn_setup():
        import jax, jax.numpy as jnp
        import numpy as np
        B, T, D = (8, 512, 128)
        key = jax.random.key(seed)
        ks = jax.random.split(key, 7)
        s1 = 1.0 / np.sqrt(D)
        return {'x': jax.random.normal(ks[0], (B, T, D), dtype=jnp.float32), 'W1': jax.random.normal(ks[1], (D, D), dtype=jnp.float32) * s1, 'b1': jnp.zeros((D,), dtype=jnp.float32), 'w2': jax.random.normal(ks[2], (1, D), dtype=jnp.float32) * s1, 'b2': jnp.zeros((1,), dtype=jnp.float32), 'Wc': jax.random.normal(ks[3], (D, 2 * D), dtype=jnp.float32) * (1.0 / np.sqrt(2 * D)), 'bc': jnp.zeros((D,), dtype=jnp.float32)}
    _L0_attn_in = _L0_attn_setup()

    def _L0_ffn_setup():
        import jax, jax.numpy as jnp
        import numpy as np
        B, L, D = (4, 64, 128)
        E, TOP_K = (16, 4)
        F = 4 * D
        key = jax.random.key(seed)
        ks = jax.random.split(key, 6)
        scale = 0.02
        return {'x': jax.random.normal(ks[0], (B, L, D), jnp.float32), 'keys': jax.random.normal(ks[1], (E, D), jnp.float32), 'w1': jax.random.normal(ks[2], (E, F, D), jnp.float32) * scale, 'b1': jnp.zeros((E, F), jnp.float32), 'w2': jax.random.normal(ks[3], (E, D, F), jnp.float32) * scale, 'b2': jnp.zeros((E, D), jnp.float32), 'rw': jax.random.normal(ks[4], (E, D), jnp.float32) * scale, 'rb': jnp.zeros((E,), jnp.float32)}
    _L0_ffn_in = _L0_ffn_setup()
    _d = {'L0_attn_x': _L0_attn_in['x'], 'L0_attn_W1': _L0_attn_in['W1'], 'L0_attn_b1': _L0_attn_in['b1'], 'L0_attn_w2': _L0_attn_in['w2'], 'L0_attn_b2': _L0_attn_in['b2'], 'L0_attn_Wc': _L0_attn_in['Wc'], 'L0_attn_bc': _L0_attn_in['bc'], 'L0_ffn_keys': _L0_ffn_in['keys'], 'L0_ffn_w1': _L0_ffn_in['w1'], 'L0_ffn_b1': _L0_ffn_in['b1'], 'L0_ffn_w2': _L0_ffn_in['w2'], 'L0_ffn_b2': _L0_ffn_in['b2'], 'L0_ffn_rw': _L0_ffn_in['rw'], 'L0_ffn_rb': _L0_ffn_in['rb']}
    _x0 = _d['L0_attn_x']
    _d['L0_attn_x'] = jax.random.normal(jax.random.fold_in(jax.random.key(seed), 1), (16, 512, 128), dtype=_x0.dtype)
    del _x0
    return _d

def reference(L0_attn_x, L0_attn_W1, L0_attn_b1, L0_attn_w2, L0_attn_b2, L0_attn_Wc, L0_attn_bc, L0_ffn_keys, L0_ffn_w1, L0_ffn_b1, L0_ffn_w2, L0_ffn_b2, L0_ffn_rw, L0_ffn_rb):

    def _L0_attn_ref(x, W1, b1, w2, b2, Wc, bc):
        import jax, jax.numpy as jnp
        import numpy as np
        B, T, D = (8, 512, 128)
        h = jnp.tanh(jnp.einsum('btd,ed->bte', x, W1) + b1)
        s = (jnp.einsum('btd,od->bto', h, w2) + b2)[..., 0]
        m = jnp.max(s, axis=1, keepdims=True)
        e = jnp.exp(s - m)
        num = jnp.cumsum(e[..., None] * x, axis=1)
        den = jnp.cumsum(e, axis=1)[..., None]
        ctx = num / den
        combined = jnp.concatenate((ctx, x), axis=2)
        out = jnp.tanh(jnp.einsum('btk,dk->btd', combined, Wc) + bc)
        return out

    def _L0_ffn_ref(x, keys, w1, b1, w2, b2, rw, rb):
        import jax, jax.numpy as jnp
        import numpy as np
        B, L, D = (4, 64, 128)
        E, TOP_K = (16, 4)
        F = 4 * D
        diff = x[:, :, None, :] - keys
        dist2 = jnp.sum(diff * diff, axis=-1)
        logits = -dist2 + jnp.einsum('bld,ed->ble', x, rw) + rb
        topv, topi = jax.lax.top_k(logits, TOP_K)
        w = jax.nn.softmax(topv, axis=-1)
        hidden = jax.nn.gelu(jnp.einsum('bld,efd->blef', x, w1) + b1, approximate=False)
        exp_out = jnp.einsum('blef,edf->bled', hidden, w2) + b2
        sel = jnp.take_along_axis(exp_out, topi[..., None], axis=2)
        fused = jnp.sum(w[..., None] * sel, axis=2)
        return fused
    x = L0_attn_x
    x = x + _layernorm(_L0_attn_ref(_layernorm(x, axis=-1), L0_attn_W1, L0_attn_b1, L0_attn_w2, L0_attn_b2, L0_attn_Wc, L0_attn_bc), axis=-1)
    x = x + _layernorm(_L0_ffn_ref(_layernorm(x, axis=-1), L0_ffn_keys, L0_ffn_w1, L0_ffn_b1, L0_ffn_w2, L0_ffn_b2, L0_ffn_rw, L0_ffn_rb), axis=-1)
    return x

_drawn_inputs = setup_inputs


def setup_inputs(seed=0):
    import zlib

    import numpy as np

    out = dict(_drawn_inputs(seed))
    spreads = {'L0_attn_b1': (0.0, 0.8),
     'L0_attn_bc': (0.0, 0.1),
     'L0_ffn_b1': (0.0, 0.1),
     'L0_ffn_b2': (0.0, 0.1),
     'L0_ffn_rb': (0.0, 0.792)}
    factors = {}
    for name, (base, spread) in spreads.items():
        noise = np.random.default_rng([zlib.crc32(name.encode()), seed]).standard_normal(out[name].shape)
        drawn = base * np.exp(spread * noise) if base else spread * noise
        out[name] = jnp.asarray(drawn.astype(out[name].dtype))
    for name, factor in factors.items():
        out[name] = (out[name] * factor).astype(out[name].dtype)
    return out
```

```python
from contextlib import ExitStack

import concourse.bass as bass
from concourse import mybir

ALU = mybir.AluOpType
ACT = mybir.ActivationFunctionType
AX = mybir.AxisListType
F32 = mybir.dt.float32
F16 = mybir.dt.float16
I32 = mybir.dt.int32
U32 = mybir.dt.uint32

P = 128
D = 128
NB, T = 16, 512
TOKENS = NB * T
BT = T // P
PT = 2 * BT
PAIRS = NB // 2
NT = TOKENS // P
E, K = 16, 4
FF = 512
FC = FF // P
EPS = 1e-5

SLOTS = 256
REGION = TOKENS + SLOTS
TILES = (TOKENS * K + E * (SLOTS - 1)) // SLOTS + 1
NO_ROW = 65536
GROUP = 4
assert TILES % GROUP == 0

HI, LO = 0, D
EXPERT, DEST, WEIGHT = D, D + K, D + 2 * K
ROW = D + 16

LN_BOUND_SQ = 130.0


class Signal:

    def __init__(self, sem, credit=0, per=1):
        self.sem, self.credit, self.per = sem, credit, per

    @property
    def start(self):
        return self.credit * self.per

    def done(self, n, part=None):
        part = self.per if part is None else part + 1
        return n * self.per + (self.start + part)

    def free(self, n, bufs):
        assert bufs <= self.credit
        return n * self.per + (self.credit - bufs + 1) * self.per


class Chain:

    def __init__(self, sem, base, steps):
        self.sem, self.base, self.steps, self.n = sem, base, steps, 0

    def step(self):
        self.n += 1
        return 1

    def now(self):
        return self.base + self.n

    def end(self):
        assert self.n == self.steps, self.n


def norm_steps(v, c, stats, rstd, nmr, scr, last):
    me, m2e, mo, m2o = stats[:, :, 1], stats[:, :, 2], stats[:, :, 4], stats[:, :, 5]
    total, diff, q, var, y, a = (scr[:, k] for k in range(6))
    v.wait_ge(c.sem, c.now())
    v.tensor_tensor(total, me, mo, ALU.add).then_inc(c.sem, c.step())
    v.tensor_tensor(diff, me, mo, ALU.subtract).then_inc(c.sem, c.step())
    v.tensor_tensor(q, m2e, m2o, ALU.add).then_inc(c.sem, c.step())
    v.wait_ge(c.sem, c.now())
    v.tensor_scalar(q, q, 1.0 / D, EPS, ALU.mult, ALU.add).then_inc(c.sem, c.step())
    v.tensor_tensor(diff, diff, diff, ALU.mult).then_inc(c.sem, c.step())
    v.wait_ge(c.sem, c.now())
    v.scalar_tensor_tensor(var, diff, 0.25, q, ALU.mult, ALU.add).then_inc(c.sem, c.step())
    v.wait_ge(c.sem, c.now())
    v.tensor_single_scalar(a.bitcast(I32), var.bitcast(I32), 1, ALU.logical_shift_right).then_inc(c.sem, c.step())
    v.wait_ge(c.sem, c.now())
    v.tensor_scalar(y.bitcast(I32), a.bitcast(I32), -1.0, float(0x5F3759DF), ALU.mult, ALU.add).then_inc(c.sem, c.step())
    for n in range(3):
        v.wait_ge(c.sem, c.now())
        v.tensor_tensor(a, y, y, ALU.mult).then_inc(c.sem, c.step())
        v.wait_ge(c.sem, c.now())
        v.scalar_tensor_tensor(a, a, -0.5, var, ALU.mult, ALU.mult).then_inc(c.sem, c.step())
        v.wait_ge(c.sem, c.now())
        v.scalar_tensor_tensor(rstd if n == 2 else y, a, 1.5, y, ALU.add, ALU.mult).then_inc(c.sem, c.step())
    v.wait_ge(c.sem, c.now())
    v.scalar_tensor_tensor(nmr, total, -0.5, rstd, ALU.mult, ALU.mult).then_inc(last, 1)


NORM_STEPS = 18
ROUTE_STEPS = 22


def build(nc, x, W1, b1, w2, b2, Wc, bc, keys, fw1, fb1, fw2, fb2, rw, rb, out):
    dispatch = nc.dram_tensor("dispatch", [E * REGION + SLOTS, ROW], F32)
    expert_out = nc.dram_tensor("expert_out", [TOKENS * K, D], F32)
    x_tiles = x.rearrange("b (t p) d -> p (b t) d", p=P)
    out_tiles = out.rearrange("b (t p) d -> p (b t) d", p=P)
    w1_src = fw1.rearrange("e (c p) d -> p e c d", p=P)
    w2_src = fw2.rearrange("e d f -> d e f")

    with ExitStack() as ctx:
        def sb(name, shape, dt=F32, scope=ctx):
            return scope.enter_context(nc.sbuf_tensor(name, shape, dt))

        def pb(name, shape, dt=F32, scope=ctx):
            return scope.enter_context(nc.psum_tensor(name, shape, dt))

        def sem(name):
            return ctx.enter_context(nc.semaphore(name))

        passed = sem("passed")

        def apart(eng):
            eng.sem_inc(passed, 1)

        X = sb("X", [P, NT, D])
        R = sb("R", [P, NT, D])
        W1H = sb("W1H", [P, E, FF], F16)
        W1L = sb("W1L", [P, E, FF], F16)
        W2H = sb("W2H", [P, E, FF], F16)
        W2L = sb("W2L", [P, E, FF], F16)
        b1T = sb("b1T", [P, E * FC])
        ident = sb("ident", [P, P])
        ident16 = sb("ident16", [P, P], F16)
        ones = sb("ones", [P, P])
        ones16 = sb("ones16", [P, P], F16)
        scales = sb("scales", [P, 3])
        unscale = sb("unscale", [P, 4])
        count16 = sb("count16", [P, E], F16)

        with ExitStack() as one:
            def s1(name, shape, dt=F32):
                return sb(name, shape, dt, one)

            rstd1 = s1("rstd1", [P, NT])
            nmr1 = s1("nmr1", [P, NT])
            W1T = s1("W1T", [P, P])
            WcT = s1("WcT", [P, 2 * D])
            bc_row = s1("bc_row", [1, D])
            b1_col = s1("b1_col", [P, 1])
            b2_col = s1("b2_col", [P, 1])
            w2_col = s1("w2_col", [P, 1])
            w2_rep = s1("w2_rep", [P, P])
            upto = s1("upto", [P, P])
            before16 = s1("before16", [P, P], F16)
            LW = s1("LW", [P, E])
            neg1 = s1("neg1", [P, E])
            crow = s1("crow", [1, E])
            b2_sel = s1("b2_sel", [P, PT, D])
            iota_e = s1("iota_e", [P, E])
            region_e = s1("region_e", [P, E])
            dest = s1("dest", [P, PT, K])
            count = s1("count", [P, E])

            psA = [pb(f"psA{b}", [P, T], F32, one) for b in range(2)]
            psZ = pb("psZ", [P, BT, 2 * D], F32, one)
            psC = pb("psC", [P, BT, D], F32, one)
            psD = pb("psD", [P, 512], F32, one)
            psN = pb("psN", [P, 512], F32, one)
            psL = pb("psL", [P, 512], F32, one)

            with ExitStack() as pre_scope:
                def s0(name, shape, dt=F32):
                    return sb(name, shape, dt, pre_scope)

                stage = [s0(f"stage0_{u}", [P, 2, 2, FF]) for u in range(2)]
                W1n = s0("W1n", [P, D])
                Wcn = s0("Wcn", [P, 2 * D])
                b2_one = s0("b2_one", [1, 1])
                keys_n = s0("keys_n", [E, D])
                rw_n = s0("rw_n", [E, D])
                rb_n = s0("rb_n", [E, 1])
                key_sq = s0("key_sq", [E, D])
                key_len = s0("key_len", [E, 2])
                fb1_n = s0("fb1_n", [E * FC, P])
                fb1_sq = s0("fb1_sq", [P, E * FC])
                group_sq = s0("group_sq", [P, 2, E // 2])
                bound = s0("bound", [P, 3])
                bound_all = s0("bound_all", [P, 3])
                sbits = s0("sbits", [P, 3], I32)
                xstats = s0("xstats", [P, NT, 6])
                xscr = s0("xscr", [P, 6, NT])
                iota_i = s0("iota_i", [P, 2 * E + PT * K], I32)

                x_in = [sem(f"x_in{q}") for q in range(4)]
                small_in = sem("small_in")
                stage_in0 = [sem(f"stage_in0_{u}") for u in range(2)]
                squared = sem("squared")
                consts = sem("consts")
                masks = sem("masks")
                setup_v = sem("setup_v")
                setup_t = sem("setup_t")
                setup_p = sem("setup_p")
                setup_ready = sem("setup_ready")
                bounds_in = sem("bounds_in")
                bounds_all = sem("bounds_all")
                ln1_ready = sem("ln1_ready")
                SMALL = 12

                with nc.Block() as block:
                    @block.sync
                    def _(sp):
                        for q in range(4):
                            n = NT // 4
                            sp.dma_start(X[:, q * n:(q + 1) * n, :], x_tiles[:, q * n:(q + 1) * n, :]).then_inc(x_in[q], 16)
                        for dst, src in ((W1n[:], W1), (Wcn[:], Wc), (bc_row[:], bc.rearrange("(a n) -> a n", a=1)),
                                         (b1_col[:], b1.rearrange("(n a) -> n a", a=1)),
                                         (w2_col[:], w2.rearrange("a n -> n a")),
                                         (b2_one[:], b2.rearrange("(a n) -> a n", a=1)),
                                         (keys_n[:], keys), (rw_n[:], rw), (rb_n[:], rb.rearrange("(n a) -> n a", a=1)),
                                         (fb1_n[:], fb1.rearrange("e (c p) -> (e c) p", p=P))):
                            sp.dma_start(dst, src).then_inc(small_in, 16)
                        sp.wait_ge(masks, 8)
                        for j in range(PT):
                            sp.dma_start(b2_sel[j * E:(j + 1) * E, j, :], fb2).then_inc(small_in, 16)

                    @block.gpsimd
                    def _(pool):
                        pool.memset(ident[:], 0.0).then_inc(masks, 1)
                        pool.memset(upto[:], 1.0).then_inc(masks, 1)
                        pool.memset(b2_sel[:], 0.0).then_inc(masks, 1)
                        pool.iota(iota_i[:, 0:E], [[1, E]], base=0, channel_multiplier=0).then_inc(masks, 1)
                        pool.iota(iota_i[:, E:2 * E], [[REGION // 256, E]], base=0, channel_multiplier=0).then_inc(masks, 1)
                        pool.iota(iota_i[:, 2 * E:], [[P * K, PT], [1, K]], base=-NO_ROW, channel_multiplier=K).then_inc(masks, 1)
                        pool.wait_ge(masks, 6)
                        pool.affine_select(out=ident[:], in_=ident[:], compare_op=ALU.not_equal, fill=1.0, base=0,
                                           pattern=[[-1, P]], channel_multiplier=1).then_inc(masks, 1)
                        pool.affine_select(out=upto[:], in_=upto[:], compare_op=ALU.is_ge, fill=0.0, base=0,
                                           pattern=[[1, P]], channel_multiplier=-1).then_inc(masks, 1)
                        pool.wait_ge(bounds_in, 1)
                        pool.partition_all_reduce(bound_all[:], bound[:], P, bass.bass_isa.ReduceOp.max).then_inc(bounds_all, 1)

                    @block.scalar
                    def _(act):
                        def square(m):
                            act.wait_ge(stage_in0[m % 2], 32 * (m // 2 + 1))
                            for a in range(2):
                                flat = stage[m % 2][:, a].rearrange("p e f -> p (e f)")
                                ins = act.activation(flat, flat, ACT.Square, accum_out=group_sq[:, a, m:m + 1])
                            ins.then_inc(squared, 1)

                        for n in range(E // 2):
                            if n >= 2:
                                act.wait_ge(squared, n - 1)
                            act.dma_start(stage[n % 2][:, 0].rearrange("p e (c d) -> p e c d", c=FC),
                                          w1_src[:, 2 * n:2 * n + 2]).then_inc(stage_in0[n % 2], 16)
                            act.dma_start(stage[n % 2][:, 1], w2_src[:, 2 * n:2 * n + 2, :]).then_inc(stage_in0[n % 2], 16)
                            if n >= 1:
                                square(n - 1)
                        square(E // 2 - 1)

                    @block.vector
                    def _(v):
                        c = Chain(setup_v, 0, 0)
                        v.memset(ones[:], 1.0).then_inc(c.sem, c.step())
                        v.memset(neg1[:], -1.0).then_inc(c.sem, c.step())
                        v.memset(count[:], 0.0).then_inc(c.sem, c.step())
                        v.memset(count16[:], 0.0).then_inc(c.sem, c.step())
                        v.wait_ge(c.sem, c.now())
                        v.tensor_copy(ones16[:], ones[:]).then_inc(c.sem, c.step())
                        v.wait_ge(masks, 8)
                        v.tensor_copy(ident16[:], ident[:]).then_inc(c.sem, c.step())
                        v.tensor_tensor(before16[:], upto[:], ident[:], ALU.subtract).then_inc(c.sem, c.step())
                        v.tensor_copy(iota_e[:], iota_i[:, 0:E]).then_inc(c.sem, c.step())
                        v.tensor_copy(region_e[:], iota_i[:, E:2 * E]).then_inc(c.sem, c.step())
                        v.tensor_copy(dest[:].rearrange("p j k -> p (j k)"), iota_i[:, 2 * E:]).then_inc(c.sem, c.step())
                        v.wait_ge(c.sem, c.now())
                        v.tensor_scalar(region_e[:], region_e[:], 256.0, None, ALU.mult).then_inc(c.sem, c.step())
                        v.wait_ge(small_in, 16 * (10 + PT))
                        v.tensor_scalar(w2_rep[:], ones[:], w2_col[:, 0:1], None, ALU.mult).then_inc(c.sem, c.step())
                        v.tensor_tensor(key_sq[:], keys_n[:], keys_n[:], ALU.mult).then_inc(c.sem, c.step())
                        v.wait_ge(c.sem, c.now())
                        v.tensor_reduce(key_len[:, 0:1], key_sq[:], AX.X, ALU.add).then_inc(c.sem, c.step())
                        v.wait_ge(c.sem, c.now())
                        v.tensor_tensor(key_len[:, 1:2], rb_n[:], key_len[:, 0:1], ALU.subtract).then_inc(c.sem, c.step())
                        v.scalar_tensor_tensor(keys_n[:], keys_n[:], 2.0, rw_n[:], ALU.mult, ALU.add).then_inc(consts, 1)
                        v.wait_ge(setup_t, 1)
                        v.tensor_copy(W1T[:], psA[0][:, 0:P])
                        v.tensor_copy(WcT[:, 0:D], psA[0][:, P:2 * P])
                        v.tensor_copy(WcT[:, D:2 * D], psA[0][:, 2 * P:3 * P])
                        v.tensor_copy(b1T[:], psA[0][:, 3 * P:3 * P + E * FC])
                        v.tensor_copy(LW[:], psA[1][:, 0:E])
                        v.tensor_copy(crow[:], psA[1][0:1, E:2 * E])
                        v.tensor_copy(b2_col[:], psA[1][:, 2 * E:2 * E + 1]).then_inc(c.sem, c.step())
                        v.wait_ge(c.sem, c.now())
                        for t in range(NT):
                            if t % (NT // 4) == 0:
                                v.wait_ge(x_in[t // (NT // 4)], 16)
                            ins = v.bn_stats(xstats[:, t, :], X[:, t, :])
                        ins.then_inc(c.sem, c.step())
                        norm_steps(v, c, xstats, rstd1[:], nmr1[:], xscr, ln1_ready)
                        v.wait_ge(squared, E // 2)
                        v.tensor_tensor(fb1_sq[:], b1T[:], b1T[:], ALU.mult).then_inc(c.sem, c.step())
                        v.tensor_reduce(bound[:, 0:2], group_sq[:], AX.X, ALU.max).then_inc(c.sem, c.step())
                        v.wait_ge(c.sem, c.now())
                        v.tensor_reduce(bound[:, 2:3], fb1_sq[:], AX.X, ALU.max).then_inc(c.sem, c.step())
                        v.wait_ge(c.sem, c.now())
                        v.tensor_scalar(bound[:, 2:3], bound[:, 2:3], 2.0, None, ALU.mult).then_inc(bounds_in, 1)
                        v.wait_ge(bounds_all, 1)
                        v.scalar_tensor_tensor(bound_all[:, 2:3], bound_all[:, 0:1], 2.0 * LN_BOUND_SQ,
                                               bound_all[:, 2:3], ALU.mult, ALU.add).then_inc(c.sem, c.step())
                        v.wait_ge(c.sem, c.now())
                        v.tensor_single_scalar(sbits[:], bound_all[:].bitcast(I32), 23, ALU.logical_shift_right).then_inc(c.sem, c.step())
                        v.wait_ge(c.sem, c.now())
                        v.tensor_scalar(sbits[:], sbits[:], 1.0, None, ALU.add).then_inc(c.sem, c.step())
                        v.wait_ge(c.sem, c.now())
                        v.tensor_single_scalar(sbits[:], sbits[:], 1, ALU.logical_shift_right).then_inc(c.sem, c.step())
                        v.wait_ge(c.sem, c.now())
                        v.tensor_scalar(sbits[:], sbits[:], -1.0, 205.0, ALU.mult, ALU.add).then_inc(c.sem, c.step())
                        v.wait_ge(c.sem, c.now())
                        v.tensor_single_scalar(scales[:].bitcast(I32), sbits[:], 23, ALU.logical_shift_left).then_inc(c.sem, c.step())
                        v.wait_ge(c.sem, c.now())
                        v.reciprocal(unscale[:, 0:3], scales[:]).then_inc(c.sem, c.step())
                        v.wait_ge(c.sem, c.now())
                        v.tensor_tensor(unscale[:, 3:4], unscale[:, 1:2], unscale[:, 2:3], ALU.mult).then_inc(setup_ready, 1)

                    @block.tensor
                    def _(pe):
                        pe.wait_ge(masks, 8)
                        pe.wait_ge(consts, 1)
                        pe.wait_ge(small_in, 16 * (10 + PT))
                        pe.transpose(psA[0][:, 0:P], W1n[:], ident[:])
                        pe.transpose(psA[0][:, P:2 * P], Wcn[:, D:2 * D], ident[:])
                        pe.transpose(psA[0][:, 2 * P:3 * P], Wcn[:, 0:D], ident[:])
                        pe.transpose(psA[0][:, 3 * P:3 * P + E * FC], fb1_n[:], ident[0:E * FC, 0:E * FC])
                        pe.transpose(psA[1][:, 0:E], keys_n[:], ident[0:E, 0:E])
                        pe.transpose(psA[1][0:1, E:2 * E], key_len[:, 1:2], ident[0:E, 0:E])
                        pe.matmul(psA[1][:, 2 * E:2 * E + 1], ones[0:1, :], b2_one[:], start=True, stop=True).then_inc(setup_t, 1)

            stage = s1("stage", [P, 2, 2, FF])
            xn1 = [s1(f"xn1_{b}", [P, BT, D]) for b in range(2)]
            xT = [s1(f"xT{b}", [P, T]) for b in range(2)]
            hT = [s1(f"hT{b}", [P, T]) for b in range(2)]
            e4 = [s1(f"e4_{b}", [P, BT]) for b in range(2)]
            mx = [s1(f"mx{b}", [P, 3]) for b in range(2)]
            xproj = [s1(f"xproj{b}", [P, BT, D]) for b in range(2)]
            wctx = [s1(f"wctx{b}", [P, BT, D]) for b in range(2)]
            rden = [s1(f"rden{b}", [P, BT]) for b in range(2)]
            pre = [s1(f"pre{b}", [P, BT, D]) for b in range(2)]

            stats = s1("stats", [P, PT, 6])
            scr = s1("scr", [P, 6, PT])
            ln2 = s1("ln2", [P, 2, PT])
            ln3 = s1("ln3", [P, 2, PT])
            normed = s1("normed", [P, PT, D])
            xnT = [s1(f"xnT{h}", [P, T]) for h in range(2)]
            xnS = [s1(f"xnS{h}", [P, T]) for h in range(2)]
            logits = s1("logits", [P, PT, E])
            top = s1("top", [P, PT, 8])
            top_e = s1("top_e", [P, PT, 8], U32)
            onehot = s1("onehot", [P, PT, K, E])
            picked = s1("picked", [P, PT, K, E])
            chosen = s1("chosen", [P, PT, E])
            chosen16 = s1("chosen16", [P, PT, E], F16)
            gap4 = s1("gap4", [P, PT, K])
            gap16 = s1("gap16", [P, PT, E])
            rsum = s1("rsum", [P, 3, PT])
            wsel = s1("wsel", [P, PT, E])
            wselT = s1("wselT", [P, P])
            slot = s1("slot", [P, PT, E])
            slot4 = s1("slot4", [P, PT, K])
            pair_count = s1("pair_count", [P, E])
            rows = [s1(f"rows{u}", [P, PT, ROW]) for u in range(2)]
            rows16 = [r[:].bitcast(F16) for r in rows]
            place = [s1(f"place{u}", [P, PT * K], U32) for u in range(2)]

            stage_in = sem("stage_in")
            xn1_ready = Signal(sem("xn1_ready"))
            xT_psum = Signal(sem("xT_psum"), credit=2)
            xT_ready = Signal(sem("xT_ready"))
            h_psum = Signal(sem("h_psum"))
            hT_ready = Signal(sem("hT_ready"))
            proj_psum = Signal(sem("proj_psum"), credit=2)
            xproj_ready = Signal(sem("xproj_ready"), credit=1)
            score_rows = Signal(sem("score_rows"), credit=2)
            max_read = Signal(sem("max_read"))
            negmax_ready = Signal(sem("negmax_ready"))
            score_cols = Signal(sem("score_cols"))
            e_ready = Signal(sem("e_ready"), credit=2)
            wctx_ready = Signal(sem("wctx_ready"), credit=1)
            cum_psum = Signal(sem("cum_psum"), credit=2)
            pre_ready = Signal(sem("pre_ready"), credit=2)
            attn_ready = Signal(sem("attn_ready"), credit=2)
            ln2_ready = Signal(sem("ln2_ready"))
            ln2_applied = Signal(sem("ln2_applied"))
            ln3_ready = Signal(sem("ln3_ready"))
            xn_ready = Signal(sem("xn_ready"))
            split_ready = Signal(sem("split_ready"), credit=1)
            xnT_psum = Signal(sem("xnT_psum"), credit=1, per=2)
            xnT_ready = Signal(sem("xnT_ready"), per=2)
            logits_psum = Signal(sem("logits_psum"), credit=1)
            chosen_ready = Signal(sem("chosen_ready"))
            gaps_ready = Signal(sem("gaps_ready"))
            exps_ready = Signal(sem("exps_ready"))
            wsel_ready = Signal(sem("wsel_ready"))
            rank_psum = Signal(sem("rank_psum"))
            rows_ready = Signal(sem("rows_ready"))
            wselT_psum = Signal(sem("wselT_psum"))
            wselT_ready = Signal(sem("wselT_ready"), credit=1)
            b2_psum = Signal(sem("b2_psum"), per=2)
            b2_ready = Signal(sem("b2_ready"), credit=1, per=2)
            wT_psum = Signal(sem("wT_psum"), credit=1, per=4)
            whi_ready = Signal(sem("whi_ready"), per=4)
            wlo_ready = Signal(sem("wlo_ready"), per=4)
            scattered = [Signal(sem(f"scattered{u}"), per=16 * PT * K) for u in range(2)]
            rows_sent = Signal(sem("rows_sent"), credit=2)
            attn_steps = sem("attn_steps")
            route_steps = sem("route_steps")
            rows_clear = sem("rows_clear")

            def run(eng, attention, routing):
                def step(a, r, r_use, r_par):
                    ai = [f for f in attention] if a is not None else []
                    for part in routing:
                        if part is None:
                            if ai:
                                ai.pop(0)(a)
                        elif r is not None:
                            part(r, r_use, r_par)
                    for f in ai:
                        f(a)

                step(0, None, None, None)
                with eng.Fori(0, PAIRS // 2 - 1) as h:
                    step(h * 2 + 1, h * 2, h, 0)
                    step(h * 2 + 2, h * 2 + 1, h, 1)
                step(PAIRS - 1, PAIRS - 2, PAIRS // 2 - 1, 0)
                step(None, PAIRS - 1, PAIRS // 2 - 1, 1)

            with nc.Block() as block:
                @block.sync
                def _(sp):
                    with sp.Fori(0, PAIRS) as n:
                        sp.wait_ge(wT_psum.sem, wT_psum.free(n, 1))
                        sp.dma_start(stage[:, 0].rearrange("p e (c d) -> p e c d", c=FC),
                                     w1_src[:, bass.ds(n * 2, 2)]).then_inc(stage_in, 16)
                        sp.dma_start(stage[:, 1], w2_src[:, bass.ds(n * 2, 2), :]).then_inc(stage_in, 16)

                @block.tensor
                def _(pe):
                    pe.sem_inc(proj_psum.sem, proj_psum.start)
                    pe.sem_inc(xT_psum.sem, xT_psum.start)
                    pe.sem_inc(score_rows.sem, score_rows.start)
                    pe.sem_inc(cum_psum.sem, cum_psum.start)
                    pe.sem_inc(xnT_psum.sem, xnT_psum.start)
                    pe.sem_inc(logits_psum.sem, logits_psum.start)
                    pe.sem_inc(wT_psum.sem, wT_psum.start)

                    def turn_x(b):
                        def f(i):
                            n = i * 2 + b
                            pe.wait_ge(xn1_ready.sem, xn1_ready.done(n))
                            pe.wait_ge(e_ready.sem, e_ready.free(n, 2))
                            for t in range(BT):
                                ins = pe.transpose(psA[b][:, t * P:(t + 1) * P], xn1[b][:, t, :], ident[:])
                            ins.then_inc(xT_psum.sem, 1)
                        return f

                    def hidden(b):
                        def f(i):
                            n = i * 2 + b
                            pe.wait_ge(xT_ready.sem, xT_ready.done(n))
                            pe.matmul(psA[b][:], W1T[:], xT[b][:], start=True, stop=True).then_inc(h_psum.sem, 1)
                        return f

                    def project(b):
                        def f(i):
                            n = i * 2 + b
                            pe.wait_ge(xproj_ready.sem, xproj_ready.free(n, 1))
                            pe.wait_ge(wctx_ready.sem, wctx_ready.free(n, 1))
                            for t in range(BT):
                                pe.matmul(psZ[:, t, :], xT[b][:, t * P:(t + 1) * P], WcT[:], start=True, stop=False)
                                ins = pe.matmul(psZ[:, t, 0:D], ones[0:1, :], bc_row[:], start=False, stop=True)
                            ins.then_inc(proj_psum.sem, 1)
                        return f

                    def scores_row(b):
                        def f(i):
                            n = i * 2 + b
                            pe.wait_ge(hT_ready.sem, hT_ready.done(n))
                            pe.matmul(psA[b][:], w2_rep[:], hT[b][:], start=True, stop=True).then_inc(score_rows.sem, 1)
                        return f

                    def scores_col(b):
                        def f(i):
                            n = i * 2 + b
                            pe.wait_ge(max_read.sem, max_read.done(n))
                            for t in range(BT):
                                ins = pe.matmul(psA[b][:, t:t + 1], hT[b][:, t * P:(t + 1) * P], w2_col[:],
                                                start=True, stop=True)
                            ins.then_inc(score_cols.sem, 1)
                        return f

                    def cumulate(b):
                        def f(i):
                            n = i * 2 + b
                            pe.wait_ge(wctx_ready.sem, wctx_ready.done(n))
                            pe.wait_ge(pre_ready.sem, pre_ready.free(n, 1))
                            for s in range(BT):
                                m = upto if s == 0 else ones
                                pe.matmul(psC[:, s:, :], m[:], wctx[b][:, 0:BT - s, :], start=(s == 0), stop=(s == BT - 1))
                            for s in range(BT):
                                m = upto if s == 0 else ones
                                ins = pe.matmul(psD[:, s:BT], m[:], e4[b][:, 0:BT - s], start=(s == 0), stop=(s == BT - 1))
                            ins.then_inc(cum_psum.sem, 1)
                        return f

                    def turn_w(k):
                        def f(r, use, u):
                            if k == 0:
                                pe.wait_ge(stage_in, r * 32 + 32)
                                pe.wait_ge(b2_ready.sem, b2_ready.free(r, 1))
                            else:
                                pe.wait_ge(wlo_ready.sem, wlo_ready.done(r, k - 1))
                            for cc in range(FC):
                                ins = pe.transpose(psN[:, cc * P:(cc + 1) * P],
                                                   stage[:, k // 2, k % 2, cc * P:(cc + 1) * P], ident[:])
                            ins.then_inc(wT_psum.sem, 1)
                        return f

                    def turn_xn(h):
                        def f(r, use, u):
                            if h == 0:
                                pe.wait_ge(xn_ready.sem, xn_ready.done(r))
                                pe.wait_ge(wlo_ready.sem, wlo_ready.done(r))
                            else:
                                pe.wait_ge(xnT_ready.sem, xnT_ready.done(r, 0))
                            for t in range(BT):
                                ins = pe.transpose(psN[:, t * P:(t + 1) * P], normed[:, h * BT + t, :], ident[:])
                            ins.then_inc(xnT_psum.sem, 1)
                        return f

                    def route_logits(r, use, u):
                        pe.wait_ge(xnT_ready.sem, xnT_ready.done(r))
                        pe.wait_ge(wselT_ready.sem, wselT_ready.free(r, 1))
                        for j in range(PT):
                            o = psL[:, j * E:(j + 1) * E]
                            cols = slice((j % BT) * P, (j % BT + 1) * P)
                            pe.matmul(o, xnT[j // BT][:, cols], LW[:], start=True, stop=False)
                            pe.matmul(o, xnS[j // BT][:, cols], neg1[:], start=False, stop=False)
                            ins = pe.matmul(o, ones[0:1, :], crow[:], start=False, stop=True)
                        ins.then_inc(logits_psum.sem, 1)

                    def ranks(r, use, u):
                        pe.wait_ge(chosen_ready.sem, chosen_ready.done(r))
                        o = psL[:, 0:PT * E]
                        pe.matmul(o, before16[:], chosen16[:].rearrange("p j e -> p (j e)"), start=True, stop=False)
                        for s in range(1, PT):
                            pe.matmul(psL[:, s * E:PT * E], ones16[:], chosen16[:, 0:PT - s, :].rearrange("p j e -> p (j e)"),
                                      start=False, stop=False)
                        pe.matmul(o.rearrange("p (j e) -> p j e", e=E), ones16[:],
                                  count16[:].unsqueeze(1).to_broadcast([P, PT, E]), start=False, stop=True)\
                            .then_inc(rank_psum.sem, 1)

                    def turn_wsel(r, use, u):
                        pe.wait_ge(wsel_ready.sem, wsel_ready.done(r))
                        pe.wait_ge(rows_ready.sem, rows_ready.done(r))
                        pe.transpose(psL[:, 0:P], wsel[:].rearrange("p j e -> p (j e)"), ident[:]).then_inc(wselT_psum.sem, 1)

                    def b2_rows(h):
                        def f(r, use, u):
                            if h == 0:
                                pe.wait_ge(wselT_ready.sem, wselT_ready.done(r))
                            else:
                                pe.wait_ge(b2_ready.sem, b2_ready.done(r, 0))
                            pe.matmul(psN[:], wselT[:], b2_sel[:, h * BT:(h + 1) * BT, :].rearrange("p j d -> p (j d)"),
                                      start=True, stop=True).then_inc(b2_psum.sem, 1)
                        return f

                    attention = [turn_x(0), turn_x(1), hidden(0), hidden(1), project(0), scores_row(0), scores_row(1),
                                 scores_col(0), scores_col(1), project(1), cumulate(0), cumulate(1)]
                    routing = [None] * 7 + [turn_w(0), turn_w(1)] + [None] * 3 + [turn_w(2), turn_w(3), None,
                               turn_xn(0), turn_xn(1), route_logits, None, ranks, turn_wsel, b2_rows(0), b2_rows(1)]
                    run(pe, attention, routing)

                @block.scalar
                def _(act):
                    act.sem_inc(xproj_ready.sem, xproj_ready.start)
                    act.sem_inc(e_ready.sem, e_ready.start)
                    act.sem_inc(attn_ready.sem, attn_ready.start)
                    act.sem_inc(wselT_ready.sem, wselT_ready.start)
                    act.sem_inc(b2_ready.sem, b2_ready.start)

                    def norm1(b):
                        def f(i):
                            n = i * 2 + b
                            act.wait_ge(xT_psum.sem, xT_psum.free(n, 2))
                            apart(act)
                            for t in range(BT):
                                j = i * PT + (b * BT + t)
                                ins = act.activation(xn1[b][:, t, :], X[:, bass.ds(j, 1), :].rearrange("p a d -> p (a d)"),
                                                     ACT.Identity, bias=nmr1[:, bass.ds(j, 1)], scale=rstd1[:, bass.ds(j, 1)])
                            ins.then_inc(xn1_ready.sem, 1)
                        return f

                    def copy_xT(b):
                        def f(i):
                            n = i * 2 + b
                            act.wait_ge(xT_psum.sem, xT_psum.done(n))
                            act.wait_ge(proj_psum.sem, proj_psum.free(n, 2))
                            act.activation(xT[b][:], psA[b][:], ACT.Copy).then_inc(xT_ready.sem, 1)
                        return f

                    def tanh_h(b):
                        def f(i):
                            n = i * 2 + b
                            act.wait_ge(h_psum.sem, h_psum.done(n))
                            act.wait_ge(e_ready.sem, e_ready.free(n, 2))
                            act.activation(hT[b][:], psA[b][:], ACT.Tanh, bias=b1_col[:]).then_inc(hT_ready.sem, 1)
                        return f

                    def copy_xproj(b):
                        def f(i):
                            n = i * 2 + b
                            act.wait_ge(proj_psum.sem, proj_psum.done(n))
                            act.wait_ge(pre_ready.sem, pre_ready.free(n, 2))
                            act.activation(xproj[b][:], psZ[:, :, 0:D], ACT.Copy).then_inc(xproj_ready.sem, 1)
                        return f

                    def exp_scores(b):
                        def f(i):
                            n = i * 2 + b
                            act.wait_ge(score_cols.sem, score_cols.done(n))
                            act.wait_ge(negmax_ready.sem, negmax_ready.done(n))
                            act.wait_ge(cum_psum.sem, cum_psum.free(n, 2))
                            act.activation(e4[b][:], psA[b][:, 0:BT], ACT.Exp, bias=mx[b][:, 2:3]).then_inc(e_ready.sem, 1)
                        return f

                    def tanh_out(b):
                        def f(i):
                            n = i * 2 + b
                            act.wait_ge(pre_ready.sem, pre_ready.done(n))
                            apart(act)
                            act.activation(R[:, bass.ds(i * PT + b * BT, BT), :], pre[b][:], ACT.Tanh).then_inc(attn_ready.sem, 1)
                        return f

                    def norm2(r, use, u):
                        act.wait_ge(ln2_ready.sem, ln2_ready.done(r))
                        act.wait_ge(split_ready.sem, split_ready.free(r, 1))
                        act.wait_ge(xnT_psum.sem, xnT_psum.free(r, 1))
                        apart(act)
                        for j in range(PT):
                            ins = act.activation(normed[:, j, :], R[:, bass.ds(r * PT + j, 1), :].rearrange("p a d -> p (a d)"),
                                                 ACT.Identity, bias=ln2[:, 1, j:j + 1], scale=ln2[:, 0, j:j + 1])
                        ins.then_inc(ln2_applied.sem, 1)

                    def norm3(r, use, u):
                        act.wait_ge(ln3_ready.sem, ln3_ready.done(r))
                        apart(act)
                        for j in range(PT):
                            ins = act.activation(normed[:, j, :], X[:, bass.ds(r * PT + j, 1), :].rearrange("p a d -> p (a d)"),
                                                 ACT.Identity, bias=ln3[:, 1, j:j + 1], scale=ln3[:, 0, j:j + 1])
                        ins.then_inc(xn_ready.sem, 1)

                    def split_w(k):
                        def f(r, use, u):
                            act.wait_ge(wT_psum.sem, wT_psum.done(r, k))
                            w = (W1H if k < 2 else W2H)[:, bass.ds(r * 2 + k % 2, 1), :].rearrange("p a f -> p (a f)")
                            apart(act)
                            act.activation(w, psN[:], ACT.Copy, scale=scales[:, k // 2:k // 2 + 1]).then_inc(whi_ready.sem, 1)
                        return f

                    def copy_xnT(h):
                        def f(r, use, u):
                            act.wait_ge(xnT_psum.sem, xnT_psum.done(r, h))
                            act.wait_ge(logits_psum.sem, logits_psum.free(r, 1))
                            act.activation(xnT[h][:], psN[:], ACT.Copy)
                            act.activation(xnS[h][:], psN[:], ACT.Square).then_inc(xnT_ready.sem, 1)
                        return f

                    def exp_gaps(r, use, u):
                        act.wait_ge(gaps_ready.sem, gaps_ready.done(r))
                        act.activation(gap4[:], gap4[:], ACT.Exp)
                        act.activation(gap16[:], gap16[:], ACT.Exp).then_inc(exps_ready.sem, 1)

                    def copy_wselT(r, use, u):
                        act.wait_ge(wselT_psum.sem, wselT_psum.done(r))
                        act.activation(wselT[:], psL[:, 0:P], ACT.Copy).then_inc(wselT_ready.sem, 1)

                    def copy_b2(h):
                        def f(r, use, u):
                            act.wait_ge(b2_psum.sem, b2_psum.done(r, h))
                            apart(act)
                            act.activation(R[:, bass.ds(r * PT + h * BT, BT), :].rearrange("p j d -> p (j d)"),
                                           psN[:], ACT.Copy).then_inc(b2_ready.sem, 1)
                        return f

                    attention = [norm1(0), norm1(1), copy_xT(0), copy_xT(1), tanh_h(0), tanh_h(1), copy_xproj(0),
                                 exp_scores(0), exp_scores(1), copy_xproj(1), tanh_out(0), tanh_out(1)]
                    routing = [None] * 4 + [norm2, None, None, split_w(0), split_w(1)] + [None] * 4 + \
                              [split_w(2), split_w(3), norm3, copy_xnT(0), copy_xnT(1), None, exp_gaps, None,
                               copy_wselT, copy_b2(0), copy_b2(1)]
                    run(act, attention, routing)

                @block.vector
                def _(v):
                    v.memset(rows[0][:], 0.0)
                    v.memset(rows[1][:], 0.0).then_inc(rows_clear, 1)
                    v.wait_ge(rows_clear, 1)
                    v.sem_inc(wctx_ready.sem, wctx_ready.start)
                    v.sem_inc(pre_ready.sem, pre_ready.start)
                    v.sem_inc(split_ready.sem, split_ready.start)
                    attn_at, route_at = [None], [None]
                    ATTN = 4

                    def row_max(b):
                        def f(i):
                            n = i * 2 + b
                            if b == 0:
                                attn_at[0] = Chain(attn_steps, i * ATTN, ATTN)
                            c = attn_at[0]
                            v.wait_ge(score_rows.sem, score_rows.done(n))
                            v.wait_ge(e_ready.sem, e_ready.free(n, 2))
                            v.tensor_reduce(mx[b][:, 0:1], psA[b][:], AX.X, ALU.max).then_inc(max_read.sem, 1)
                            v.wait_ge(max_read.sem, max_read.done(n))
                            v.tensor_tensor(mx[b][:, 1:2], mx[b][:, 0:1], b2_col[:], ALU.add).then_inc(c.sem, c.step())
                            v.wait_ge(c.sem, c.now())
                            v.tensor_tensor(mx[b][:, 2:3], b2_col[:], mx[b][:, 1:2], ALU.subtract).then_inc(negmax_ready.sem, 1)
                        return f

                    def weigh(b):
                        def f(i):
                            n = i * 2 + b
                            v.wait_ge(xproj_ready.sem, xproj_ready.done(n))
                            v.wait_ge(e_ready.sem, e_ready.done(n))
                            v.wait_ge(cum_psum.sem, cum_psum.free(n, 2))
                            for t in range(BT):
                                ins = v.tensor_scalar(wctx[b][:, t, :], psZ[:, t, D:2 * D], e4[b][:, t:t + 1], None, ALU.mult)
                            ins.then_inc(wctx_ready.sem, 1)
                        return f

                    def combine(b):
                        def f(i):
                            n = i * 2 + b
                            c = attn_at[0]
                            v.wait_ge(cum_psum.sem, cum_psum.done(n))
                            v.reciprocal(rden[b][:], psD[:, 0:BT]).then_inc(c.sem, c.step())
                            v.wait_ge(c.sem, c.now())
                            v.wait_ge(xproj_ready.sem, xproj_ready.done(n))
                            v.wait_ge(attn_ready.sem, attn_ready.free(n, 2))
                            for t in range(BT):
                                ins = v.scalar_tensor_tensor(pre[b][:, t, :], psC[:, t, :], rden[b][:, t:t + 1],
                                                             xproj[b][:, t, :], ALU.mult, ALU.add)
                            ins.then_inc(pre_ready.sem, 1)
                            if b == 1:
                                c.end()
                        return f

                    def stats2(r, use, u):
                        c = route_at[0] = Chain(route_steps, r * (2 * NORM_STEPS + ROUTE_STEPS), 2 * NORM_STEPS + ROUTE_STEPS)
                        v.wait_ge(attn_ready.sem, attn_ready.done(r * 2 + 1))
                        apart(v)
                        for j in range(PT):
                            ins = v.bn_stats(stats[:, j, :], R[:, bass.ds(r * PT + j, 1), :].rearrange("p a d -> p (a d)"))
                        ins.then_inc(c.sem, c.step())
                        norm_steps(v, c, stats, ln2[:, 0, :], ln2[:, 1, :], scr, ln2_ready.sem)

                    def stats3(r, use, u):
                        c = route_at[0]
                        v.wait_ge(ln2_applied.sem, ln2_applied.done(r))
                        x2 = X[:, bass.ds(r * PT, PT), :]
                        v.tensor_tensor(x2, x2, normed[:], ALU.add).then_inc(c.sem, c.step())
                        v.wait_ge(c.sem, c.now())
                        apart(v)
                        for j in range(PT):
                            ins = v.bn_stats(stats[:, j, :], X[:, bass.ds(r * PT + j, 1), :].rearrange("p a d -> p (a d)"))
                        ins.then_inc(c.sem, c.step())
                        norm_steps(v, c, stats, ln3[:, 0, :], ln3[:, 1, :], scr, ln3_ready.sem)

                    def split_w(k):
                        def f(r, use, u):
                            v.wait_ge(whi_ready.sem, whi_ready.done(r, k))
                            h, l = (W1H, W1L) if k < 2 else (W2H, W2L)
                            at = bass.ds(r * 2 + k % 2, 1)
                            v.scalar_tensor_tensor(l[:, at, :].rearrange("p a f -> p (a f)"), psN[:], scales[:, k // 2:k // 2 + 1],
                                                   h[:, at, :].rearrange("p a f -> p (a f)"), ALU.mult, ALU.subtract)\
                                .then_inc(wlo_ready.sem, 1)
                        return f

                    def split_xn(r, use, u):
                        c = route_at[0]
                        v.wait_ge(xn_ready.sem, xn_ready.done(r))
                        v.wait_ge(rows_sent.sem, rows_sent.free(r, 2))
                        hi, lo = rows16[u][:, :, HI:HI + D], rows16[u][:, :, LO:LO + D]
                        v.tensor_copy(hi, normed[:]).then_inc(c.sem, c.step())
                        v.wait_ge(c.sem, c.now())
                        v.tensor_tensor(lo, normed[:], hi, ALU.subtract).then_inc(split_ready.sem, 1)

                    def choose(r, use, u):
                        c = route_at[0]
                        v.wait_ge(logits_psum.sem, logits_psum.done(r))
                        v.tensor_copy(logits[:].rearrange("p j e -> p (j e)"), psL[:, 0:PT * E]).then_inc(c.sem, c.step())
                        v.wait_ge(c.sem, c.now())
                        apart(v)
                        for j in range(PT):
                            ins = v.max(top[:, j, :], logits[:, j, :])
                        ins.then_inc(c.sem, c.step())
                        v.wait_ge(c.sem, c.now())
                        apart(v)
                        for j in range(PT):
                            ins = v.max_index(top_e[:, j, :], top[:, j, :], logits[:, j, :])
                        ins.then_inc(c.sem, c.step())
                        best = top[:, :, 0:1]
                        v.tensor_tensor(gap4[:], top[:, :, 0:K], best.to_broadcast([P, PT, K]), ALU.subtract).then_inc(c.sem, c.step())
                        v.tensor_tensor(gap16[:], logits[:], best.to_broadcast([P, PT, E]), ALU.subtract).then_inc(gaps_ready.sem, 1)
                        v.wait_ge(c.sem, c.now())
                        expert = rows[u][:, :, EXPERT:EXPERT + K]
                        v.tensor_copy(expert, top_e[:, :, 0:K]).then_inc(c.sem, c.step())
                        v.tensor_copy(rows[u][:, :, DEST:DEST + K], dest[:]).then_inc(c.sem, c.step())
                        v.wait_ge(c.sem, c.now())
                        v.tensor_tensor(onehot[:], iota_e[:].unsqueeze(1).unsqueeze(1).to_broadcast([P, PT, K, E]),
                                        expert.unsqueeze(3).to_broadcast([P, PT, K, E]), ALU.is_equal).then_inc(c.sem, c.step())
                        v.tensor_scalar(dest[:], dest[:], float(PT * P * K), None, ALU.add).then_inc(c.sem, c.step())
                        v.wait_ge(c.sem, c.now())
                        v.tensor_reduce(chosen[:], onehot[:].rearrange("p j k e -> p j e k"), AX.X, ALU.add).then_inc(c.sem, c.step())
                        v.wait_ge(c.sem, c.now())
                        v.tensor_copy(chosen16[:], chosen[:]).then_inc(chosen_ready.sem, 1)

                    def weights(r, use, u):
                        c = route_at[0]
                        v.wait_ge(exps_ready.sem, exps_ready.done(r))
                        total, inv, inv_out = rsum[:, 0, :], rsum[:, 1, :], rsum[:, 2, :]
                        v.tensor_reduce(total, gap4[:], AX.X, ALU.add).then_inc(c.sem, c.step())
                        v.tensor_tensor(wsel[:], gap16[:], chosen[:], ALU.mult).then_inc(c.sem, c.step())
                        v.wait_ge(c.sem, c.now())
                        v.reciprocal(inv, total).then_inc(c.sem, c.step())
                        v.wait_ge(c.sem, c.now())
                        v.tensor_scalar(inv_out, inv, unscale[:, 3:4], None, ALU.mult).then_inc(c.sem, c.step())
                        v.tensor_tensor(wsel[:], wsel[:], inv.unsqueeze(2).to_broadcast([P, PT, E]), ALU.mult).then_inc(wsel_ready.sem, 1)
                        v.wait_ge(c.sem, c.now())
                        v.tensor_tensor(rows[u][:, :, WEIGHT:WEIGHT + K], gap4[:],
                                        inv_out.unsqueeze(2).to_broadcast([P, PT, K]), ALU.mult).then_inc(c.sem, c.step())

                    def places(r, use, u):
                        c = route_at[0]
                        v.wait_ge(rank_psum.sem, rank_psum.done(r))
                        v.tensor_tensor(slot[:], psL[:, 0:PT * E].rearrange("p (j e) -> p j e", e=E),
                                        region_e[:].unsqueeze(1).to_broadcast([P, PT, E]), ALU.add).then_inc(c.sem, c.step())
                        v.tensor_reduce(pair_count[:], chosen[:].rearrange("p j e -> p e j"), AX.X, ALU.add).then_inc(c.sem, c.step())
                        v.wait_ge(c.sem, c.now())
                        v.tensor_tensor(picked[:], onehot[:], slot[:].unsqueeze(2).to_broadcast([P, PT, K, E]), ALU.mult).then_inc(c.sem, c.step())
                        v.tensor_tensor(count[:], count[:], pair_count[:], ALU.add).then_inc(c.sem, c.step())
                        v.wait_ge(c.sem, c.now())
                        v.tensor_reduce(slot4[:], picked[:], AX.X, ALU.add).then_inc(c.sem, c.step())
                        v.tensor_copy(count16[:], count[:]).then_inc(c.sem, c.step())
                        v.wait_ge(c.sem, c.now())
                        v.tensor_copy(place[u][:], slot4[:].rearrange("p j k -> p (j k)")).then_inc(rows_ready.sem, 1)
                        c.end()

                    attention = [row_max(0), row_max(1), weigh(0), weigh(1), combine(0), combine(1)]
                    routing = [stats2, None, None, stats3, split_w(0), split_w(1), None, None, split_w(2), split_w(3),
                               split_xn, None, choose, None, weights, places]
                    run(v, attention, routing)

                @block.gpsimd
                def _(pool):
                    pool.sem_inc(rows_sent.sem, rows_sent.start)

                    def send(r, u):
                        pool.wait_ge(rows_ready.sem, rows_ready.done(r))
                        apart(pool)
                        for j in range(PT):
                            for k in range(K):
                                pool.indirect_dma_start(
                                    dispatch[:, :], bass.IndirectOffsetOnAxis(ap=place[u][:, j * K + k:j * K + k + 1], axis=0),
                                    rows[u][:, j, :], None).then_inc(scattered[u].sem, 16)

                    def landed(use, u):
                        pool.wait_ge(scattered[u].sem, scattered[u].done(use))
                        pool.sem_inc(rows_sent.sem, 1)

                    send(0, 0)
                    with pool.Fori(0, PAIRS // 2 - 1) as h:
                        send(h * 2 + 1, 1)
                        landed(h, 0)
                        send(h * 2 + 2, 0)
                        landed(h, 1)
                    send(PAIRS - 1, 1)
                    landed(PAIRS // 2 - 1, 0)
                    landed(PAIRS // 2 - 1, 1)

        with ExitStack() as two:
            def s2(name, shape, dt=F32):
                return sb(name, shape, dt, two)

            tile_e = s2("tile_e", [P, TILES])
            tile_tab = s2("tile_tab", [1, 2, TILES], I32)
            with ExitStack() as tab:
                def st(name, shape, dt=F32):
                    return sb(name, shape, dt, tab)

                C = 2
                n_e = st("n_e", [P, E])
                tiles_i = st("tiles_i", [P, E], I32)
                tiles_f = st("tiles_f", [P, E])
                one_e = st("one_e", [P, E])
                end_e = st("end_e", [P, E])
                tile_i = st("tile_i", [P, C + E], I32)
                tile_n = st("tile_n", [P, C])
                past = st("past", [P, C, E])
                past_n = st("past_n", [P, C, E])
                cols = st("cols", [P, 2, C])
                before = st("before", [P, 2, C])
                spread = st("spread", [P, 2, C, P])
                pad_f = st("pad_f", [1, E])
                pad_at = st("pad_at", [1, E], I32)
                blank = st("blank", [P, 2, ROW])
                psT = pb("psT", [P, 512], F32, tab)
                psR = pb("psR", [P, 2, 256], F32, tab)
                tab_c = sem("tab_c")
                tab_count = sem("tab_count")
                tab_iota = sem("tab_iota")
                tab_spread = sem("tab_spread")
                tab_rows = sem("tab_rows")
                pads_at = sem("pads_at")
                padded = sem("padded")

                with nc.Block() as block:
                    @block.gpsimd
                    def _(pool):
                        pool.iota(tile_i[:, 0:C], [[P, C]], base=0, channel_multiplier=1).then_inc(tab_iota, 1)
                        pool.iota(tile_i[:, C:], [[REGION // 256, E]], base=0, channel_multiplier=0).then_inc(tab_iota, 1)

                    @block.tensor
                    def _(pe):
                        pe.matmul(psT[:, 0:E], ones16[:], count16[:], start=True, stop=True).then_inc(tab_count, 1)
                        pe.wait_ge(tab_spread, 1)
                        for a in range(2):
                            pe.matmul(psR[:, a, 0:P], spread[:, a, 0, :], ident[:], start=True, stop=True)
                            ins = pe.matmul(psR[:, a, P:TILES], spread[:, a, 1, :], ident[:, 0:TILES - P], start=True, stop=True)
                        ins.then_inc(tab_rows, 1)

                    @block.vector
                    def _(v):
                        c = Chain(tab_c, 0, 0)
                        v.memset(blank[:], 0.0).then_inc(c.sem, c.step())
                        v.memset(one_e[:], 1.0).then_inc(c.sem, c.step())
                        v.wait_ge(c.sem, c.now())
                        v.memset(blank[:, :, EXPERT:EXPERT + K], -1.0).then_inc(c.sem, c.step())
                        v.wait_ge(tab_count, 1)
                        v.wait_ge(tab_iota, 2)
                        v.tensor_copy(n_e[:], psT[:, 0:E]).then_inc(c.sem, c.step())
                        v.tensor_copy(tile_n[:], tile_i[:, 0:C]).then_inc(c.sem, c.step())
                        v.tensor_copy(pad_f[:], tile_i[0:1, C:]).then_inc(c.sem, c.step())
                        v.wait_ge(c.sem, c.now())
                        v.scalar_tensor_tensor(pad_f[:], pad_f[:], 256.0, n_e[0:1, :], ALU.mult, ALU.add).then_inc(c.sem, c.step())
                        v.tensor_scalar(tiles_i[:], n_e[:], float(SLOTS - 1), None, ALU.add).then_inc(c.sem, c.step())
                        v.wait_ge(c.sem, c.now())
                        v.tensor_copy(pad_at[:], pad_f[:]).then_inc(pads_at, 1)
                        v.tensor_single_scalar(tiles_i[:], tiles_i[:], 8, ALU.logical_shift_right).then_inc(c.sem, c.step())
                        v.wait_ge(c.sem, c.now())
                        v.tensor_copy(tiles_f[:], tiles_i[:]).then_inc(c.sem, c.step())
                        v.wait_ge(c.sem, c.now())
                        v.tensor_tensor_scan(end_e[:], one_e[:], tiles_f[:], 0.0, ALU.mult, ALU.add).then_inc(c.sem, c.step())
                        v.wait_ge(c.sem, c.now())
                        v.tensor_tensor(past[:], tile_n[:].unsqueeze(2).to_broadcast([P, C, E]),
                                        end_e[:].unsqueeze(1).to_broadcast([P, C, E]), ALU.is_ge).then_inc(c.sem, c.step())
                        v.wait_ge(c.sem, c.now())
                        v.tensor_tensor(past_n[:], past[:], tiles_f[:].unsqueeze(1).to_broadcast([P, C, E]), ALU.mult).then_inc(c.sem, c.step())
                        v.tensor_reduce(before[:, 0, :], past[:], AX.X, ALU.add).then_inc(c.sem, c.step())
                        v.wait_ge(c.sem, c.now())
                        v.tensor_reduce(before[:, 1, :], past_n[:], AX.X, ALU.add).then_inc(c.sem, c.step())
                        v.tensor_scalar(cols[:, 0, :], before[:, 0, :], float(E - 1), None, ALU.min).then_inc(c.sem, c.step())
                        v.wait_ge(c.sem, c.now())
                        v.tensor_tensor(before[:, 1, :], tile_n[:], before[:, 1, :], ALU.subtract).then_inc(c.sem, c.step())
                        v.tensor_scalar(cols[:, 1, :], before[:, 0, :], float(REGION), None, ALU.mult).then_inc(c.sem, c.step())
                        v.wait_ge(c.sem, c.now())
                        v.scalar_tensor_tensor(cols[:, 1, :], before[:, 1, :], float(SLOTS), cols[:, 1, :], ALU.mult, ALU.add).then_inc(c.sem, c.step())
                        v.wait_ge(c.sem, c.now())
                        v.tensor_scalar(cols[:, 1, :], cols[:, 1, :], float(E * REGION), None, ALU.min).then_inc(c.sem, c.step())
                        v.wait_ge(c.sem, c.now())
                        for a in range(2):
                            for b in range(C):
                                ins = v.tensor_scalar(spread[:, a, b, :], ones[:], cols[:, a, b:b + 1], None, ALU.mult)
                        ins.then_inc(tab_spread, 1)
                        v.wait_ge(tab_rows, 1)
                        v.tensor_copy(tile_e[:], psR[:, 0, 0:TILES])
                        v.tensor_copy(tile_tab[:], psR[0:1, :, 0:TILES]).then_inc(c.sem, c.step())
                        v.wait_ge(c.sem, c.now())

                    def pad(eng, experts):
                        for e in experts:
                            at = eng.value_load(pad_at[0:1, e:e + 1], min_val=e * REGION, max_val=e * REGION + TOKENS)
                            eng.dma_start(dispatch[bass.ds(at, SLOTS), :].rearrange("(h p) w -> p h w", p=P), blank[:])\
                               .then_inc(padded, 16)

                    @block.sync
                    def _(sp):
                        sp.wait_ge(pads_at, 1)
                        pad(sp, range(0, E // 2))
                        sp.dma_start(dispatch[E * REGION:E * REGION + SLOTS, :].rearrange("(h p) w -> p h w", p=P), blank[:])\
                          .then_inc(padded, 16)
                        sp.wait_ge(padded, 16 * (E + 1))

                    @block.scalar
                    def _(act):
                        act.wait_ge(pads_at, 1)
                        pad(act, range(E // 2, E))

            rows2 = [s2(f"rows2_{q}", [P, 2, ROW]) for q in range(GROUP)]
            rows2h = [r[:].bitcast(F16) for r in rows2]
            meta = [s2(f"meta{q}", [P, 2, 2]) for q in range(GROUP)]
            back = [s2(f"back{q}", [P, 2], U32) for q in range(GROUP)]
            match = s2("match", [P, 2, 2, K])
            xT16 = [s2(f"xT16_{u}", [P, 2, SLOTS], F16) for u in range(2)]
            act_h = [s2(f"act_h{u}", [P, FC, SLOTS]) for u in range(2)]
            h_hi = [s2(f"h_hi{u}", [P, FC, SLOTS], F16) for u in range(2)]
            h_lo = [s2(f"h_lo{u}", [P, FC, SLOTS], F16) for u in range(2)]
            y = [s2(f"y{q}", [P, 2, D]) for q in range(GROUP)]
            psX = [pb(f"psX{u}", [P, 2, SLOTS], F16, two) for u in range(2)]
            psU = [pb(f"psU{u}", [P, FC, SLOTS], F32, two) for u in range(2)]
            psY = [pb(f"psY{u}", [P, 512], F32, two) for u in range(2)]

            rows_in = [sem(f"rows_in{q}") for q in range(GROUP)]
            turned = Signal(sem("turned"), credit=GROUP)
            xT16_ready = Signal(sem("xT16_ready"), credit=2)
            up_psum = Signal(sem("up_psum"), credit=2, per=2)
            gelu_ready = Signal(sem("gelu_ready"), credit=2, per=2)
            h_ready = Signal(sem("h_ready"), credit=2, per=2)
            down_psum = Signal(sem("down_psum"), credit=2)
            meta_ready = Signal(sem("meta_ready"), credit=GROUP)
            y_ready = Signal(sem("y_ready"), credit=2)
            returned = [Signal(sem(f"returned{q}"), per=32) for q in range(GROUP)]
            y_sent = Signal(sem("y_sent"), credit=GROUP)
            tile_steps = sem("tile_steps")
            TSTEPS = 4

            def tiles(eng, body, ahead=0):
                with eng.Fori(0, TILES // GROUP) as h:
                    for q in range(GROUP):
                        body(h * GROUP + q, h, q)

            with nc.Block() as block:
                @block.sync
                def _(sp):
                    def load(n, h, q):
                        sp.wait_ge(turned.sem, turned.free(n, GROUP))
                        sp.wait_ge(meta_ready.sem, meta_ready.free(n, GROUP))
                        at = sp.value_load(tile_tab[0:1, 1, bass.ds(n, 1)], min_val=0, max_val=E * REGION)
                        sp.dma_start(rows2[q][:], dispatch[bass.ds(at, SLOTS), :].rearrange("(h p) w -> p h w", p=P))\
                          .then_inc(rows_in[q], 16)
                    tiles(sp, load)

                @block.tensor
                def _(pe):
                    pe.sem_inc(turned.sem, turned.start)
                    pe.sem_inc(up_psum.sem, up_psum.start)
                    pe.sem_inc(down_psum.sem, down_psum.start)

                    def turn(n, h, q):
                        u = q % 2
                        pe.wait_ge(rows_in[q], h * 16 + 16)
                        pe.wait_ge(xT16_ready.sem, xT16_ready.free(n, 2))
                        for part in range(2):
                            for s in range(2):
                                ins = pe.transpose(psX[u][:, part, s * P:(s + 1) * P], rows2h[q][:, s, part * D:(part + 1) * D],
                                                   ident16[:])
                        ins.then_inc(turned.sem, 1)

                    def up(n, h, q):
                        u = q % 2
                        pe.wait_ge(xT16_ready.sem, xT16_ready.done(n))
                        e = pe.value_load(tile_tab[0:1, 0, bass.ds(n, 1)], min_val=0, max_val=E - 1)
                        pe.wait_ge(gelu_ready.sem, gelu_ready.free(n, 2))
                        hi, lo = xT16[u][:, 0, :], xT16[u][:, 1, :]
                        for cc in range(FC):
                            wh = W1H[:, bass.ds(e, 1), cc * P:(cc + 1) * P].rearrange("p a f -> p (a f)")
                            wl = W1L[:, bass.ds(e, 1), cc * P:(cc + 1) * P].rearrange("p a f -> p (a f)")
                            pe.matmul(psU[u][:, cc, :], wh, hi, start=True, stop=False)
                            pe.matmul(psU[u][:, cc, :], wh, lo, start=False, stop=False)
                            ins = pe.matmul(psU[u][:, cc, :], wl, hi, start=False, stop=True)
                            if cc % 2:
                                ins.then_inc(up_psum.sem, 1)

                    def down(n, h, q):
                        u = q % 2
                        e = pe.value_load(tile_tab[0:1, 0, bass.ds(n, 1)], min_val=0, max_val=E - 1)
                        pe.wait_ge(h_ready.sem, h_ready.done(n))
                        pe.wait_ge(y_ready.sem, y_ready.free(n, 2))
                        for s in range(2):
                            o = psY[u][:, s * D:(s + 1) * D]
                            for cc in range(FC):
                                wh = W2H[:, bass.ds(e, 1), cc * P:(cc + 1) * P].rearrange("p a f -> p (a f)")
                                wl = W2L[:, bass.ds(e, 1), cc * P:(cc + 1) * P].rearrange("p a f -> p (a f)")
                                hh, hl = h_hi[u][:, cc, s * P:(s + 1) * P], h_lo[u][:, cc, s * P:(s + 1) * P]
                                pe.matmul(o, hh, wh, start=(cc == 0), stop=False)
                                pe.matmul(o, hh, wl, start=False, stop=False)
                                ins = pe.matmul(o, hl, wh, start=False, stop=(cc == FC - 1))
                        ins.then_inc(down_psum.sem, 1)

                    turn(0, 0, 0)
                    turn(1, 0, 1)
                    up(0, 0, 0)
                    turn(2, 0, 2)
                    up(1, 0, 1)
                    with pe.Fori(0, TILES // GROUP - 1) as h:
                        for q in range(GROUP):
                            n = h * GROUP + q
                            turn(n + 3, h + (q + 3) // GROUP, (q + 3) % GROUP)
                            up(n + 2, h + (q + 2) // GROUP, (q + 2) % GROUP)
                            down(n, h, q)
                    for n in range(TILES - GROUP, TILES):
                        if n + 3 < TILES:
                            turn(n + 3, (n + 3) // GROUP, (n + 3) % GROUP)
                        if n + 2 < TILES:
                            up(n + 2, (n + 2) // GROUP, (n + 2) % GROUP)
                        down(n, n // GROUP, n % GROUP)

                @block.scalar
                def _(act):
                    act.sem_inc(gelu_ready.sem, gelu_ready.start)
                    act.sem_inc(y_ready.sem, y_ready.start)

                    def gelu(n, h, q):
                        u = q % 2
                        e = act.value_load(tile_tab[0:1, 0, bass.ds(n, 1)], min_val=0, max_val=E - 1)
                        for part in range(2):
                            act.wait_ge(up_psum.sem, up_psum.done(n, part))
                            if part == 0:
                                act.wait_ge(h_ready.sem, h_ready.free(n, 2))
                            apart(act)
                            for cc in range(2 * part, 2 * part + 2):
                                ins = act.activation(act_h[u][:, cc, :], psU[u][:, cc, :], ACT.Gelu,
                                                     bias=b1T[:, bass.ds(e * FC + cc, 1)], scale=unscale[:, 0:1])
                            ins.then_inc(gelu_ready.sem, 1)

                    def weigh(n, h, q):
                        u = q % 2
                        act.wait_ge(down_psum.sem, down_psum.done(n))
                        act.wait_ge(meta_ready.sem, meta_ready.done(n))
                        act.wait_ge(y_sent.sem, y_sent.free(n, GROUP))
                        for s in range(2):
                            ins = act.activation(y[q][:, s, :], psY[u][:, s * D:(s + 1) * D], ACT.Copy, scale=meta[q][:, 1, s:s + 1])
                        ins.then_inc(y_ready.sem, 1)

                    gelu(0, 0, 0)
                    gelu(1, 0, 1)
                    with act.Fori(0, TILES // GROUP - 1) as h:
                        for q in range(GROUP):
                            gelu(h * GROUP + (q + 2), h + (q + 2) // GROUP, (q + 2) % GROUP)
                            weigh(h * GROUP + q, h, q)
                    for n in range(TILES - GROUP, TILES):
                        if n + 2 < TILES:
                            gelu(n + 2, (n + 2) // GROUP, (n + 2) % GROUP)
                        weigh(n, n // GROUP, n % GROUP)

                @block.vector
                def _(v):
                    v.sem_inc(xT16_ready.sem, xT16_ready.start)
                    v.sem_inc(h_ready.sem, h_ready.start)
                    v.sem_inc(meta_ready.sem, meta_ready.start)

                    def split(n, h, q, c):
                        u = q % 2
                        v.wait_ge(down_psum.sem, down_psum.free(n, 2))
                        for part in range(2):
                            v.wait_ge(gelu_ready.sem, gelu_ready.done(n, part))
                            s = slice(2 * part, 2 * part + 2)
                            v.tensor_scalar(h_hi[u][:, s, :], act_h[u][:, s, :], scales[:, 2:3], None, ALU.mult).then_inc(c.sem, c.step())
                            v.wait_ge(c.sem, c.now())
                            v.scalar_tensor_tensor(h_lo[u][:, s, :], act_h[u][:, s, :], scales[:, 2:3], h_hi[u][:, s, :],
                                                   ALU.mult, ALU.subtract).then_inc(h_ready.sem, 1)

                    def head(n, h, q, c):
                        u = q % 2
                        v.wait_ge(rows_in[q], h * 16 + 16)
                        v.wait_ge(y_sent.sem, y_sent.free(n, GROUP))
                        mine = rows2[q][:, :, EXPERT:EXPERT + K]
                        for a, word in enumerate((DEST, WEIGHT)):
                            ins = v.scalar_tensor_tensor(match[:, a], mine, tile_e[:, bass.ds(n, 1)],
                                                         rows2[q][:, :, word:word + K], ALU.is_equal, ALU.mult)
                        ins.then_inc(c.sem, c.step())
                        v.wait_ge(turned.sem, turned.done(n))
                        v.wait_ge(up_psum.sem, up_psum.free(n, 2))
                        v.tensor_copy(xT16[u][:].bitcast(F32), psX[u][:].bitcast(F32)).then_inc(xT16_ready.sem, 1)
                        v.wait_ge(c.sem, c.now())
                        v.tensor_reduce(meta[q][:], match[:], AX.X, ALU.add).then_inc(c.sem, c.step())
                        v.wait_ge(c.sem, c.now())
                        v.tensor_scalar(back[q][:], meta[q][:, 0, :], float(NO_ROW), None, ALU.add).then_inc(meta_ready.sem, 1)

                    for n in range(2):
                        head(n, 0, n, Chain(tile_steps, n * 2, 2))
                    with v.Fori(0, TILES // GROUP - 1) as h:
                        for q in range(GROUP):
                            n = h * GROUP + q
                            c = Chain(tile_steps, n * TSTEPS + 2 * 2, TSTEPS)
                            head(n + 2, h + (q + 2) // GROUP, (q + 2) % GROUP, c)
                            split(n, h, q, c)
                            c.end()
                    for n in range(TILES - GROUP, TILES):
                        c = Chain(tile_steps, n * TSTEPS + 2 * 2, TSTEPS)
                        if n + 2 < TILES:
                            head(n + 2, (n + 2) // GROUP, (n + 2) % GROUP, c)
                        else:
                            c.base -= 2 * (n + 2 - TILES)
                        split(n, n // GROUP, n % GROUP, c)

                @block.gpsimd
                def _(pool):
                    pool.sem_inc(y_sent.sem, y_sent.start)
                    last_row = pool.alloc_register("last_row")
                    pool.reg_mov(last_row, TOKENS * K - 1)
                    limit = pool.snap(last_row)

                    def send(n, q):
                        pool.wait_ge(y_ready.sem, y_ready.done(n))
                        apart(pool)
                        for s in range(2):
                            pool.indirect_dma_start(
                                expert_out[:, :], bass.IndirectOffsetOnAxis(ap=back[q][:, s:s + 1], axis=0),
                                y[q][:, s, :], None, bounds_check=limit, oob_is_err=False).then_inc(returned[q].sem, 16)

                    def landed(h, q):
                        pool.wait_ge(returned[q].sem, returned[q].done(h))
                        pool.sem_inc(y_sent.sem, 1)

                    send(0, 0)
                    send(1, 1)
                    with pool.Fori(0, TILES // GROUP - 1) as h:
                        for q in range(GROUP):
                            landed(h, q)
                            send(h * GROUP + (q + 2), (q + 2) % GROUP)
                    for q in range(GROUP):
                        landed(TILES // GROUP - 1, q)
                        if q < 2:
                            send(TILES - 2 + q, GROUP - 2 + q)

        with ExitStack() as three:
            def s3(name, shape, dt=F32):
                return sb(name, shape, dt, three)

            picks = [s3(f"picks{q}", [P, BT, K, D]) for q in range(4)]
            z = [s3(f"z{u}", [P, PT, D]) for u in range(2)]
            zn = [s3(f"zn{u}", [P, PT, D]) for u in range(2)]
            zo = [s3(f"zo{u}", [P, PT, D]) for u in range(2)]
            zstats = s3("zstats", [P, PT, 6])
            zscr = s3("zscr", [P, 6, PT])
            ln4 = [s3(f"ln4_{u}", [P, 2, PT]) for u in range(2)]
            psS = [pb(f"psS{q}", [P, BT, D], F32, three) for q in range(4)]

            picks_in = [sem(f"picks_in{q}") for q in range(4)]
            sum_psum = Signal(sem("sum_psum"), credit=4)
            z_ready = Signal(sem("z_ready"), credit=4)
            ln4_ready = Signal(sem("ln4_ready"))
            zn_ready = Signal(sem("zn_ready"), credit=2)
            zo_ready = Signal(sem("zo_ready"), credit=2)
            stored = [Signal(sem(f"stored{u}"), credit=1, per=16) for u in range(2)]
            z_steps = sem("z_steps")
            expert_tiles = expert_out[:, :].rearrange("(j p k) d -> p j k d", p=P, k=K)

            with nc.Block() as block:
                @block.sync
                def _(sp):
                    with sp.Fori(0, NB // 4) as h:
                        for q in range(4):
                            sp.wait_ge(sum_psum.sem, sum_psum.free(h * 4 + q, 4))
                            sp.dma_start(picks[q][:], expert_tiles[:, bass.ds(h * NB + q * BT, BT)]).then_inc(picks_in[q], 16)

                @block.tensor
                def _(pe):
                    pe.sem_inc(sum_psum.sem, sum_psum.start)
                    with pe.Fori(0, NB // 4) as h:
                        for q in range(4):
                            pe.wait_ge(picks_in[q], h * 16 + 16)
                            pe.wait_ge(z_ready.sem, z_ready.free(h * 4 + q, 4))
                            for k in range(K):
                                ins = pe.matmul(psS[q][:], ident[:], picks[q][:, :, k, :], start=(k == 0), stop=(k == K - 1))
                            ins.then_inc(sum_psum.sem, 1)

                @block.vector
                def _(v):
                    v.sem_inc(z_ready.sem, z_ready.start)
                    STEPS = NORM_STEPS
                    with v.Fori(0, PAIRS // 2) as h:
                        for u in range(2):
                            i = h * 2 + u
                            c = Chain(z_steps, i * STEPS, STEPS)
                            v.wait_ge(zn_ready.sem, zn_ready.free(i, 2))
                            for b in range(2):
                                q = 2 * u + b
                                v.wait_ge(sum_psum.sem, sum_psum.done(i * 2 + b))
                                v.tensor_tensor(z[u][:, b * BT:(b + 1) * BT, :], psS[q][:],
                                                R[:, bass.ds(i * PT + b * BT, BT), :], ALU.add).then_inc(z_ready.sem, 1)
                            v.wait_ge(z_ready.sem, z_ready.done(i * 2 + 1))
                            for j in range(PT):
                                ins = v.bn_stats(zstats[:, j, :], z[u][:, j, :])
                            ins.then_inc(c.sem, c.step())
                            norm_steps(v, c, zstats, ln4[u][:, 0, :], ln4[u][:, 1, :], zscr, ln4_ready.sem)
                            c.end()

                @block.scalar
                def _(act):
                    act.sem_inc(zn_ready.sem, zn_ready.start)
                    with act.Fori(0, PAIRS // 2) as h:
                        for u in range(2):
                            i = h * 2 + u
                            act.wait_ge(ln4_ready.sem, ln4_ready.done(i))
                            act.wait_ge(zo_ready.sem, zo_ready.free(i, 2))
                            for j in range(PT):
                                ins = act.activation(zn[u][:, j, :], z[u][:, j, :], ACT.Identity,
                                                     bias=ln4[u][:, 1, j:j + 1], scale=ln4[u][:, 0, j:j + 1])
                            ins.then_inc(zn_ready.sem, 1)
                            act.wait_ge(zo_ready.sem, zo_ready.done(i))
                            act.dma_start(out_tiles[:, bass.ds(i * PT, PT), :], zo[u][:]).then_inc(stored[u].sem, 16)
                    for u in range(2):
                        act.wait_ge(stored[u].sem, stored[u].done(PAIRS // 2 - 1))

                @block.gpsimd
                def _(pool):
                    pool.sem_inc(zo_ready.sem, zo_ready.start)
                    for u in range(2):
                        pool.sem_inc(stored[u].sem, stored[u].start)
                    with pool.Fori(0, PAIRS // 2) as h:
                        for u in range(2):
                            i = h * 2 + u
                            pool.wait_ge(zn_ready.sem, zn_ready.done(i))
                            pool.wait_ge(stored[u].sem, stored[u].free(h, 1))
                            pool.tensor_tensor(zo[u][:], zn[u][:], X[:, bass.ds(i * PT, PT), :], ALU.add).then_inc(zo_ready.sem, 1)


_INS = ['L0_attn_x', 'L0_attn_W1', 'L0_attn_b1', 'L0_attn_w2', 'L0_attn_b2', 'L0_attn_Wc', 'L0_attn_bc', 'L0_ffn_keys',
        'L0_ffn_w1', 'L0_ffn_b1', 'L0_ffn_w2', 'L0_ffn_b2', 'L0_ffn_rw', 'L0_ffn_rb']
_OUTS = [((NB, T, D), 'float32')]


def kernel(**inputs):
    import numpy as _np
    import concourse.bacc as _bacc
    from concourse import mybir as _mybir
    from concourse.bass_utils import run_bass_kernel_spmd as _run

    nc = _bacc.Bacc("TRN2", target_bir_lowering=False, num_devices=1)
    arrays, args = {}, []
    for name in _INS:
        a = _np.ascontiguousarray(inputs[name])
        arrays[f"in_{name}_dram"] = a
        args.append(nc.dram_tensor(f"in_{name}_dram", a.shape, _mybir.dt.from_np(a.dtype), kind="ExternalInput").ap())
    for i, (shape, dtype) in enumerate(_OUTS):
        dt = _mybir.dt.from_np(_np.dtype(dtype))
        args.append(nc.dram_tensor(f"out_{i}_dram", shape, dt, kind="ExternalOutput").ap())
    build(nc, *args)
    r = _run(nc, [arrays], core_ids=[0])
    got = tuple(r.results[0][f"out_{i}_dram"] for i in range(len(_OUTS)))
    return got[0]
```

```python
from contextlib import ExitStack

import concourse.bass as bass
from concourse import mybir

ALU = mybir.AluOpType
ACT = mybir.ActivationFunctionType
AX = mybir.AxisListType
F32 = mybir.dt.float32
F16 = mybir.dt.float16
I32 = mybir.dt.int32
U32 = mybir.dt.uint32

P = 128
D = 128
NB, T = 16, 512
TOKENS = NB * T
BT = T // P
PT = 2 * BT
PAIRS = NB // 2
NT = TOKENS // P
E, K = 16, 4
FF = 512
FC = FF // P
EPS = 1e-5

SLOTS = 256
REGION = TOKENS + SLOTS
TILES = (TOKENS * K + E * (SLOTS - 1)) // SLOTS + 1
NO_ROW = 65536
GROUP = 4
assert TILES % GROUP == 0

HI, LO = 0, D
EXPERT, DEST, WEIGHT = D, D + 2 * K, D + 3 * K
ROW = D + 4 * K

LN_BOUND_SQ = 130.0


class Signal:

    def __init__(self, sem, credit=0, per=1):
        self.sem, self.credit, self.per = sem, credit, per

    @property
    def start(self):
        return self.credit * self.per

    def done(self, n, part=None):
        part = self.per if part is None else part + 1
        return n * self.per + (self.start + part)

    def free(self, n, bufs):
        assert bufs <= self.credit
        return n * self.per + (self.credit - bufs + 1) * self.per


class Chain:

    def __init__(self, sem, base, steps):
        self.sem, self.base, self.steps, self.n = sem, base, steps, 0

    def step(self):
        self.n += 1
        return 1

    def now(self):
        return self.base + self.n

    def end(self):
        assert self.n == self.steps, self.n


def norm_steps(v, c, stats, rstd, nmr, scr, last):
    me, m2e, mo, m2o = stats[:, :, 1], stats[:, :, 2], stats[:, :, 4], stats[:, :, 5]
    total, diff, q, var, y, a = (scr[:, k] for k in range(6))
    v.wait_ge(c.sem, c.now())
    v.tensor_tensor(total, me, mo, ALU.add).then_inc(c.sem, c.step())
    v.tensor_tensor(diff, me, mo, ALU.subtract).then_inc(c.sem, c.step())
    v.tensor_tensor(q, m2e, m2o, ALU.add).then_inc(c.sem, c.step())
    v.wait_ge(c.sem, c.now())
    v.tensor_scalar(q, q, 1.0 / D, EPS, ALU.mult, ALU.add).then_inc(c.sem, c.step())
    v.tensor_tensor(diff, diff, diff, ALU.mult).then_inc(c.sem, c.step())
    v.wait_ge(c.sem, c.now())
    v.scalar_tensor_tensor(var, diff, 0.25, q, ALU.mult, ALU.add).then_inc(c.sem, c.step())
    v.wait_ge(c.sem, c.now())
    v.tensor_single_scalar(a.bitcast(I32), var.bitcast(I32), 1, ALU.logical_shift_right).then_inc(c.sem, c.step())
    v.wait_ge(c.sem, c.now())
    v.tensor_scalar(y.bitcast(I32), a.bitcast(I32), -1.0, float(0x5F3759DF), ALU.mult, ALU.add).then_inc(c.sem, c.step())
    for n in range(3):
        v.wait_ge(c.sem, c.now())
        v.tensor_tensor(a, y, y, ALU.mult).then_inc(c.sem, c.step())
        v.wait_ge(c.sem, c.now())
        v.scalar_tensor_tensor(a, a, -0.5, var, ALU.mult, ALU.mult).then_inc(c.sem, c.step())
        v.wait_ge(c.sem, c.now())
        v.scalar_tensor_tensor(rstd if n == 2 else y, a, 1.5, y, ALU.add, ALU.mult).then_inc(c.sem, c.step())
    v.wait_ge(c.sem, c.now())
    v.scalar_tensor_tensor(nmr, total, -0.5, rstd, ALU.mult, ALU.mult).then_inc(last, 1)


NORM_STEPS = 18
ROUTE_STEPS = 21


def build(nc, x, W1, b1, w2, b2, Wc, bc, keys, fw1, fb1, fw2, fb2, rw, rb, out):
    dispatch = nc.dram_tensor("dispatch", [E * REGION + SLOTS, ROW], F32)
    expert_out = nc.dram_tensor("expert_out", [TOKENS * K, D], F32)
    x_tiles = x.rearrange("b (t p) d -> p (b t) d", p=P)
    out_tiles = out.rearrange("b (t p) d -> p (b t) d", p=P)
    w1_src = fw1.rearrange("e (c p) d -> p e c d", p=P)
    w2_src = fw2.rearrange("e d f -> d e f")

    with ExitStack() as ctx:
        def sb(name, shape, dt=F32, scope=ctx):
            return scope.enter_context(nc.sbuf_tensor(name, shape, dt))

        def pb(name, shape, dt=F32, scope=ctx):
            return scope.enter_context(nc.psum_tensor(name, shape, dt))

        def sem(name):
            return ctx.enter_context(nc.semaphore(name))

        passed = sem("passed")

        def apart(eng):
            eng.sem_inc(passed, 1)

        X = sb("X", [P, NT, D])
        R = sb("R", [P, NT, D])
        W1H = sb("W1H", [P, E, FF], F16)
        W1L = sb("W1L", [P, E, FF], F16)
        W2H = sb("W2H", [P, E, FF], F16)
        W2L = sb("W2L", [P, E, FF], F16)
        b1T = sb("b1T", [P, E * FC])
        ident = sb("ident", [P, P])
        ident16 = sb("ident16", [P, P], F16)
        ones = sb("ones", [P, P])
        ones16 = sb("ones16", [P, P], F16)
        scales = sb("scales", [P, 3])
        unscale = sb("unscale", [P, 4])
        count16 = sb("count16", [P, E], F16)
        tile_e = sb("tile_e", [P, TILES])
        tile_tab = sb("tile_tab", [1, 2, TILES], I32)
        turn_experts = sb("turn_experts", [1, TILES // GROUP], I32)

        with ExitStack() as one:
            def s1(name, shape, dt=F32):
                return sb(name, shape, dt, one)

            rstd1 = s1("rstd1", [P, NT])
            nmr1 = s1("nmr1", [P, NT])
            W1T = s1("W1T", [P, P])
            WcT = s1("WcT", [P, 2 * D])
            bc_row = s1("bc_row", [1, D])
            b1_col = s1("b1_col", [P, 1])
            b2_col = s1("b2_col", [P, 1])
            w2_col = s1("w2_col", [P, 1])
            w2_rep = s1("w2_rep", [P, P])
            upto = s1("upto", [P, P])
            before16 = s1("before16", [P, P], F16)
            LW = s1("LW", [P, E])
            neg1 = s1("neg1", [P, E])
            key_bias = s1("key_bias", [E, 1])
            b2_sel = s1("b2_sel", [P, PT, D])
            iota_e = s1("iota_e", [P, E])
            region_e = s1("region_e", [P, E])
            dest = s1("dest", [P, PT, K])
            count = s1("count", [P, E])

            psA = [pb(f"psA{b}", [P, T], F32, one) for b in range(2)]
            psZ = [pb(f"psZ{b}", [P, BT, D], F32, one) for b in range(2)]
            psC = pb("psC", [P, BT, D], F32, one)
            psD = pb("psD", [P, 512], F32, one)
            DEN = BT
            psN = pb("psN", [P, 512], F32, one)
            psL = pb("psL", [P, 512], F32, one)

            with ExitStack() as pre_scope:
                def s0(name, shape, dt=F32):
                    return sb(name, shape, dt, pre_scope)

                stage = [s0(f"stage0_{u}", [P, 2, 2, FF]) for u in range(2)]
                W1n = s0("W1n", [P, D])
                Wcn = s0("Wcn", [P, 2 * D])
                b2_one = s0("b2_one", [1, 1])
                keys_n = s0("keys_n", [E, D])
                rw_n = s0("rw_n", [E, D])
                rb_n = s0("rb_n", [E, 1])
                key_sq = s0("key_sq", [E, D])
                key_len = s0("key_len", [E, 1])
                fb1_n = s0("fb1_n", [E * FC, P])
                fb1_sq = s0("fb1_sq", [P, E * FC])
                group_sq = s0("group_sq", [P, 2, E // 2])
                bound = s0("bound", [P, 3])
                bound_all = s0("bound_all", [P, 3])
                sbits = s0("sbits", [P, 3], I32)
                xstats = s0("xstats", [P, NT, 6])
                xscr = s0("xscr", [P, 6, NT])
                iota_i = s0("iota_i", [P, 2 * E + PT * K], I32)

                x_in = [sem(f"x_in{q}") for q in range(4)]
                small_in = sem("small_in")
                stage_in0 = [sem(f"stage_in0_{u}") for u in range(2)]
                squared = sem("squared")
                consts = sem("consts")
                masks = sem("masks")
                setup_v = sem("setup_v")
                setup_t = sem("setup_t")
                setup_p = sem("setup_p")
                setup_ready = sem("setup_ready")
                bounds_in = sem("bounds_in")
                bounds_all = sem("bounds_all")
                ln1_ready = sem("ln1_ready")
                SMALL = 12

                with nc.Block() as block:
                    @block.sync
                    def _(sp):
                        for q in range(4):
                            n = NT // 4
                            sp.dma_start(X[:, q * n:(q + 1) * n, :], x_tiles[:, q * n:(q + 1) * n, :]).then_inc(x_in[q], 16)
                        for dst, src in ((W1n[:], W1), (Wcn[:], Wc), (bc_row[:], bc.rearrange("(a n) -> a n", a=1)),
                                         (b1_col[:], b1.rearrange("(n a) -> n a", a=1)),
                                         (w2_col[:], w2.rearrange("a n -> n a")),
                                         (b2_one[:], b2.rearrange("(a n) -> a n", a=1)),
                                         (keys_n[:], keys), (rw_n[:], rw), (rb_n[:], rb.rearrange("(n a) -> n a", a=1)),
                                         (fb1_n[:], fb1.rearrange("e (c p) -> (e c) p", p=P))):
                            sp.dma_start(dst, src).then_inc(small_in, 16)
                        sp.wait_ge(masks, 8)
                        for j in range(PT):
                            sp.dma_start(b2_sel[j * E:(j + 1) * E, j, :], fb2).then_inc(small_in, 16)

                    @block.gpsimd
                    def _(pool):
                        pool.memset(ident[:], 0.0).then_inc(masks, 1)
                        pool.memset(upto[:], 1.0).then_inc(masks, 1)
                        pool.memset(b2_sel[:], 0.0).then_inc(masks, 1)
                        pool.iota(iota_i[:, 0:E], [[1, E]], base=0, channel_multiplier=0).then_inc(masks, 1)
                        pool.iota(iota_i[:, E:2 * E], [[REGION // 256, E]], base=0, channel_multiplier=0).then_inc(masks, 1)
                        pool.iota(iota_i[:, 2 * E:], [[P * K, PT], [1, K]], base=-NO_ROW, channel_multiplier=K).then_inc(masks, 1)
                        pool.wait_ge(masks, 6)
                        pool.affine_select(out=ident[:], in_=ident[:], compare_op=ALU.not_equal, fill=1.0, base=0,
                                           pattern=[[-1, P]], channel_multiplier=1).then_inc(masks, 1)
                        pool.affine_select(out=upto[:], in_=upto[:], compare_op=ALU.is_ge, fill=0.0, base=0,
                                           pattern=[[1, P]], channel_multiplier=-1).then_inc(masks, 1)
                        pool.wait_ge(bounds_in, 1)
                        pool.partition_all_reduce(bound_all[:], bound[:], P, bass.bass_isa.ReduceOp.max).then_inc(bounds_all, 1)

                    @block.scalar
                    def _(act):
                        def square(m):
                            act.wait_ge(stage_in0[m % 2], 32 * (m // 2 + 1))
                            for a in range(2):
                                flat = stage[m % 2][:, a].rearrange("p e f -> p (e f)")
                                ins = act.activation(flat, flat, ACT.Square, accum_out=group_sq[:, a, m:m + 1])
                            ins.then_inc(squared, 1)

                        for n in range(E // 2):
                            if n >= 2:
                                act.wait_ge(squared, n - 1)
                            act.dma_start(stage[n % 2][:, 0].rearrange("p e (c d) -> p e c d", c=FC),
                                          w1_src[:, 2 * n:2 * n + 2]).then_inc(stage_in0[n % 2], 16)
                            act.dma_start(stage[n % 2][:, 1], w2_src[:, 2 * n:2 * n + 2, :]).then_inc(stage_in0[n % 2], 16)
                            if n >= 1:
                                square(n - 1)
                        square(E // 2 - 1)

                    @block.vector
                    def _(v):
                        c = Chain(setup_v, 0, 0)
                        v.memset(ones[:], 1.0).then_inc(c.sem, c.step())
                        v.memset(neg1[:], -1.0).then_inc(c.sem, c.step())
                        v.memset(count[:], 0.0).then_inc(c.sem, c.step())
                        v.memset(count16[:], 0.0).then_inc(c.sem, c.step())
                        v.wait_ge(c.sem, c.now())
                        v.tensor_copy(ones16[:], ones[:]).then_inc(c.sem, c.step())
                        v.wait_ge(masks, 8)
                        v.tensor_copy(ident16[:], ident[:]).then_inc(c.sem, c.step())
                        v.tensor_tensor(before16[:], upto[:], ident[:], ALU.subtract).then_inc(c.sem, c.step())
                        v.tensor_copy(iota_e[:], iota_i[:, 0:E]).then_inc(c.sem, c.step())
                        v.tensor_copy(region_e[:], iota_i[:, E:2 * E]).then_inc(c.sem, c.step())
                        v.tensor_copy(dest[:].rearrange("p j k -> p (j k)"), iota_i[:, 2 * E:]).then_inc(c.sem, c.step())
                        v.wait_ge(c.sem, c.now())
                        v.tensor_scalar(region_e[:], region_e[:], 256.0, None, ALU.mult).then_inc(c.sem, c.step())
                        v.wait_ge(small_in, 16 * (10 + PT))
                        v.tensor_scalar(w2_rep[:], ones[:], w2_col[:, 0:1], None, ALU.mult).then_inc(c.sem, c.step())
                        v.tensor_tensor(key_sq[:], keys_n[:], keys_n[:], ALU.mult).then_inc(c.sem, c.step())
                        v.wait_ge(c.sem, c.now())
                        v.tensor_reduce(key_len[:], key_sq[:], AX.X, ALU.add).then_inc(c.sem, c.step())
                        v.wait_ge(c.sem, c.now())
                        v.tensor_tensor(key_bias[:], rb_n[:], key_len[:], ALU.subtract).then_inc(c.sem, c.step())
                        v.scalar_tensor_tensor(keys_n[:], keys_n[:], 2.0, rw_n[:], ALU.mult, ALU.add).then_inc(consts, 1)
                        v.wait_ge(setup_t, 1)
                        v.tensor_copy(W1T[:], psA[0][:, 0:P])
                        v.tensor_copy(WcT[:, 0:D], psA[0][:, P:2 * P])
                        v.tensor_copy(WcT[:, D:2 * D], psA[0][:, 2 * P:3 * P])
                        v.tensor_copy(b1T[:], psA[0][:, 3 * P:3 * P + E * FC])
                        v.tensor_copy(LW[:], psA[1][:, 0:E])
                        v.tensor_copy(b2_col[:], psA[1][:, 2 * E:2 * E + 1]).then_inc(c.sem, c.step())
                        v.wait_ge(c.sem, c.now())
                        for t in range(NT):
                            if t % (NT // 4) == 0:
                                v.wait_ge(x_in[t // (NT // 4)], 16)
                            ins = v.bn_stats(xstats[:, t, :], X[:, t, :])
                        ins.then_inc(c.sem, c.step())
                        norm_steps(v, c, xstats, rstd1[:], nmr1[:], xscr, ln1_ready)
                        v.wait_ge(squared, E // 2)
                        v.tensor_tensor(fb1_sq[:], b1T[:], b1T[:], ALU.mult).then_inc(c.sem, c.step())
                        v.tensor_reduce(bound[:, 0:2], group_sq[:], AX.X, ALU.max).then_inc(c.sem, c.step())
                        v.wait_ge(c.sem, c.now())
                        v.tensor_reduce(bound[:, 2:3], fb1_sq[:], AX.X, ALU.max).then_inc(c.sem, c.step())
                        v.wait_ge(c.sem, c.now())
                        v.tensor_scalar(bound[:, 2:3], bound[:, 2:3], 2.0, None, ALU.mult).then_inc(bounds_in, 1)
                        v.wait_ge(bounds_all, 1)
                        v.scalar_tensor_tensor(bound_all[:, 2:3], bound_all[:, 0:1], 2.0 * LN_BOUND_SQ,
                                               bound_all[:, 2:3], ALU.mult, ALU.add).then_inc(c.sem, c.step())
                        v.wait_ge(c.sem, c.now())
                        v.tensor_single_scalar(sbits[:], bound_all[:].bitcast(I32), 23, ALU.logical_shift_right).then_inc(c.sem, c.step())
                        v.wait_ge(c.sem, c.now())
                        v.tensor_scalar(sbits[:], sbits[:], 1.0, None, ALU.add).then_inc(c.sem, c.step())
                        v.wait_ge(c.sem, c.now())
                        v.tensor_single_scalar(sbits[:], sbits[:], 1, ALU.logical_shift_right).then_inc(c.sem, c.step())
                        v.wait_ge(c.sem, c.now())
                        v.tensor_scalar(sbits[:], sbits[:], -1.0, 205.0, ALU.mult, ALU.add).then_inc(c.sem, c.step())
                        v.wait_ge(c.sem, c.now())
                        v.tensor_single_scalar(scales[:].bitcast(I32), sbits[:], 23, ALU.logical_shift_left).then_inc(c.sem, c.step())
                        v.wait_ge(c.sem, c.now())
                        v.reciprocal(unscale[:, 0:3], scales[:]).then_inc(c.sem, c.step())
                        v.wait_ge(c.sem, c.now())
                        v.tensor_tensor(unscale[:, 3:4], unscale[:, 1:2], unscale[:, 2:3], ALU.mult).then_inc(setup_ready, 1)

                    @block.tensor
                    def _(pe):
                        pe.wait_ge(masks, 8)
                        pe.wait_ge(consts, 1)
                        pe.wait_ge(small_in, 16 * (10 + PT))
                        pe.transpose(psA[0][:, 0:P], W1n[:], ident[:])
                        pe.transpose(psA[0][:, P:2 * P], Wcn[:, D:2 * D], ident[:])
                        pe.transpose(psA[0][:, 2 * P:3 * P], Wcn[:, 0:D], ident[:])
                        pe.transpose(psA[0][:, 3 * P:3 * P + E * FC], fb1_n[:], ident[0:E * FC, 0:E * FC])
                        pe.transpose(psA[1][:, 0:E], keys_n[:], ident[0:E, 0:E])
                        pe.matmul(psA[1][:, 2 * E:2 * E + 1], ones[0:1, :], b2_one[:], start=True, stop=True).then_inc(setup_t, 1)

            stage = s1("stage", [P, 2, 2, FF])
            xn1 = [s1(f"xn1_{b}", [P, BT, D]) for b in range(2)]
            xT = [s1(f"xT{b}", [P, T]) for b in range(2)]
            hT = [s1(f"hT{b}", [P, T]) for b in range(2)]
            e4 = [s1(f"e4_{b}", [P, BT]) for b in range(2)]
            mx = [s1(f"mx{b}", [P, 3]) for b in range(2)]
            xproj = [s1(f"xproj{b}", [P, BT, D]) for b in range(2)]
            wctx = [s1(f"wctx{b}", [P, BT, D]) for b in range(2)]
            rden = [s1(f"rden{b}", [P, BT]) for b in range(2)]
            pre = [s1(f"pre{b}", [P, BT, D]) for b in range(2)]

            stats = s1("stats", [P, PT, 6])
            scr = s1("scr", [P, 6, PT])
            ln2 = s1("ln2", [P, 2, PT])
            ln3 = s1("ln3", [P, 2, PT])
            normed = s1("normed", [P, PT, D])
            xnT = [s1(f"xnT{h}", [P, T]) for h in range(2)]
            xnS = [s1(f"xnS{h}", [P, T]) for h in range(2)]
            logitsT = s1("logitsT", [E, PT * P])
            logits = s1("logits", [P, PT, E])
            top = s1("top", [P, PT, 8])
            top_e = s1("top_e", [P, PT, 8], U32)
            onehot = s1("onehot", [P, PT, K, E])
            picked = s1("picked", [P, PT, K, E])
            chosen = s1("chosen", [P, PT, E])
            chosen16 = s1("chosen16", [P, PT, E], F16)
            gap4 = s1("gap4", [P, PT, K])
            gap16 = s1("gap16", [P, PT, E])
            rsum = s1("rsum", [P, 3, PT])
            wsel = s1("wsel", [P, PT, E])
            wselT = s1("wselT", [P, P])
            slot = s1("slot", [P, PT, E])
            slot4 = s1("slot4", [P, PT, K])
            pair_count = s1("pair_count", [P, E])
            rows = [s1(f"rows{u}", [P, PT, ROW]) for u in range(2)]
            rows16 = [r[:].bitcast(F16) for r in rows]
            place = [s1(f"place{u}", [P, PT * K], U32) for u in range(2)]

            C = 2
            n_e = s1("n_e", [P, E])
            tiles_i = s1("tiles_i", [P, E], I32)
            tiles_f = s1("tiles_f", [P, E])
            one_e = s1("one_e", [P, E])
            end_e = s1("end_e", [P, E])
            tile_i = s1("tile_i", [P, C + E], I32)
            tile_n = s1("tile_n", [P, C])
            past = s1("past", [P, C, E])
            past_n = s1("past_n", [P, C, E])
            cols = s1("cols", [P, 2, C])
            before = s1("before", [P, 2, C])
            spread = stage[:, 0, 0].rearrange("p (a b t) -> p a b t", a=2, b=C)
            pad_f = s1("pad_f", [1, E])
            row_e = s1("row_e", [1, TILES // GROUP + 1, GROUP])
            packed = s1("packed", [1, TILES // GROUP])
            pad_at = s1("pad_at", [1, E], I32)
            blank = stage[:, 1, 0, 0:2 * ROW].rearrange("p (h w) -> p h w", h=2)
            tab_c = sem("tab_c")
            tab_count = sem("tab_count")
            tab_iota = sem("tab_iota")
            tab_spread = sem("tab_spread")
            tab_rows = sem("tab_rows")
            pads_at = sem("pads_at")
            padded = sem("padded")


            stage_in = sem("stage_in")
            xn1_ready = Signal(sem("xn1_ready"))
            xT_psum = Signal(sem("xT_psum"), credit=2)
            xT_ready = Signal(sem("xT_ready"))
            h_psum = Signal(sem("h_psum"))
            hT_ready = Signal(sem("hT_ready"))
            zctx_psum = Signal(sem("zctx_psum"))
            xproj_psum = Signal(sem("xproj_psum"), credit=2)
            xproj_ready = Signal(sem("xproj_ready"), credit=1)
            score_rows = Signal(sem("score_rows"), credit=2)
            max_read = Signal(sem("max_read"))
            negmax_ready = Signal(sem("negmax_ready"))
            score_cols = Signal(sem("score_cols"))
            e_ready = Signal(sem("e_ready"), credit=2)
            wctx_ready = Signal(sem("wctx_ready"), credit=2)
            cum_psum = Signal(sem("cum_psum"), credit=2)
            pre_ready = Signal(sem("pre_ready"), credit=2)
            attn_ready = Signal(sem("attn_ready"), credit=2)
            ln2_ready = Signal(sem("ln2_ready"))
            ln2_applied = Signal(sem("ln2_applied"))
            ln3_ready = Signal(sem("ln3_ready"))
            xn_ready = Signal(sem("xn_ready"))
            hi_ready = Signal(sem("hi_ready"))
            split_ready = Signal(sem("split_ready"), credit=1)
            xnT_psum = Signal(sem("xnT_psum"), credit=1, per=2)
            xnT_ready = Signal(sem("xnT_ready"), per=2)
            logitsT_psum = Signal(sem("logitsT_psum"), credit=1, per=2)
            logitsT_ready = Signal(sem("logitsT_ready"), per=2)
            logits_psum = Signal(sem("logits_psum"), credit=1)
            chosen_ready = Signal(sem("chosen_ready"))
            gaps_ready = Signal(sem("gaps_ready"))
            exps_ready = Signal(sem("exps_ready"))
            wsel_ready = Signal(sem("wsel_ready"))
            rank_psum = Signal(sem("rank_psum"))
            rows_ready = Signal(sem("rows_ready"))
            wselT_psum = Signal(sem("wselT_psum"))
            wselT_ready = Signal(sem("wselT_ready"), credit=1)
            b2_psum = Signal(sem("b2_psum"), per=2)
            b2_ready = Signal(sem("b2_ready"), credit=1, per=2)
            wT_psum = Signal(sem("wT_psum"), credit=1, per=4)
            whi_ready = Signal(sem("whi_ready"), per=4)
            wlo_ready = Signal(sem("wlo_ready"), credit=1, per=4)
            scattered = [Signal(sem(f"scattered{u}"), per=16 * PT * K) for u in range(2)]
            rows_sent = Signal(sem("rows_sent"), credit=2)
            attn_steps = sem("attn_steps")
            norms_steps = sem("norms_steps")
            route_steps = sem("route_steps")
            rows_clear = sem("rows_clear")

            def steps(eng, step):
                step(0, None, None, None, 1)
                step(1, 0, None, None, 0)
                step(2, 1, 0, None, 1)
                with eng.Fori(0, PAIRS // 2 - 2) as h:
                    step(h * 2 + 3, h * 2 + 2, h * 2 + 1, h * 2, 0)
                    step(h * 2 + 4, h * 2 + 3, h * 2 + 2, h * 2 + 1, 1)
                step(PAIRS - 1, PAIRS - 2, PAIRS - 3, PAIRS - 4, 0)
                step(None, PAIRS - 1, PAIRS - 2, PAIRS - 3, 1)
                step(None, None, PAIRS - 1, PAIRS - 2, 0)
                step(None, None, None, PAIRS - 1, 1)

            with nc.Block() as block:
                def pad(eng, experts):
                    for e in experts:
                        at = eng.value_load(pad_at[0:1, e:e + 1], min_val=e * REGION, max_val=e * REGION + TOKENS)
                        eng.dma_start(dispatch[bass.ds(at, SLOTS), :].rearrange("(h p) w -> p h w", p=P), blank)\
                           .then_inc(padded, 16)

                @block.sync
                def _(sp):
                    with sp.Fori(0, PAIRS) as n:
                        sp.wait_ge(wT_psum.sem, wT_psum.free(n, 1))
                        sp.dma_start(stage[:, 0].rearrange("p e (c d) -> p e c d", c=FC),
                                     w1_src[:, bass.ds(n * 2, 2)]).then_inc(stage_in, 16)
                        sp.dma_start(stage[:, 1], w2_src[:, bass.ds(n * 2, 2), :]).then_inc(stage_in, 16)

                    sp.wait_ge(pads_at, 1)
                    pad(sp, range(0, E // 2))
                    sp.dma_start(dispatch[E * REGION:E * REGION + SLOTS, :].rearrange("(h p) w -> p h w", p=P), blank)\
                      .then_inc(padded, 16)
                    sp.wait_ge(padded, 16 * (E + 1))

                @block.tensor
                def _(pe):
                    pe.sem_inc(xproj_psum.sem, xproj_psum.start)
                    pe.sem_inc(xT_psum.sem, xT_psum.start)
                    pe.sem_inc(score_rows.sem, score_rows.start)
                    pe.sem_inc(cum_psum.sem, cum_psum.start)
                    pe.sem_inc(xnT_psum.sem, xnT_psum.start)
                    pe.sem_inc(logits_psum.sem, logits_psum.start)
                    pe.sem_inc(logitsT_psum.sem, logitsT_psum.start)
                    pe.sem_inc(wT_psum.sem, wT_psum.start)

                    def turn_x(b, i):
                        n = i * 2 + b
                        pe.wait_ge(xn1_ready.sem, xn1_ready.done(n))
                        pe.wait_ge(pre_ready.sem, pre_ready.free(n, 2))
                        for t in range(BT):
                            ins = pe.transpose(psA[b][:, t * P:(t + 1) * P], xn1[b][:, t, :], ident[:])
                        ins.then_inc(xT_psum.sem, 1)

                    def hidden(b, i):
                        n = i * 2 + b
                        pe.wait_ge(xT_ready.sem, xT_ready.done(n))
                        pe.matmul(psA[b][:], W1T[:], xT[b][:], start=True, stop=True).then_inc(h_psum.sem, 1)

                    def project_ctx(b, i):
                        n = i * 2 + b
                        pe.wait_ge(wctx_ready.sem, wctx_ready.free(n, 2))
                        for t in range(BT):
                            ins = pe.matmul(psZ[b][:, t, :], xT[b][:, t * P:(t + 1) * P], WcT[:, D:2 * D], start=True, stop=True)
                        ins.then_inc(zctx_psum.sem, 1)

                    def project_x(b, i):
                        n = i * 2 + b
                        pe.wait_ge(xproj_ready.sem, xproj_ready.free(n, 1))
                        for t in range(BT):
                            o = psD[:, t * D:(t + 1) * D]
                            pe.matmul(o, xT[b][:, t * P:(t + 1) * P], WcT[:, 0:D], start=True, stop=False)
                            ins = pe.matmul(o, ones[0:1, :], bc_row[:], start=False, stop=True)
                        ins.then_inc(xproj_psum.sem, 1)

                    def scores_row(b, i):
                        n = i * 2 + b
                        pe.wait_ge(hT_ready.sem, hT_ready.done(n))
                        pe.matmul(psA[b][:], w2_rep[:], hT[b][:], start=True, stop=True).then_inc(score_rows.sem, 1)

                    def scores_col(b, i):
                        n = i * 2 + b
                        pe.wait_ge(max_read.sem, max_read.done(n))
                        for t in range(BT):
                            ins = pe.matmul(psA[b][:, t:t + 1], hT[b][:, t * P:(t + 1) * P], w2_col[:],
                                            start=True, stop=True)
                        ins.then_inc(score_cols.sem, 1)

                    def cumulate(b, i):
                        n = i * 2 + b
                        pe.wait_ge(wctx_ready.sem, wctx_ready.done(n))
                        pe.wait_ge(pre_ready.sem, pre_ready.free(n, 1))
                        for s in range(BT):
                            m = upto if s == 0 else ones
                            pe.matmul(psC[:, s:, :], m[:], wctx[b][:, 0:BT - s, :], start=(s == 0), stop=(s == BT - 1))
                        for s in range(BT):
                            m = upto if s == 0 else ones
                            ins = pe.matmul(psA[b][:, DEN + s:DEN + BT], m[:], e4[b][:, 0:BT - s], start=(s == 0), stop=(s == BT - 1))
                        ins.then_inc(cum_psum.sem, 1)

                    def turn_w(k, r):
                        if k == 0:
                            pe.wait_ge(stage_in, r * 32 + 32)
                            pe.wait_ge(wlo_ready.sem, wlo_ready.free(r, 1))
                        else:
                            pe.wait_ge(wlo_ready.sem, wlo_ready.done(r, k - 1))
                        for cc in range(FC):
                            ins = pe.transpose(psN[:, cc * P:(cc + 1) * P],
                                               stage[:, k // 2, k % 2, cc * P:(cc + 1) * P], ident[:])
                        ins.then_inc(wT_psum.sem, 1)

                    def turn_xn(h, r):
                        if h == 0:
                            pe.wait_ge(xn_ready.sem, xn_ready.done(r))
                            pe.wait_ge(b2_ready.sem, b2_ready.free(r, 1))
                            if not (isinstance(r, int) and r == PAIRS - 1):
                                pe.wait_ge(xproj_ready.sem, xproj_ready.done(r * 2 + 3))
                        else:
                            pe.wait_ge(xnT_ready.sem, xnT_ready.done(r, 0))
                        for t in range(BT):
                            ins = pe.transpose(psD[:, t * P:(t + 1) * P], normed[:, h * BT + t, :], ident[:])
                        ins.then_inc(xnT_psum.sem, 1)

                    def route_logits(h, r):
                        if h == 0:
                            pe.wait_ge(xnT_ready.sem, xnT_ready.done(r))
                        else:
                            pe.wait_ge(logitsT_ready.sem, logitsT_ready.done(r, 0))
                        pe.matmul(psD[0:E, :], LW[:], xnT[h][:], start=True, stop=False)
                        pe.matmul(psD[0:E, :], neg1[:], xnS[h][:], start=False, stop=True).then_inc(logitsT_psum.sem, 1)

                    def turn_logits(r):
                        pe.wait_ge(logitsT_ready.sem, logitsT_ready.done(r))
                        pe.wait_ge(wselT_ready.sem, wselT_ready.free(r, 1))
                        apart(pe)
                        for j in range(PT):
                            ins = pe.transpose(psL[:, j * E:(j + 1) * E], logitsT[:, j * P:(j + 1) * P], ident[0:E, 0:E])
                        ins.then_inc(logits_psum.sem, 1)

                    def ranks(r):
                        pe.wait_ge(chosen_ready.sem, chosen_ready.done(r))
                        o = psL[:, 0:PT * E]
                        pe.matmul(o, before16[:], chosen16[:].rearrange("p j e -> p (j e)"), start=True, stop=False)
                        for s in range(1, PT):
                            pe.matmul(psL[:, s * E:PT * E], ones16[:], chosen16[:, 0:PT - s, :].rearrange("p j e -> p (j e)"),
                                      start=False, stop=False)
                        pe.matmul(o.rearrange("p (j e) -> p j e", e=E), ones16[:],
                                  count16[:].unsqueeze(1).to_broadcast([P, PT, E]), start=False, stop=True)\
                            .then_inc(rank_psum.sem, 1)

                    def turn_wsel(r):
                        pe.wait_ge(wsel_ready.sem, wsel_ready.done(r))
                        pe.wait_ge(rows_ready.sem, rows_ready.done(r))
                        pe.transpose(psL[:, 0:P], wsel[:].rearrange("p j e -> p (j e)"), ident[:]).then_inc(wselT_psum.sem, 1)

                    def b2_rows(h, r):
                        if h == 0:
                            if not (isinstance(r, int) and r >= PAIRS - 2):
                                pe.wait_ge(xproj_ready.sem, xproj_ready.done(r * 2 + 5))
                            pe.wait_ge(wselT_ready.sem, wselT_ready.done(r))
                        else:
                            pe.wait_ge(b2_ready.sem, b2_ready.done(r, 0))
                        pe.matmul(psD[:], wselT[:], b2_sel[:, h * BT:(h + 1) * BT, :].rearrange("p j d -> p (j d)"),
                                  start=True, stop=True).then_inc(b2_psum.sem, 1)

                    def step(x, i, n, c, u):
                        if c is not None:
                            turn_xn(0, c)
                        if i is not None:
                            turn_x(0, i)
                            turn_x(1, i)
                        if c is not None:
                            turn_xn(1, c)
                        if i is not None:
                            hidden(0, i)
                            hidden(1, i)
                        if c is not None:
                            route_logits(0, c)
                        if i is not None:
                            scores_row(0, i)
                            scores_row(1, i)
                        if c is not None:
                            route_logits(1, c)
                        if i is not None:
                            project_ctx(0, i)
                            project_ctx(1, i)
                            scores_col(0, i)
                            scores_col(1, i)
                        if c is not None:
                            turn_logits(c)
                        if i is not None:
                            turn_w(0, i)
                            project_x(0, i)
                            turn_w(1, i)
                            project_x(1, i)
                        if c is not None:
                            ranks(c)
                        if i is not None:
                            cumulate(0, i)
                            turn_w(2, i)
                        if c is not None:
                            turn_wsel(c)
                        if i is not None:
                            cumulate(1, i)
                        if c is not None:
                            b2_rows(0, c)
                        if i is not None:
                            turn_w(3, i)
                        if c is not None:
                            b2_rows(1, c)

                    steps(pe, step)

                    table = psC[:].rearrange("p (a b) d -> p a (b d)", a=2)
                    pe.wait_ge(rows_ready.sem, rows_ready.done(PAIRS - 1))
                    pe.wait_ge(pre_ready.sem, pre_ready.done(NB - 1))
                    pe.matmul(psA[0][:, 0:E], ones16[:], count16[:], start=True, stop=True).then_inc(tab_count, 1)
                    pe.wait_ge(tab_spread, 1)
                    for a in range(2):
                        pe.matmul(table[:, a, 0:P], spread[:, a, 0, :], ident[:], start=True, stop=True)
                        ins = pe.matmul(table[:, a, P:TILES], spread[:, a, 1, :], ident[:, 0:TILES - P], start=True, stop=True)
                    ins.then_inc(tab_rows, 1)

                @block.scalar
                def _(act):
                    act.sem_inc(xproj_ready.sem, xproj_ready.start)
                    act.sem_inc(wctx_ready.sem, wctx_ready.start)
                    act.sem_inc(e_ready.sem, e_ready.start)
                    act.sem_inc(attn_ready.sem, attn_ready.start)
                    act.sem_inc(wselT_ready.sem, wselT_ready.start)
                    act.sem_inc(b2_ready.sem, b2_ready.start)

                    def norm1(b, i):
                        n = i * 2 + b
                        act.wait_ge(xT_psum.sem, xT_psum.free(n, 2))
                        apart(act)
                        for t in range(BT):
                            j = i * PT + (b * BT + t)
                            ins = act.activation(xn1[b][:, t, :], X[:, bass.ds(j, 1), :].rearrange("p a d -> p (a d)"),
                                                 ACT.Identity, bias=nmr1[:, bass.ds(j, 1)], scale=rstd1[:, bass.ds(j, 1)])
                        ins.then_inc(xn1_ready.sem, 1)

                    def copy_xT(b, i):
                        n = i * 2 + b
                        act.wait_ge(xT_psum.sem, xT_psum.done(n))
                        act.wait_ge(xproj_psum.sem, xproj_psum.free(n, 2))
                        act.activation(xT[b][:], psA[b][:], ACT.Copy).then_inc(xT_ready.sem, 1)

                    def tanh_h(b, i):
                        n = i * 2 + b
                        act.wait_ge(h_psum.sem, h_psum.done(n))
                        act.wait_ge(e_ready.sem, e_ready.free(n, 2))
                        act.activation(hT[b][:], psA[b][:], ACT.Tanh, bias=b1_col[:]).then_inc(hT_ready.sem, 1)

                    def copy_xproj(b, i):
                        n = i * 2 + b
                        act.wait_ge(xproj_psum.sem, xproj_psum.done(n))
                        act.wait_ge(pre_ready.sem, pre_ready.free(n, 2))
                        act.activation(xproj[b][:].rearrange("p t d -> p (t d)"), psD[:], ACT.Copy).then_inc(xproj_ready.sem, 1)

                    def exp_scores(b, i):
                        n = i * 2 + b
                        act.wait_ge(score_cols.sem, score_cols.done(n))
                        act.wait_ge(negmax_ready.sem, negmax_ready.done(n))
                        act.wait_ge(cum_psum.sem, cum_psum.free(n, 2))
                        act.activation(e4[b][:], psA[b][:, 0:BT], ACT.Exp, bias=mx[b][:, 2:3]).then_inc(e_ready.sem, 1)

                    def weigh(b, i):
                        n = i * 2 + b
                        act.wait_ge(e_ready.sem, e_ready.done(n))
                        act.wait_ge(zctx_psum.sem, zctx_psum.done(n))
                        act.wait_ge(cum_psum.sem, cum_psum.free(n, 2))
                        for t in range(BT):
                            ins = act.activation(wctx[b][:, t, :], psZ[b][:, t, :], ACT.Copy, scale=e4[b][:, t:t + 1])
                        ins.then_inc(wctx_ready.sem, 1)

                    def tanh_out(b, i):
                        n = i * 2 + b
                        act.wait_ge(pre_ready.sem, pre_ready.done(n))
                        apart(act)
                        act.activation(R[:, bass.ds(i * PT + b * BT, BT), :], pre[b][:], ACT.Tanh).then_inc(attn_ready.sem, 1)

                    def norm2(r):
                        act.wait_ge(ln2_ready.sem, ln2_ready.done(r))
                        act.wait_ge(split_ready.sem, split_ready.free(r, 1))
                        act.wait_ge(xnT_psum.sem, xnT_psum.free(r, 1))
                        apart(act)
                        for j in range(PT):
                            ins = act.activation(normed[:, j, :], R[:, bass.ds(r * PT + j, 1), :].rearrange("p a d -> p (a d)"),
                                                 ACT.Identity, bias=ln2[:, 1, j:j + 1], scale=ln2[:, 0, j:j + 1])
                        ins.then_inc(ln2_applied.sem, 1)

                    def norm3(r):
                        act.wait_ge(ln3_ready.sem, ln3_ready.done(r))
                        apart(act)
                        for j in range(PT):
                            ins = act.activation(normed[:, j, :], X[:, bass.ds(r * PT + j, 1), :].rearrange("p a d -> p (a d)"),
                                                 ACT.Identity, bias=ln3[:, 1, j:j + 1], scale=ln3[:, 0, j:j + 1])
                        ins.then_inc(xn_ready.sem, 1)

                    def high_xn(r, u):
                        act.wait_ge(xn_ready.sem, xn_ready.done(r))
                        act.wait_ge(rows_sent.sem, rows_sent.free(r, 2))
                        act.activation(rows16[u][:, :, HI:HI + D], normed[:], ACT.Copy).then_inc(hi_ready.sem, 1)

                    def split_w(k, r):
                        act.wait_ge(wT_psum.sem, wT_psum.done(r, k))
                        w = (W1H if k < 2 else W2H)[:, bass.ds(r * 2 + k % 2, 1), :].rearrange("p a f -> p (a f)")
                        apart(act)
                        act.activation(w, psN[:], ACT.Copy, scale=scales[:, k // 2:k // 2 + 1]).then_inc(whi_ready.sem, 1)

                    def copy_xnT(h, r):
                        act.wait_ge(xnT_psum.sem, xnT_psum.done(r, h))
                        act.wait_ge(logitsT_psum.sem, logitsT_psum.free(r, 1))
                        act.activation(xnT[h][:], psD[:], ACT.Copy)
                        act.activation(xnS[h][:], psD[:], ACT.Square).then_inc(xnT_ready.sem, 1)

                    def copy_logitsT(h, r):
                        act.wait_ge(logitsT_psum.sem, logitsT_psum.done(r, h))
                        act.wait_ge(logits_psum.sem, logits_psum.free(r, 1))
                        act.activation(logitsT[:, h * T:(h + 1) * T], psD[0:E, :], ACT.Identity, bias=key_bias[:])\
                            .then_inc(logitsT_ready.sem, 1)

                    def exp_gaps(r):
                        act.wait_ge(gaps_ready.sem, gaps_ready.done(r))
                        act.activation(gap4[:], gap4[:], ACT.Exp)
                        act.activation(gap16[:], gap16[:], ACT.Exp).then_inc(exps_ready.sem, 1)

                    def copy_wselT(r):
                        act.wait_ge(wselT_psum.sem, wselT_psum.done(r))
                        act.activation(wselT[:], psL[:, 0:P], ACT.Copy).then_inc(wselT_ready.sem, 1)

                    def copy_b2(h, r):
                        act.wait_ge(b2_psum.sem, b2_psum.done(r, h))
                        apart(act)
                        act.activation(R[:, bass.ds(r * PT + h * BT, BT), :].rearrange("p j d -> p (j d)"),
                                       psD[:], ACT.Copy).then_inc(b2_ready.sem, 1)

                    def step(x, i, n, c, u):
                        if c is not None:
                            copy_xnT(0, c)
                        if i is not None:
                            copy_xT(0, i)
                            copy_xT(1, i)
                        if c is not None:
                            copy_xnT(1, c)
                        if i is not None:
                            tanh_h(0, i)
                            tanh_h(1, i)
                        if n is not None:
                            norm2(n)
                        if c is not None:
                            copy_logitsT(0, c)
                            copy_logitsT(1, c)
                        if i is not None:
                            exp_scores(0, i)
                            weigh(0, i)
                            exp_scores(1, i)
                            weigh(1, i)
                            split_w(0, i)
                            copy_xproj(0, i)
                        if n is not None:
                            norm3(n)
                        if i is not None:
                            split_w(1, i)
                            copy_xproj(1, i)
                        if c is not None:
                            exp_gaps(c)
                        if i is not None:
                            split_w(2, i)
                        if c is not None:
                            copy_wselT(c)
                        if i is not None:
                            tanh_out(0, i)
                        if x is not None:
                            norm1(0, x)
                        if n is not None:
                            high_xn(n, 1 - u)
                        if c is not None:
                            copy_b2(0, c)
                        if i is not None:
                            tanh_out(1, i)
                            split_w(3, i)
                        if c is not None:
                            copy_b2(1, c)
                        if x is not None:
                            norm1(1, x)

                    steps(act, step)

                    act.wait_ge(pads_at, 1)
                    pad(act, range(E // 2, E))

                @block.vector
                def _(v):
                    v.memset(rows[0][:], 0.0)
                    v.memset(rows[1][:], 0.0).then_inc(rows_clear, 1)
                    v.wait_ge(rows_clear, 1)
                    v.sem_inc(pre_ready.sem, pre_ready.start)
                    v.sem_inc(split_ready.sem, split_ready.start)
                    v.sem_inc(wlo_ready.sem, wlo_ready.start)
                    attn_at, norm_at, route_at = [None], [None], [None]
                    ATTN = 4

                    def row_max(b, i):
                        n = i * 2 + b
                        if b == 0:
                            attn_at[0] = Chain(attn_steps, i * ATTN, ATTN)
                        c = attn_at[0]
                        v.wait_ge(score_rows.sem, score_rows.done(n))
                        v.wait_ge(e_ready.sem, e_ready.free(n, 2))
                        v.tensor_reduce(mx[b][:, 0:1], psA[b][:], AX.X, ALU.max).then_inc(max_read.sem, 1)
                        v.wait_ge(max_read.sem, max_read.done(n))
                        v.tensor_tensor(mx[b][:, 1:2], mx[b][:, 0:1], b2_col[:], ALU.add).then_inc(c.sem, c.step())
                        v.wait_ge(c.sem, c.now())
                        v.tensor_tensor(mx[b][:, 2:3], b2_col[:], mx[b][:, 1:2], ALU.subtract).then_inc(negmax_ready.sem, 1)

                    def combine(b, i):
                        n = i * 2 + b
                        c = attn_at[0]
                        v.wait_ge(cum_psum.sem, cum_psum.done(n))
                        v.reciprocal(rden[b][:], psA[b][:, DEN:DEN + BT]).then_inc(c.sem, c.step())
                        v.wait_ge(c.sem, c.now())
                        v.wait_ge(xproj_ready.sem, xproj_ready.done(n))
                        v.wait_ge(attn_ready.sem, attn_ready.free(n, 2))
                        for t in range(BT):
                            ins = v.scalar_tensor_tensor(pre[b][:, t, :], psC[:, t, :], rden[b][:, t:t + 1],
                                                         xproj[b][:, t, :], ALU.mult, ALU.add)
                        ins.then_inc(pre_ready.sem, 1)
                        if b == 1:
                            c.end()

                    def stats2(r):
                        c = norm_at[0] = Chain(norms_steps, r * (2 * NORM_STEPS + 1), 2 * NORM_STEPS + 1)
                        v.wait_ge(attn_ready.sem, attn_ready.done(r * 2 + 1))
                        apart(v)
                        for j in range(PT):
                            ins = v.bn_stats(stats[:, j, :], R[:, bass.ds(r * PT + j, 1), :].rearrange("p a d -> p (a d)"))
                        ins.then_inc(c.sem, c.step())
                        norm_steps(v, c, stats, ln2[:, 0, :], ln2[:, 1, :], scr, ln2_ready.sem)

                    def stats3(r):
                        c = norm_at[0]
                        v.wait_ge(ln2_applied.sem, ln2_applied.done(r))
                        x2 = X[:, bass.ds(r * PT, PT), :]
                        v.tensor_tensor(x2, x2, normed[:], ALU.add).then_inc(c.sem, c.step())
                        v.wait_ge(c.sem, c.now())
                        apart(v)
                        for j in range(PT):
                            ins = v.bn_stats(stats[:, j, :], X[:, bass.ds(r * PT + j, 1), :].rearrange("p a d -> p (a d)"))
                        ins.then_inc(c.sem, c.step())
                        norm_steps(v, c, stats, ln3[:, 0, :], ln3[:, 1, :], scr, ln3_ready.sem)

                    def split_w(k, r):
                        v.wait_ge(whi_ready.sem, whi_ready.done(r, k))
                        h, l = (W1H, W1L) if k < 2 else (W2H, W2L)
                        at = bass.ds(r * 2 + k % 2, 1)
                        v.scalar_tensor_tensor(l[:, at, :].rearrange("p a f -> p (a f)"), psN[:], scales[:, k // 2:k // 2 + 1],
                                               h[:, at, :].rearrange("p a f -> p (a f)"), ALU.mult, ALU.subtract)\
                            .then_inc(wlo_ready.sem, 1)

                    def split_xn(r, u):
                        c = norm_at[0]
                        v.wait_ge(hi_ready.sem, hi_ready.done(r))
                        v.tensor_tensor(rows16[u][:, :, LO:LO + D], normed[:], rows16[u][:, :, HI:HI + D], ALU.subtract)\
                            .then_inc(split_ready.sem, 1)
                        c.end()

                    def choose(r, u):
                        c = route_at[0] = Chain(route_steps, r * ROUTE_STEPS, ROUTE_STEPS)
                        v.wait_ge(logits_psum.sem, logits_psum.done(r))
                        v.tensor_copy(logits[:].rearrange("p j e -> p (j e)"), psL[:, 0:PT * E]).then_inc(c.sem, c.step())
                        v.wait_ge(c.sem, c.now())
                        apart(v)
                        for j in range(PT):
                            ins = v.max(top[:, j, :], logits[:, j, :])
                        ins.then_inc(c.sem, c.step())
                        v.wait_ge(c.sem, c.now())
                        apart(v)
                        for j in range(PT):
                            ins = v.max_index(top_e[:, j, :], top[:, j, :], logits[:, j, :])
                        ins.then_inc(c.sem, c.step())
                        best = top[:, :, 0:1]
                        v.tensor_tensor(gap4[:], top[:, :, 0:K], best.to_broadcast([P, PT, K]), ALU.subtract).then_inc(c.sem, c.step())
                        v.tensor_tensor(gap16[:], logits[:], best.to_broadcast([P, PT, E]), ALU.subtract).then_inc(gaps_ready.sem, 1)
                        v.wait_ge(c.sem, c.now())
                        expert = rows[u][:, :, EXPERT:EXPERT + K]
                        v.tensor_copy(expert, top_e[:, :, 0:K]).then_inc(c.sem, c.step())
                        v.tensor_copy(rows[u][:, :, EXPERT + K:DEST], top_e[:, :, 0:K]).then_inc(c.sem, c.step())
                        v.tensor_copy(rows[u][:, :, DEST:DEST + K], dest[:]).then_inc(c.sem, c.step())
                        v.wait_ge(c.sem, c.now())
                        v.tensor_tensor(onehot[:], iota_e[:].unsqueeze(1).unsqueeze(1).to_broadcast([P, PT, K, E]),
                                        expert.unsqueeze(3).to_broadcast([P, PT, K, E]), ALU.is_equal).then_inc(c.sem, c.step())
                        v.tensor_scalar(dest[:], dest[:], float(PT * P * K), None, ALU.add).then_inc(c.sem, c.step())
                        v.wait_ge(c.sem, c.now())
                        v.tensor_reduce(chosen[:], onehot[:].rearrange("p j k e -> p j e k"), AX.X, ALU.add).then_inc(c.sem, c.step())
                        v.wait_ge(c.sem, c.now())
                        v.tensor_copy(chosen16[:], chosen[:]).then_inc(chosen_ready.sem, 1)

                    def weights(r, u):
                        c = route_at[0]
                        v.wait_ge(exps_ready.sem, exps_ready.done(r))
                        total, inv, inv_out = rsum[:, 0, :], rsum[:, 1, :], rsum[:, 2, :]
                        v.tensor_reduce(total, gap4[:], AX.X, ALU.add).then_inc(c.sem, c.step())
                        v.tensor_tensor(wsel[:], gap16[:], chosen[:], ALU.mult).then_inc(c.sem, c.step())
                        v.wait_ge(c.sem, c.now())
                        v.reciprocal(inv, total).then_inc(c.sem, c.step())
                        v.wait_ge(c.sem, c.now())
                        v.tensor_scalar(inv_out, inv, unscale[:, 3:4], None, ALU.mult).then_inc(c.sem, c.step())
                        v.tensor_tensor(wsel[:], wsel[:], inv.unsqueeze(2).to_broadcast([P, PT, E]), ALU.mult).then_inc(wsel_ready.sem, 1)
                        v.wait_ge(c.sem, c.now())
                        v.tensor_tensor(rows[u][:, :, WEIGHT:WEIGHT + K], gap4[:],
                                        inv_out.unsqueeze(2).to_broadcast([P, PT, K]), ALU.mult).then_inc(c.sem, c.step())

                    def places(r, u):
                        c = route_at[0]
                        v.wait_ge(rank_psum.sem, rank_psum.done(r))
                        v.tensor_tensor(slot[:], psL[:, 0:PT * E].rearrange("p (j e) -> p j e", e=E),
                                        region_e[:].unsqueeze(1).to_broadcast([P, PT, E]), ALU.add).then_inc(c.sem, c.step())
                        v.tensor_reduce(pair_count[:], chosen[:].rearrange("p j e -> p e j"), AX.X, ALU.add).then_inc(c.sem, c.step())
                        v.wait_ge(c.sem, c.now())
                        v.tensor_tensor(picked[:], onehot[:], slot[:].unsqueeze(2).to_broadcast([P, PT, K, E]), ALU.mult).then_inc(c.sem, c.step())
                        v.tensor_tensor(count[:], count[:], pair_count[:], ALU.add).then_inc(c.sem, c.step())
                        v.wait_ge(c.sem, c.now())
                        v.tensor_reduce(slot4[:], picked[:], AX.X, ALU.add).then_inc(c.sem, c.step())
                        v.tensor_copy(count16[:], count[:]).then_inc(c.sem, c.step())
                        v.wait_ge(c.sem, c.now())
                        v.tensor_copy(place[u][:], slot4[:].rearrange("p j k -> p (j k)")).then_inc(rows_ready.sem, 1)
                        c.end()

                    def step(x, i, n, c, u):
                        if n is not None:
                            stats2(n)
                        if i is not None:
                            row_max(0, i)
                            row_max(1, i)
                        if n is not None:
                            stats3(n)
                        if i is not None:
                            split_w(0, i)
                        if c is not None:
                            choose(c, u)
                        if i is not None:
                            split_w(1, i)
                        if c is not None:
                            weights(c, u)
                            places(c, u)
                        if i is not None:
                            combine(0, i)
                            split_w(2, i)
                            combine(1, i)
                        if n is not None:
                            split_xn(n, 1 - u)
                        if i is not None:
                            split_w(3, i)

                    steps(v, step)

                    table = psC[:].rearrange("p (a b) d -> p a (b d)", a=2)
                    c = Chain(tab_c, 0, 0)
                    v.memset(blank, 0.0).then_inc(c.sem, c.step())
                    v.memset(row_e[:], 0.0).then_inc(c.sem, c.step())
                    v.memset(one_e[:], 1.0).then_inc(c.sem, c.step())
                    v.wait_ge(c.sem, c.now())
                    v.memset(blank[:, :, EXPERT:DEST], -1.0).then_inc(c.sem, c.step())
                    v.wait_ge(tab_count, 1)
                    v.wait_ge(tab_iota, 2)
                    v.tensor_copy(n_e[:], psA[0][:, 0:E]).then_inc(c.sem, c.step())
                    v.tensor_copy(tile_n[:], tile_i[:, 0:C]).then_inc(c.sem, c.step())
                    v.tensor_copy(pad_f[:], tile_i[0:1, C:]).then_inc(c.sem, c.step())
                    v.wait_ge(c.sem, c.now())
                    v.scalar_tensor_tensor(pad_f[:], pad_f[:], 256.0, n_e[0:1, :], ALU.mult, ALU.add).then_inc(c.sem, c.step())
                    v.tensor_scalar(tiles_i[:], n_e[:], float(SLOTS - 1), None, ALU.add).then_inc(c.sem, c.step())
                    v.wait_ge(c.sem, c.now())
                    v.tensor_copy(pad_at[:], pad_f[:]).then_inc(pads_at, 1)
                    v.tensor_single_scalar(tiles_i[:], tiles_i[:], 8, ALU.logical_shift_right).then_inc(c.sem, c.step())
                    v.wait_ge(c.sem, c.now())
                    v.tensor_copy(tiles_f[:], tiles_i[:]).then_inc(c.sem, c.step())
                    v.wait_ge(c.sem, c.now())
                    v.tensor_tensor_scan(end_e[:], one_e[:], tiles_f[:], 0.0, ALU.mult, ALU.add).then_inc(c.sem, c.step())
                    v.wait_ge(c.sem, c.now())
                    v.tensor_tensor(past[:], tile_n[:].unsqueeze(2).to_broadcast([P, C, E]),
                                    end_e[:].unsqueeze(1).to_broadcast([P, C, E]), ALU.is_ge).then_inc(c.sem, c.step())
                    v.wait_ge(c.sem, c.now())
                    v.tensor_tensor(past_n[:], past[:], tiles_f[:].unsqueeze(1).to_broadcast([P, C, E]), ALU.mult).then_inc(c.sem, c.step())
                    v.tensor_reduce(before[:, 0, :], past[:], AX.X, ALU.add).then_inc(c.sem, c.step())
                    v.wait_ge(c.sem, c.now())
                    v.tensor_reduce(before[:, 1, :], past_n[:], AX.X, ALU.add).then_inc(c.sem, c.step())
                    v.tensor_scalar(cols[:, 0, :], before[:, 0, :], float(E - 1), None, ALU.min).then_inc(c.sem, c.step())
                    v.wait_ge(c.sem, c.now())
                    v.tensor_tensor(before[:, 1, :], tile_n[:], before[:, 1, :], ALU.subtract).then_inc(c.sem, c.step())
                    v.tensor_scalar(cols[:, 1, :], before[:, 0, :], float(REGION), None, ALU.mult).then_inc(c.sem, c.step())
                    v.wait_ge(c.sem, c.now())
                    v.scalar_tensor_tensor(cols[:, 1, :], before[:, 1, :], float(SLOTS), cols[:, 1, :], ALU.mult, ALU.add).then_inc(c.sem, c.step())
                    v.wait_ge(c.sem, c.now())
                    v.tensor_scalar(cols[:, 1, :], cols[:, 1, :], float(E * REGION), None, ALU.min).then_inc(c.sem, c.step())
                    v.wait_ge(c.sem, c.now())
                    for a in range(2):
                        for b in range(C):
                            ins = v.tensor_scalar(spread[:, a, b, :], ones[:], cols[:, a, b:b + 1], None, ALU.mult)
                    ins.then_inc(tab_spread, 1)
                    v.wait_ge(tab_rows, 1)
                    v.tensor_copy(tile_e[:], table[:, 0, 0:TILES])
                    v.tensor_copy(tile_tab[:], table[0:1, :, 0:TILES])
                    v.tensor_copy(row_e[:, 0:TILES // GROUP, :].rearrange("a g q -> a (g q)"), table[0:1, 0, 0:TILES])\
                        .then_inc(c.sem, c.step())
                    v.wait_ge(c.sem, c.now())
                    v.tensor_copy(packed[:], row_e[:, 0:TILES // GROUP, 0]).then_inc(c.sem, c.step())
                    for k in range(1, GROUP + 2):
                        g, q = divmod(k, GROUP)
                        v.wait_ge(c.sem, c.now())
                        v.scalar_tensor_tensor(packed[:], row_e[:, g:g + TILES // GROUP, q], float(16 ** k), packed[:],
                                               ALU.mult, ALU.add).then_inc(c.sem, c.step())
                    v.wait_ge(c.sem, c.now())
                    v.tensor_copy(turn_experts[:], packed[:]).then_inc(c.sem, c.step())

                @block.gpsimd
                def _(pool):
                    pool.iota(tile_i[:, 0:C], [[P, C]], base=0, channel_multiplier=1).then_inc(tab_iota, 1)
                    pool.iota(tile_i[:, C:], [[REGION // 256, E]], base=0, channel_multiplier=0).then_inc(tab_iota, 1)
                    pool.sem_inc(rows_sent.sem, rows_sent.start)

                    def send(r, u, before):
                        pool.wait_ge(rows_ready.sem, rows_ready.done(r))
                        apart(pool)
                        for j in range(PT):
                            if j == 1 and before is not None:
                                landed(before, 1 - u)
                            for k in range(K):
                                pool.indirect_dma_start(
                                    dispatch[:, :], bass.IndirectOffsetOnAxis(ap=place[u][:, j * K + k:j * K + k + 1], axis=0),
                                    rows[u][:, j, :], None).then_inc(scattered[u].sem, 16)

                    def landed(use, u):
                        pool.wait_ge(scattered[u].sem, scattered[u].done(use))
                        pool.sem_inc(rows_sent.sem, 1)

                    send(0, 0, None)
                    with pool.Fori(0, PAIRS // 2 - 1) as h:
                        send(h * 2 + 1, 1, h)
                        send(h * 2 + 2, 0, h)
                    send(PAIRS - 1, 1, PAIRS // 2 - 1)
                    landed(PAIRS // 2 - 1, 1)

        with ExitStack() as two:
            def s2(name, shape, dt=F32):
                return sb(name, shape, dt, two)

            rows2 = [s2(f"rows2_{q}", [P, 2, ROW]) for q in range(GROUP)]
            rows2h = [r[:].bitcast(F16) for r in rows2]
            meta = [s2(f"meta{q}", [P, 2 * 2]) for q in range(GROUP)]
            back = [s2(f"back{q}", [P, 2], U32) for q in range(GROUP)]
            match = [s2(f"match{q}", [P, 2, 2 * K]) for q in range(GROUP)]
            xT16 = [s2(f"xT16_{u}", [P, 2, SLOTS], F16) for u in range(2)]
            act_h = [s2(f"act_h{u}", [P, FC, SLOTS]) for u in range(2)]
            h_hi = [s2(f"h_hi{u}", [P, FC, SLOTS], F16) for u in range(2)]
            h_lo = [s2(f"h_lo{u}", [P, FC, SLOTS], F16) for u in range(2)]
            y = [s2(f"y{q}", [P, 2, D]) for q in range(GROUP)]
            psX = [pb(f"psX{u}", [P, 2, SLOTS], F16, two) for u in range(2)]
            psU = [pb(f"psU{u}", [P, FC, SLOTS], F32, two) for u in range(2)]
            psY = [pb(f"psY{u}", [P, 512], F32, two) for u in range(2)]

            rows_in = [sem(f"rows_in{q}") for q in range(GROUP)]
            turned = Signal(sem("turned"), credit=GROUP)
            xT16_ready = Signal(sem("xT16_ready"), credit=2)
            match_ready = Signal(sem("match_ready"), credit=GROUP)
            up_psum = Signal(sem("up_psum"), credit=2, per=2)
            gelu_ready = Signal(sem("gelu_ready"), credit=2, per=2)
            h_ready = Signal(sem("h_ready"), credit=2, per=2)
            down_psum = Signal(sem("down_psum"), credit=2)
            meta_ready = Signal(sem("meta_ready"), credit=1)
            y_ready = Signal(sem("y_ready"), credit=2)
            returned = [Signal(sem(f"returned{q}"), per=32) for q in range(GROUP)]
            y_sent = Signal(sem("y_sent"), credit=GROUP)
            tile_steps = sem("tile_steps")
            TSTEPS = 3

            def tiles(eng, body, ahead=0):
                with eng.Fori(0, TILES // GROUP) as h:
                    for q in range(GROUP):
                        body(h * GROUP + q, h, q)

            with nc.Block() as block:
                @block.sync
                def _(sp):
                    def load(n, h, q):
                        sp.wait_ge(turned.sem, turned.free(n, GROUP))
                        sp.wait_ge(match_ready.sem, match_ready.free(n, GROUP))
                        at = sp.value_load(tile_tab[0:1, 1, bass.ds(n, 1)], min_val=0, max_val=E * REGION)
                        sp.dma_start(rows2[q][:], dispatch[bass.ds(at, SLOTS), :].rearrange("(h p) w -> p h w", p=P))\
                          .then_inc(rows_in[q], 16)
                    tiles(sp, load)

                @block.tensor
                def _(pe):
                    pe.sem_inc(turned.sem, turned.start)
                    pe.sem_inc(up_psum.sem, up_psum.start)
                    pe.sem_inc(down_psum.sem, down_psum.start)

                    def turn(n, h, q):
                        u = q % 2
                        pe.wait_ge(rows_in[q], h * 16 + 16)
                        pe.wait_ge(xT16_ready.sem, xT16_ready.free(n, 2))
                        for part in range(2):
                            for s in range(2):
                                ins = pe.transpose(psX[u][:, part, s * P:(s + 1) * P], rows2h[q][:, s, part * D:(part + 1) * D],
                                                   ident16[:])
                        ins.then_inc(turned.sem, 1)

                    def expert(n):
                        return pe.value_load(tile_tab[0:1, 0, bass.ds(n, 1)], min_val=0, max_val=E - 1)

                    def up(n, h, q, e):
                        u = q % 2
                        pe.wait_ge(xT16_ready.sem, xT16_ready.done(n))
                        pe.wait_ge(gelu_ready.sem, gelu_ready.free(n, 2))
                        hi, lo = xT16[u][:, 0, :], xT16[u][:, 1, :]
                        for cc in range(FC):
                            wh = W1H[:, bass.ds(e, 1), cc * P:(cc + 1) * P].rearrange("p a f -> p (a f)")
                            wl = W1L[:, bass.ds(e, 1), cc * P:(cc + 1) * P].rearrange("p a f -> p (a f)")
                            pe.matmul(psU[u][:, cc, :], wh, hi, start=True, stop=False)
                            pe.matmul(psU[u][:, cc, :], wh, lo, start=False, stop=False)
                            ins = pe.matmul(psU[u][:, cc, :], wl, hi, start=False, stop=True)
                            if cc % 2:
                                ins.then_inc(up_psum.sem, 1)

                    def down(n, h, q, e):
                        u = q % 2
                        pe.wait_ge(h_ready.sem, h_ready.done(n))
                        pe.wait_ge(y_ready.sem, y_ready.free(n, 2))
                        for s in range(2):
                            o = psY[u][:, s * D:(s + 1) * D]
                            for cc in range(FC):
                                wh = W2H[:, bass.ds(e, 1), cc * P:(cc + 1) * P].rearrange("p a f -> p (a f)")
                                wl = W2L[:, bass.ds(e, 1), cc * P:(cc + 1) * P].rearrange("p a f -> p (a f)")
                                hh, hl = h_hi[u][:, cc, s * P:(s + 1) * P], h_lo[u][:, cc, s * P:(s + 1) * P]
                                pe.matmul(o, hh, wh, start=(cc == 0), stop=False)
                                pe.matmul(o, hh, wl, start=False, stop=False)
                                ins = pe.matmul(o, hl, wh, start=False, stop=(cc == FC - 1))
                        ins.then_inc(down_psum.sem, 1)

                    turn(0, 0, 0)
                    turn(1, 0, 1)
                    up(0, 0, 0, expert(0))
                    turn(2, 0, 2)
                    up(1, 0, 1, expert(1))
                    with pe.Fori(0, TILES // GROUP - 1) as h:
                        word = pe.value_load(turn_experts[0:1, bass.ds(h, 1)], min_val=0, max_val=16 ** (GROUP + 2) - 1)
                        e = [pe.snap(word // 16 ** q % 16, min_val=0, max_val=E - 1) for q in range(GROUP + 2)]
                        for q in range(GROUP):
                            n = h * GROUP + q
                            turn(n + 3, h + (q + 3) // GROUP, (q + 3) % GROUP)
                            up(n + 2, h + (q + 2) // GROUP, (q + 2) % GROUP, e[q + 2])
                            down(n, h, q, e[q])
                    for n in range(TILES - GROUP, TILES):
                        if n + 3 < TILES:
                            turn(n + 3, (n + 3) // GROUP, (n + 3) % GROUP)
                        if n + 2 < TILES:
                            up(n + 2, (n + 2) // GROUP, (n + 2) % GROUP, expert(n + 2))
                        down(n, n // GROUP, n % GROUP, expert(n))

                @block.scalar
                def _(act):
                    act.sem_inc(xT16_ready.sem, xT16_ready.start)
                    act.sem_inc(gelu_ready.sem, gelu_ready.start)
                    act.sem_inc(y_ready.sem, y_ready.start)

                    def expert(n):
                        return act.value_load(tile_tab[0:1, 0, bass.ds(n, 1)], min_val=0, max_val=E - 1)

                    def gelu(n, h, q, e):
                        u = q % 2
                        for part in range(2):
                            act.wait_ge(up_psum.sem, up_psum.done(n, part))
                            if part == 0:
                                act.wait_ge(h_ready.sem, h_ready.free(n, 2))
                            apart(act)
                            for cc in range(2 * part, 2 * part + 2):
                                ins = act.activation(act_h[u][:, cc, :], psU[u][:, cc, :], ACT.Gelu,
                                                     bias=b1T[:, bass.ds(e * FC + cc, 1)], scale=unscale[:, 0:1])
                            ins.then_inc(gelu_ready.sem, 1)

                    def copy_rows(n, q):
                        u = q % 2
                        act.wait_ge(turned.sem, turned.done(n))
                        act.wait_ge(up_psum.sem, up_psum.free(n, 2))
                        act.activation(xT16[u][:].bitcast(F32), psX[u][:].bitcast(F32), ACT.Copy).then_inc(xT16_ready.sem, 1)

                    def weigh(n, h, q):
                        u = q % 2
                        act.wait_ge(down_psum.sem, down_psum.done(n))
                        act.wait_ge(meta_ready.sem, meta_ready.done(n))
                        act.wait_ge(y_sent.sem, y_sent.free(n, GROUP))
                        for s in range(2):
                            ins = act.activation(y[q][:, s, :], psY[u][:, s * D:(s + 1) * D], ACT.Copy, scale=meta[q][:, 2 * s + 1:2 * s + 2])
                        ins.then_inc(y_ready.sem, 1)

                    copy_rows(0, 0)
                    copy_rows(1, 1)
                    gelu(0, 0, 0, expert(0))
                    copy_rows(2, 2)
                    gelu(1, 0, 1, expert(1))
                    with act.Fori(0, TILES // GROUP - 1) as h:
                        word = act.value_load(turn_experts[0:1, bass.ds(h, 1)], min_val=0, max_val=16 ** (GROUP + 2) - 1)
                        e = [act.snap(word // 16 ** q % 16, min_val=0, max_val=E - 1) for q in range(GROUP + 2)]
                        for q in range(GROUP):
                            copy_rows(h * GROUP + (q + 3), (q + 3) % GROUP)
                            gelu(h * GROUP + (q + 2), h + (q + 2) // GROUP, (q + 2) % GROUP, e[q + 2])
                            weigh(h * GROUP + q, h, q)
                    for n in range(TILES - GROUP, TILES):
                        if n + 3 < TILES:
                            copy_rows(n + 3, (n + 3) % GROUP)
                        if n + 2 < TILES:
                            gelu(n + 2, (n + 2) // GROUP, (n + 2) % GROUP, expert(n + 2))
                        weigh(n, n // GROUP, n % GROUP)

                @block.vector
                def _(v):
                    v.sem_inc(match_ready.sem, match_ready.start)
                    v.sem_inc(h_ready.sem, h_ready.start)
                    v.sem_inc(meta_ready.sem, meta_ready.start)

                    def split(n, h, q, c):
                        u = q % 2
                        v.wait_ge(down_psum.sem, down_psum.free(n, 2))
                        for part in range(2):
                            v.wait_ge(gelu_ready.sem, gelu_ready.done(n, part))
                            s = slice(2 * part, 2 * part + 2)
                            v.tensor_scalar(h_hi[u][:, s, :], act_h[u][:, s, :], scales[:, 2:3], None, ALU.mult).then_inc(c.sem, c.step())
                            v.wait_ge(c.sem, c.now())
                            v.scalar_tensor_tensor(h_lo[u][:, s, :], act_h[u][:, s, :], scales[:, 2:3], h_hi[u][:, s, :],
                                                   ALU.mult, ALU.subtract).then_inc(h_ready.sem, 1)

                    def head(n, h, q):
                        v.wait_ge(rows_in[q], h * 16 + 16)
                        v.scalar_tensor_tensor(match[q][:], rows2[q][:, :, EXPERT:DEST], tile_e[:, bass.ds(n, 1)],
                                               rows2[q][:, :, DEST:WEIGHT + K], ALU.is_equal, ALU.mult)\
                            .then_inc(match_ready.sem, 1)

                    def choice(n, q, c):
                        v.wait_ge(y_sent.sem, y_sent.free(n, GROUP))
                        v.wait_ge(match_ready.sem, match_ready.done(n))
                        v.tensor_reduce(meta[q][:], match[q][:].rearrange("p s (a k) -> p (s a) k", k=K), AX.X, ALU.add).then_inc(c.sem, c.step())
                        v.wait_ge(c.sem, c.now())
                        v.tensor_scalar(back[q][:], meta[q][:, 0:4:2], float(NO_ROW), None, ALU.add).then_inc(meta_ready.sem, 1)

                    head(0, 0, 0)
                    head(1, 0, 1)
                    with v.Fori(0, TILES // GROUP - 1) as h:
                        for q in range(GROUP):
                            n = h * GROUP + q
                            c = Chain(tile_steps, n * TSTEPS, TSTEPS)
                            head(n + 2, h + (q + 2) // GROUP, (q + 2) % GROUP)
                            split(n, h, q, c)
                            choice(n, q, c)
                            c.end()
                    for n in range(TILES - GROUP, TILES):
                        c = Chain(tile_steps, n * TSTEPS, TSTEPS)
                        if n + 2 < TILES:
                            head(n + 2, (n + 2) // GROUP, (n + 2) % GROUP)
                        split(n, n // GROUP, n % GROUP, c)
                        choice(n, n % GROUP, c)

                @block.gpsimd
                def _(pool):
                    pool.sem_inc(y_sent.sem, y_sent.start)
                    last_row = pool.alloc_register("last_row")
                    pool.reg_mov(last_row, TOKENS * K - 1)
                    limit = pool.snap(last_row)

                    def send(n, q):
                        pool.wait_ge(y_ready.sem, y_ready.done(n))
                        apart(pool)
                        for s in range(2):
                            pool.indirect_dma_start(
                                expert_out[:, :], bass.IndirectOffsetOnAxis(ap=back[q][:, s:s + 1], axis=0),
                                y[q][:, s, :], None, bounds_check=limit, oob_is_err=False).then_inc(returned[q].sem, 16)

                    def landed(h, q):
                        pool.wait_ge(returned[q].sem, returned[q].done(h))
                        pool.sem_inc(y_sent.sem, 1)

                    for n in range(3):
                        send(n, n)
                    with pool.Fori(0, TILES // GROUP - 1) as h:
                        for q in range(GROUP):
                            send(h * GROUP + (q + 3), (q + 3) % GROUP)
                            landed(h, q)
                    send(TILES - 1, GROUP - 1)
                    for q in range(GROUP):
                        landed(TILES // GROUP - 1, q)

        with ExitStack() as three:
            def s3(name, shape, dt=F32):
                return sb(name, shape, dt, three)

            picks = [s3(f"picks{q}", [P, BT, K, D]) for q in range(4)]
            z = [s3(f"z{u}", [P, PT, D]) for u in range(2)]
            zn = [s3(f"zn{u}", [P, PT, D]) for u in range(2)]
            zo = [s3(f"zo{u}", [P, PT, D]) for u in range(2)]
            zstats = s3("zstats", [P, PT, 6])
            zscr = s3("zscr", [P, 6, PT])
            ln4 = [s3(f"ln4_{u}", [P, 2, PT]) for u in range(2)]
            psS = [pb(f"psS{q}", [P, BT, D], F32, three) for q in range(4)]

            picks_in = [sem(f"picks_in{q}") for q in range(4)]
            sum_psum = Signal(sem("sum_psum"), credit=4)
            z_ready = Signal(sem("z_ready"), credit=4)
            ln4_ready = Signal(sem("ln4_ready"))
            zn_ready = Signal(sem("zn_ready"), credit=2)
            zo_ready = Signal(sem("zo_ready"), credit=2)
            stored = [Signal(sem(f"stored{u}"), credit=1, per=16) for u in range(2)]
            z_steps = sem("z_steps")
            expert_tiles = expert_out[:, :].rearrange("(j p k) d -> p j k d", p=P, k=K)

            with nc.Block() as block:
                @block.sync
                def _(sp):
                    with sp.Fori(0, NB // 4) as h:
                        for q in range(4):
                            sp.wait_ge(sum_psum.sem, sum_psum.free(h * 4 + q, 4))
                            sp.dma_start(picks[q][:], expert_tiles[:, bass.ds(h * NB + q * BT, BT)]).then_inc(picks_in[q], 16)

                @block.tensor
                def _(pe):
                    pe.sem_inc(sum_psum.sem, sum_psum.start)
                    with pe.Fori(0, NB // 4) as h:
                        for q in range(4):
                            pe.wait_ge(picks_in[q], h * 16 + 16)
                            pe.wait_ge(z_ready.sem, z_ready.free(h * 4 + q, 4))
                            for k in range(K):
                                ins = pe.matmul(psS[q][:], ident[:], picks[q][:, :, k, :], start=(k == 0), stop=(k == K - 1))
                            ins.then_inc(sum_psum.sem, 1)

                @block.vector
                def _(v):
                    v.sem_inc(z_ready.sem, z_ready.start)
                    STEPS = NORM_STEPS
                    with v.Fori(0, PAIRS // 2) as h:
                        for u in range(2):
                            i = h * 2 + u
                            c = Chain(z_steps, i * STEPS, STEPS)
                            v.wait_ge(zn_ready.sem, zn_ready.free(i, 2))
                            for b in range(2):
                                q = 2 * u + b
                                v.wait_ge(sum_psum.sem, sum_psum.done(i * 2 + b))
                                v.tensor_tensor(z[u][:, b * BT:(b + 1) * BT, :], psS[q][:],
                                                R[:, bass.ds(i * PT + b * BT, BT), :], ALU.add).then_inc(z_ready.sem, 1)
                            v.wait_ge(z_ready.sem, z_ready.done(i * 2 + 1))
                            for j in range(PT):
                                ins = v.bn_stats(zstats[:, j, :], z[u][:, j, :])
                            ins.then_inc(c.sem, c.step())
                            norm_steps(v, c, zstats, ln4[u][:, 0, :], ln4[u][:, 1, :], zscr, ln4_ready.sem)
                            c.end()

                @block.scalar
                def _(act):
                    act.sem_inc(zn_ready.sem, zn_ready.start)
                    with act.Fori(0, PAIRS // 2) as h:
                        for u in range(2):
                            i = h * 2 + u
                            act.wait_ge(ln4_ready.sem, ln4_ready.done(i))
                            act.wait_ge(zo_ready.sem, zo_ready.free(i, 2))
                            for j in range(PT):
                                ins = act.activation(zn[u][:, j, :], z[u][:, j, :], ACT.Identity,
                                                     bias=ln4[u][:, 1, j:j + 1], scale=ln4[u][:, 0, j:j + 1])
                            ins.then_inc(zn_ready.sem, 1)
                            act.wait_ge(zo_ready.sem, zo_ready.done(i))
                            act.dma_start(out_tiles[:, bass.ds(i * PT, PT), :], zo[u][:]).then_inc(stored[u].sem, 16)
                    for u in range(2):
                        act.wait_ge(stored[u].sem, stored[u].done(PAIRS // 2 - 1))

                @block.gpsimd
                def _(pool):
                    pool.sem_inc(zo_ready.sem, zo_ready.start)
                    for u in range(2):
                        pool.sem_inc(stored[u].sem, stored[u].start)
                    with pool.Fori(0, PAIRS // 2) as h:
                        for u in range(2):
                            i = h * 2 + u
                            pool.wait_ge(zn_ready.sem, zn_ready.done(i))
                            pool.wait_ge(stored[u].sem, stored[u].free(h, 1))
                            pool.tensor_tensor(zo[u][:], zn[u][:], X[:, bass.ds(i * PT, PT), :], ALU.add).then_inc(zo_ready.sem, 1)


_INS = ['L0_attn_x', 'L0_attn_W1', 'L0_attn_b1', 'L0_attn_w2', 'L0_attn_b2', 'L0_attn_Wc', 'L0_attn_bc', 'L0_ffn_keys',
        'L0_ffn_w1', 'L0_ffn_b1', 'L0_ffn_w2', 'L0_ffn_b2', 'L0_ffn_rw', 'L0_ffn_rb']
_OUTS = [((NB, T, D), 'float32')]


def kernel(**inputs):
    import numpy as _np
    import concourse.bacc as _bacc
    from concourse import mybir as _mybir
    from concourse.bass_utils import run_bass_kernel_spmd as _run

    nc = _bacc.Bacc("TRN2", target_bir_lowering=False, num_devices=1)
    arrays, args = {}, []
    for name in _INS:
        a = _np.ascontiguousarray(inputs[name])
        arrays[f"in_{name}_dram"] = a
        args.append(nc.dram_tensor(f"in_{name}_dram", a.shape, _mybir.dt.from_np(a.dtype), kind="ExternalInput").ap())
    for i, (shape, dtype) in enumerate(_OUTS):
        dt = _mybir.dt.from_np(_np.dtype(dtype))
        args.append(nc.dram_tensor(f"out_{i}_dram", shape, dt, kind="ExternalOutput").ap())
    build(nc, *args)
    r = _run(nc, [arrays], core_ids=[0])
    got = tuple(r.results[0][f"out_{i}_dram"] for i in range(len(_OUTS)))
    return got[0]
```

```python
from contextlib import ExitStack

import concourse.bass as bass
from concourse import mybir

ALU = mybir.AluOpType
ACT = mybir.ActivationFunctionType
AX = mybir.AxisListType
F32 = mybir.dt.float32
F16 = mybir.dt.float16
I32 = mybir.dt.int32
U32 = mybir.dt.uint32

P = 128
D = 128
NB, T = 16, 512
TOKENS = NB * T
BT = T // P
PT = 2 * BT
PAIRS = NB // 2
NT = TOKENS // P
E, K = 16, 4
FF = 512
FC = FF // P
EPS = 1e-5

SLOTS = 256
REGION = TOKENS + SLOTS
TILES = (TOKENS * K + E * (SLOTS - 1)) // SLOTS + 1
NO_ROW = 65536
GROUP = 4
TURN = 2 * GROUP
assert TILES % TURN == 0

HI, LO = 0, D
EXPERT, DEST, WEIGHT = D, D + 2 * K, D + 3 * K
ROW = D + 4 * K

LN_BOUND_SQ = 130.0


class Signal:

    def __init__(self, sem, credit=0, per=1):
        self.sem, self.credit, self.per = sem, credit, per

    @property
    def start(self):
        return self.credit * self.per

    def done(self, n, part=None):
        part = self.per if part is None else part + 1
        return n * self.per + (self.start + part)

    def free(self, n, bufs, part=None):
        assert bufs <= self.credit
        part = self.per if part is None else part + 1
        return n * self.per + ((self.credit - bufs) * self.per + part)


class Chain:

    def __init__(self, sem, base, steps):
        self.sem, self.base, self.steps, self.n = sem, base, steps, 0

    def step(self):
        self.n += 1
        return 1

    def now(self):
        return self.base + self.n

    def end(self):
        assert self.n == self.steps, self.n


def norm_steps(v, c, stats, rstd, nmr, scr, last):
    me, m2e, mo, m2o = stats[:, :, 1], stats[:, :, 2], stats[:, :, 4], stats[:, :, 5]
    total, diff, q, var, y, a = (scr[:, k] for k in range(6))
    v.wait_ge(c.sem, c.now())
    v.tensor_tensor(total, me, mo, ALU.add).then_inc(c.sem, c.step())
    v.tensor_tensor(diff, me, mo, ALU.subtract).then_inc(c.sem, c.step())
    v.tensor_tensor(q, m2e, m2o, ALU.add).then_inc(c.sem, c.step())
    v.wait_ge(c.sem, c.now())
    v.tensor_scalar(q, q, 1.0 / D, EPS, ALU.mult, ALU.add).then_inc(c.sem, c.step())
    v.tensor_tensor(diff, diff, diff, ALU.mult).then_inc(c.sem, c.step())
    v.wait_ge(c.sem, c.now())
    v.scalar_tensor_tensor(var, diff, 0.25, q, ALU.mult, ALU.add).then_inc(c.sem, c.step())
    v.wait_ge(c.sem, c.now())
    v.tensor_single_scalar(a.bitcast(I32), var.bitcast(I32), 1, ALU.logical_shift_right).then_inc(c.sem, c.step())
    v.wait_ge(c.sem, c.now())
    v.tensor_scalar(y.bitcast(I32), a.bitcast(I32), -1.0, float(0x5F3759DF), ALU.mult, ALU.add).then_inc(c.sem, c.step())
    for n in range(3):
        v.wait_ge(c.sem, c.now())
        v.tensor_tensor(a, y, y, ALU.mult).then_inc(c.sem, c.step())
        v.wait_ge(c.sem, c.now())
        v.scalar_tensor_tensor(a, a, -0.5, var, ALU.mult, ALU.mult).then_inc(c.sem, c.step())
        v.wait_ge(c.sem, c.now())
        v.scalar_tensor_tensor(rstd if n == 2 else y, a, 1.5, y, ALU.add, ALU.mult).then_inc(c.sem, c.step())
    v.wait_ge(c.sem, c.now())
    v.scalar_tensor_tensor(nmr, total, -0.5, rstd, ALU.mult, ALU.mult).then_inc(last, 1)


NORM_STEPS = 18
ROUTE_STEPS = 21


def build(nc, x, W1, b1, w2, b2, Wc, bc, keys, fw1, fb1, fw2, fb2, rw, rb, out):
    dispatch = nc.dram_tensor("dispatch", [E * REGION + SLOTS, ROW], F32)
    expert_out = nc.dram_tensor("expert_out", [TOKENS * K, D], F32)
    x_tiles = x.rearrange("b (t p) d -> p (b t) d", p=P)
    out_tiles = out.rearrange("b (t p) d -> p (b t) d", p=P)
    w1_src = fw1.rearrange("e (c p) d -> p e c d", p=P)
    w2_src = fw2.rearrange("e d f -> d e f")

    with ExitStack() as ctx:
        def sb(name, shape, dt=F32, scope=ctx):
            return scope.enter_context(nc.sbuf_tensor(name, shape, dt))

        def pb(name, shape, dt=F32, scope=ctx):
            return scope.enter_context(nc.psum_tensor(name, shape, dt))

        def sem(name):
            return ctx.enter_context(nc.semaphore(name))

        passed = sem("passed")

        def apart(eng):
            eng.sem_inc(passed, 1)

        X = sb("X", [P, NT, D])
        R = sb("R", [P, NT, D])
        W1H = sb("W1H", [P, E, FF], F16)
        W1L = sb("W1L", [P, E, FF], F16)
        W2H = sb("W2H", [P, E, FF], F16)
        W2L = sb("W2L", [P, E, FF], F16)
        b1T = sb("b1T", [P, E * FC])
        ident = sb("ident", [P, P])
        ident16 = sb("ident16", [P, P], F16)
        ones = sb("ones", [P, P])
        ones16 = sb("ones16", [P, P], F16)
        scales = sb("scales", [P, 3])
        unscale = sb("unscale", [P, 4])
        count16 = sb("count16", [P, E], F16)
        tile_e = sb("tile_e", [P, TILES])
        tile_tab = sb("tile_tab", [1, 2, TILES], I32)
        turn_experts = sb("turn_experts", [1, TILES // GROUP], I32)

        with ExitStack() as one:
            def s1(name, shape, dt=F32):
                return sb(name, shape, dt, one)

            rstd1 = s1("rstd1", [P, NT])
            nmr1 = s1("nmr1", [P, NT])
            W1T = s1("W1T", [P, P])
            WcT = s1("WcT", [P, 2 * D])
            bc_row = s1("bc_row", [1, D])
            b1_col = s1("b1_col", [P, 1])
            b2_col = s1("b2_col", [P, 1])
            w2_col = s1("w2_col", [P, 1])
            w2_rep = s1("w2_rep", [P, P])
            upto = s1("upto", [P, P])
            before16 = s1("before16", [P, P], F16)
            LW = s1("LW", [P, E])
            neg1 = s1("neg1", [P, E])
            key_bias = s1("key_bias", [E, 1])
            b2_sel = s1("b2_sel", [P, PT, D])
            iota_e = s1("iota_e", [P, E])
            region_e = s1("region_e", [P, E])
            dest = s1("dest", [P, PT, K])
            count = s1("count", [P, E])
            group_sq = s1("group_sq", [P, 2, E // 2])
            bound = s1("bound", [P, 3])
            bound_all = s1("bound_all", [P, 3])
            sbits = s1("sbits", [P, 3], I32)
            fb1_sq = s1("fb1_sq", [P, E * FC])
            w_raw = [[w[:].rearrange("p e f -> p (e f)").bitcast(F32).rearrange("p (e f) -> p e f", f=FF) for w in pair]
                     for pair in ((W1H, W1L), (W2H, W2L))]
            FIRST = NT // 4

            psA = [pb(f"psA{b}", [P, T], F32, one) for b in range(2)]
            psZ = [pb(f"psZ{b}", [P, BT, D], F32, one) for b in range(2)]
            psC = pb("psC", [P, BT, D], F32, one)
            psD = pb("psD", [P, 512], F32, one)
            DEN = BT
            psN = pb("psN", [P, 512], F32, one)
            psL = pb("psL", [P, 512], F32, one)

            with ExitStack() as pre_scope:
                def s0(name, shape, dt=F32):
                    return sb(name, shape, dt, pre_scope)

                W1n = s0("W1n", [P, D])
                Wcn = s0("Wcn", [P, 2 * D])
                b2_one = s0("b2_one", [1, 1])
                keys_n = s0("keys_n", [E, D])
                rw_n = s0("rw_n", [E, D])
                rb_n = s0("rb_n", [E, 1])
                key_sq = s0("key_sq", [E, D])
                key_len = s0("key_len", [E, 1])
                fb1_n = s0("fb1_n", [E * FC, P])
                xstats = s0("xstats", [P, FIRST, 6])
                xscr = s0("xscr", [P, 6, FIRST])
                iota_i = s0("iota_i", [P, 2 * E + PT * K], I32)

                x_in = [sem(f"x_in{q}") for q in range(4)]
                small_in = sem("small_in")
                squared = sem("squared")
                consts = sem("consts")
                masks = sem("masks")
                setup_v = sem("setup_v")
                setup_t = sem("setup_t")
                setup_ready = sem("setup_ready")
                bounds_in = sem("bounds_in")
                bounds_all = sem("bounds_all")
                ln1_ready = sem("ln1_ready")
                raw_in = [sem(f"raw_in{half}") for half in range(2)]

                with nc.Block() as block:
                    @block.sync
                    def _(sp):
                        for q in range(4):
                            if q == 1:
                                sp.wait_ge(small_in, 16 * (10 + PT))
                            sp.dma_start(X[:, q * FIRST:(q + 1) * FIRST, :], x_tiles[:, q * FIRST:(q + 1) * FIRST, :])\
                              .then_inc(x_in[q], 16)
                        for half in range(2):
                            e = slice(half * E // 2, (half + 1) * E // 2)
                            sp.dma_start(w_raw[0][half].rearrange("p e (c d) -> p e c d", c=FC), w1_src[:, e]).then_inc(raw_in[half], 16)
                            sp.dma_start(w_raw[1][half], w2_src[:, e, :]).then_inc(raw_in[half], 16)

                    @block.gpsimd
                    def _(pool):
                        pool.memset(ident[:], 0.0).then_inc(masks, 1)
                        pool.memset(upto[:], 1.0).then_inc(masks, 1)
                        pool.memset(b2_sel[:], 0.0).then_inc(masks, 1)
                        pool.iota(iota_i[:, 0:E], [[1, E]], base=0, channel_multiplier=0).then_inc(masks, 1)
                        pool.iota(iota_i[:, E:2 * E], [[REGION // 256, E]], base=0, channel_multiplier=0).then_inc(masks, 1)
                        pool.iota(iota_i[:, 2 * E:], [[P * K, PT], [1, K]], base=-NO_ROW, channel_multiplier=K).then_inc(masks, 1)
                        pool.wait_ge(masks, 6)
                        pool.affine_select(out=ident[:], in_=ident[:], compare_op=ALU.not_equal, fill=1.0, base=0,
                                           pattern=[[-1, P]], channel_multiplier=1).then_inc(masks, 1)
                        pool.affine_select(out=upto[:], in_=upto[:], compare_op=ALU.is_ge, fill=0.0, base=0,
                                           pattern=[[1, P]], channel_multiplier=-1).then_inc(masks, 1)

                    @block.scalar
                    def _(act):
                        for dst, src in ((W1n[:], W1), (Wcn[:], Wc), (bc_row[:], bc.rearrange("(a n) -> a n", a=1)),
                                         (b1_col[:], b1.rearrange("(n a) -> n a", a=1)),
                                         (w2_col[:], w2.rearrange("a n -> n a")),
                                         (b2_one[:], b2.rearrange("(a n) -> a n", a=1)),
                                         (keys_n[:], keys), (rw_n[:], rw), (rb_n[:], rb.rearrange("(n a) -> n a", a=1)),
                                         (fb1_n[:], fb1.rearrange("e (c p) -> (e c) p", p=P))):
                            act.dma_start(dst, src).then_inc(small_in, 16)
                        act.wait_ge(masks, 8)
                        for j in range(PT):
                            act.dma_start(b2_sel[j * E:(j + 1) * E, j, :], fb2).then_inc(small_in, 16)

                    @block.vector
                    def _(v):
                        c = Chain(setup_v, 0, 0)
                        v.memset(ones[:], 1.0).then_inc(c.sem, c.step())
                        v.memset(neg1[:], -1.0).then_inc(c.sem, c.step())
                        v.memset(count[:], 0.0).then_inc(c.sem, c.step())
                        v.memset(count16[:], 0.0).then_inc(c.sem, c.step())
                        v.wait_ge(c.sem, c.now())
                        v.tensor_copy(ones16[:], ones[:]).then_inc(c.sem, c.step())
                        v.wait_ge(x_in[0], 16)
                        for t in range(FIRST):
                            ins = v.bn_stats(xstats[:, t, :], X[:, t, :])
                        ins.then_inc(c.sem, c.step())
                        norm_steps(v, c, xstats, rstd1[:, 0:FIRST], nmr1[:, 0:FIRST], xscr, ln1_ready)
                        v.wait_ge(masks, 8)
                        v.tensor_copy(ident16[:], ident[:]).then_inc(c.sem, c.step())
                        v.tensor_tensor(before16[:], upto[:], ident[:], ALU.subtract).then_inc(c.sem, c.step())
                        v.tensor_copy(iota_e[:], iota_i[:, 0:E]).then_inc(c.sem, c.step())
                        v.tensor_copy(region_e[:], iota_i[:, E:2 * E]).then_inc(c.sem, c.step())
                        v.tensor_copy(dest[:].rearrange("p j k -> p (j k)"), iota_i[:, 2 * E:]).then_inc(c.sem, c.step())
                        v.wait_ge(c.sem, c.now())
                        v.tensor_scalar(region_e[:], region_e[:], 256.0, None, ALU.mult).then_inc(c.sem, c.step())
                        v.wait_ge(small_in, 16 * (10 + PT))
                        v.tensor_scalar(w2_rep[:], ones[:], w2_col[:, 0:1], None, ALU.mult).then_inc(c.sem, c.step())
                        v.tensor_tensor(key_sq[:], keys_n[:], keys_n[:], ALU.mult).then_inc(c.sem, c.step())
                        v.wait_ge(c.sem, c.now())
                        v.tensor_reduce(key_len[:], key_sq[:], AX.X, ALU.add).then_inc(c.sem, c.step())
                        v.wait_ge(c.sem, c.now())
                        v.tensor_tensor(key_bias[:], rb_n[:], key_len[:], ALU.subtract).then_inc(c.sem, c.step())
                        v.scalar_tensor_tensor(keys_n[:], keys_n[:], 2.0, rw_n[:], ALU.mult, ALU.add).then_inc(consts, 1)
                        v.wait_ge(setup_t, 1)
                        v.tensor_copy(W1T[:], psA[0][:, 0:P])
                        v.tensor_copy(WcT[:, 0:D], psA[0][:, P:2 * P])
                        v.tensor_copy(WcT[:, D:2 * D], psA[0][:, 2 * P:3 * P])
                        v.tensor_copy(b1T[:], psA[0][:, 3 * P:3 * P + E * FC])
                        v.tensor_copy(LW[:], psA[1][:, 0:E])
                        v.tensor_copy(b2_col[:], psA[1][:, 2 * E:2 * E + 1]).then_inc(c.sem, c.step())
                        v.wait_ge(c.sem, c.now())

                    @block.tensor
                    def _(pe):
                        pe.wait_ge(masks, 8)
                        pe.wait_ge(consts, 1)
                        pe.wait_ge(small_in, 16 * (10 + PT))
                        pe.transpose(psA[0][:, 0:P], W1n[:], ident[:])
                        pe.transpose(psA[0][:, P:2 * P], Wcn[:, D:2 * D], ident[:])
                        pe.transpose(psA[0][:, 2 * P:3 * P], Wcn[:, 0:D], ident[:])
                        pe.transpose(psA[0][:, 3 * P:3 * P + E * FC], fb1_n[:], ident[0:E * FC, 0:E * FC])
                        pe.transpose(psA[1][:, 0:E], keys_n[:], ident[0:E, 0:E])
                        pe.matmul(psA[1][:, 2 * E:2 * E + 1], ones[0:1, :], b2_one[:], start=True, stop=True).then_inc(setup_t, 1)

            stage = s1("stage", [P, 2, 2, FF])
            xn1 = [s1(f"xn1_{b}", [P, BT, D]) for b in range(2)]
            xT = [s1(f"xT{b}", [P, T]) for b in range(2)]
            hT = [s1(f"hT{b}", [P, T]) for b in range(2)]
            e4 = [s1(f"e4_{b}", [P, BT]) for b in range(2)]
            mx = [s1(f"mx{b}", [P, 3]) for b in range(2)]
            xproj = [s1(f"xproj{b}", [P, BT, D]) for b in range(2)]
            wctx = [s1(f"wctx{b}", [P, BT, D]) for b in range(2)]
            rden = [s1(f"rden{b}", [P, BT]) for b in range(2)]
            pre = [s1(f"pre{b}", [P, BT, D]) for b in range(2)]

            stats = s1("stats", [P, PT, 6])
            scr = s1("scr", [P, 6, PT])
            ln2 = s1("ln2", [P, 2, PT])
            ln3 = s1("ln3", [P, 2, PT])
            normed = s1("normed", [P, PT, D])
            xnT = [s1(f"xnT{h}", [P, T]) for h in range(2)]
            xnS = [s1(f"xnS{h}", [P, T]) for h in range(2)]
            logitsT = s1("logitsT", [E, PT * P])
            logits = s1("logits", [P, PT, E])
            top = s1("top", [P, PT, 8])
            top_e = s1("top_e", [P, PT, 8], U32)
            onehot = s1("onehot", [P, PT, K, E])
            picked = s1("picked", [P, PT, K, E])
            chosen = s1("chosen", [P, PT, E])
            chosen16 = s1("chosen16", [P, PT, E], F16)
            gap4 = s1("gap4", [P, PT, K])
            gap16 = s1("gap16", [P, PT, E])
            rsum = s1("rsum", [P, 3, PT])
            wsel = s1("wsel", [P, PT, E])
            wselT = s1("wselT", [P, P])
            slot = s1("slot", [P, PT, E])
            slot4 = s1("slot4", [P, PT, K])
            pair_count = s1("pair_count", [P, E])
            rows = [s1(f"rows{u}", [P, PT, ROW]) for u in range(2)]
            rows16 = [r[:].bitcast(F16) for r in rows]
            place = [s1(f"place{u}", [P, PT * K], U32) for u in range(2)]

            C = 2
            n_e = s1("n_e", [P, E])
            tiles_i = s1("tiles_i", [P, E], I32)
            tiles_f = s1("tiles_f", [P, E])
            one_e = s1("one_e", [P, E])
            end_e = s1("end_e", [P, E])
            tile_i = s1("tile_i", [P, C + E], I32)
            tile_n = s1("tile_n", [P, C])
            past = s1("past", [P, C, E])
            past_n = s1("past_n", [P, C, E])
            cols = s1("cols", [P, 2, C])
            before = s1("before", [P, 2, C])
            spread = stage[:, 0, 0].rearrange("p (a b t) -> p a b t", a=2, b=C)
            pad_f = s1("pad_f", [1, E])
            packed = s1("packed", [1, TILES // GROUP])
            pad_at = s1("pad_at", [1, E], I32)
            row_e = stage[0:1, 1, 1, 0:TILES + GROUP].rearrange("p (g q) -> p g q", q=GROUP)
            blank = stage[:, 1, 0, 0:2 * ROW].rearrange("p (h w) -> p h w", h=2)
            tab_c = sem("tab_c")
            tab_count = sem("tab_count")
            tab_iota = sem("tab_iota")
            tab_spread = sem("tab_spread")
            tab_rows = sem("tab_rows")
            pads_at = sem("pads_at")
            padded = sem("padded")


            stage_in = sem("stage_in")
            xn1_ready = Signal(sem("xn1_ready"))
            xT_psum = Signal(sem("xT_psum"), credit=2)
            xT_ready = Signal(sem("xT_ready"))
            h_psum = Signal(sem("h_psum"))
            hT_ready = Signal(sem("hT_ready"))
            zctx_psum = Signal(sem("zctx_psum"))
            xproj_psum = Signal(sem("xproj_psum"), credit=2)
            xproj_ready = Signal(sem("xproj_ready"), credit=1)
            score_rows = Signal(sem("score_rows"), credit=2)
            max_read = Signal(sem("max_read"))
            negmax_ready = Signal(sem("negmax_ready"))
            score_cols = Signal(sem("score_cols"))
            e_ready = Signal(sem("e_ready"), credit=2)
            wctx_ready = Signal(sem("wctx_ready"), credit=2)
            cum_psum = Signal(sem("cum_psum"), credit=2)
            pre_ready = Signal(sem("pre_ready"), credit=2)
            attn_ready = Signal(sem("attn_ready"), credit=2)
            ln2_ready = Signal(sem("ln2_ready"))
            ln2_applied = Signal(sem("ln2_applied"))
            ln3_ready = Signal(sem("ln3_ready"))
            xn_ready = Signal(sem("xn_ready"))
            hi_ready = Signal(sem("hi_ready"))
            split_ready = Signal(sem("split_ready"), credit=1)
            xnT_psum = Signal(sem("xnT_psum"), credit=1, per=2)
            xnT_ready = Signal(sem("xnT_ready"), per=2)
            logitsT_psum = Signal(sem("logitsT_psum"), credit=1, per=2)
            logitsT_ready = Signal(sem("logitsT_ready"), per=2)
            logits_psum = Signal(sem("logits_psum"), credit=1)
            chosen_ready = Signal(sem("chosen_ready"))
            gaps_ready = Signal(sem("gaps_ready"))
            exps_ready = Signal(sem("exps_ready"))
            wsel_ready = Signal(sem("wsel_ready"))
            rank_psum = Signal(sem("rank_psum"))
            rows_ready = Signal(sem("rows_ready"))
            wselT_psum = Signal(sem("wselT_psum"))
            wselT_ready = Signal(sem("wselT_ready"), credit=1)
            b2_psum = Signal(sem("b2_psum"), per=2)
            b2_ready = Signal(sem("b2_ready"), credit=1, per=2)
            wT_psum = Signal(sem("wT_psum"), credit=1, per=4)
            whi_ready = Signal(sem("whi_ready"), per=4)
            wlo_ready = Signal(sem("wlo_ready"), credit=1, per=4)
            scattered = [Signal(sem(f"scattered{u}"), per=16 * PT * K) for u in range(2)]
            rows_sent = Signal(sem("rows_sent"), credit=2)
            attn_steps = sem("attn_steps")
            norms_steps = sem("norms_steps")
            route_steps = sem("route_steps")
            rest_steps = sem("rest_steps")
            rows_clear = sem("rows_clear")

            def at(i, n):
                return isinstance(i, int) and i == n

            def steps(eng, step):
                step(0, None, None, None, 1)
                step(1, 0, None, None, 0)
                step(2, 1, 0, None, 1)
                with eng.Fori(0, PAIRS // 2 - 2) as h:
                    step(h * 2 + 3, h * 2 + 2, h * 2 + 1, h * 2, 0)
                    step(h * 2 + 4, h * 2 + 3, h * 2 + 2, h * 2 + 1, 1)
                step(PAIRS - 1, PAIRS - 2, PAIRS - 3, PAIRS - 4, 0)
                step(None, PAIRS - 1, PAIRS - 2, PAIRS - 3, 1)
                step(None, None, PAIRS - 1, PAIRS - 2, 0)
                step(None, None, None, PAIRS - 1, 1)

            with nc.Block() as block:
                def pad(eng, experts):
                    for e in experts:
                        at = eng.value_load(pad_at[0:1, e:e + 1], min_val=e * REGION, max_val=e * REGION + TOKENS)
                        eng.dma_start(dispatch[bass.ds(at, SLOTS), :].rearrange("(h p) w -> p h w", p=P), blank)\
                           .then_inc(padded, 16)

                @block.sync
                def _(sp):
                    with sp.Fori(0, PAIRS) as n:
                        sp.wait_ge(wT_psum.sem, wT_psum.free(n, 1))
                        sp.dma_start(stage[:, 0].rearrange("p e (c d) -> p e c d", c=FC),
                                     w1_src[:, bass.ds(n * 2, 2)]).then_inc(stage_in, 16)
                        sp.dma_start(stage[:, 1], w2_src[:, bass.ds(n * 2, 2), :]).then_inc(stage_in, 16)

                    sp.wait_ge(pads_at, 1)
                    pad(sp, range(0, E // 2))
                    sp.dma_start(dispatch[E * REGION:E * REGION + SLOTS, :].rearrange("(h p) w -> p h w", p=P), blank)\
                      .then_inc(padded, 16)
                    sp.wait_ge(padded, 16 * (E + 1))

                @block.tensor
                def _(pe):
                    pe.sem_inc(xproj_psum.sem, xproj_psum.start)
                    pe.sem_inc(xT_psum.sem, xT_psum.start)
                    pe.sem_inc(score_rows.sem, score_rows.start)
                    pe.sem_inc(cum_psum.sem, cum_psum.start)
                    pe.sem_inc(xnT_psum.sem, xnT_psum.start)
                    pe.sem_inc(logits_psum.sem, logits_psum.start)
                    pe.sem_inc(logitsT_psum.sem, logitsT_psum.start)
                    pe.sem_inc(wT_psum.sem, wT_psum.start)

                    def turn_x(b, i):
                        n = i * 2 + b
                        pe.wait_ge(xn1_ready.sem, xn1_ready.done(n))
                        pe.wait_ge(pre_ready.sem, pre_ready.free(n, 2))
                        for t in range(BT):
                            ins = pe.transpose(psA[b][:, t * P:(t + 1) * P], xn1[b][:, t, :], ident[:])
                        ins.then_inc(xT_psum.sem, 1)

                    def hidden(b, i):
                        n = i * 2 + b
                        pe.wait_ge(xT_ready.sem, xT_ready.done(n))
                        pe.matmul(psA[b][:], W1T[:], xT[b][:], start=True, stop=True).then_inc(h_psum.sem, 1)

                    def project_ctx(b, i):
                        n = i * 2 + b
                        pe.wait_ge(wctx_ready.sem, wctx_ready.free(n, 2))
                        for t in range(BT):
                            ins = pe.matmul(psZ[b][:, t, :], xT[b][:, t * P:(t + 1) * P], WcT[:, D:2 * D], start=True, stop=True)
                        ins.then_inc(zctx_psum.sem, 1)

                    def project_x(b, i):
                        n = i * 2 + b
                        pe.wait_ge(xproj_ready.sem, xproj_ready.free(n, 1))
                        for t in range(BT):
                            o = psD[:, t * D:(t + 1) * D]
                            pe.matmul(o, xT[b][:, t * P:(t + 1) * P], WcT[:, 0:D], start=True, stop=False)
                            ins = pe.matmul(o, ones[0:1, :], bc_row[:], start=False, stop=True)
                        ins.then_inc(xproj_psum.sem, 1)

                    def scores_row(b, i):
                        n = i * 2 + b
                        pe.wait_ge(hT_ready.sem, hT_ready.done(n))
                        pe.matmul(psA[b][:], w2_rep[:], hT[b][:], start=True, stop=True).then_inc(score_rows.sem, 1)

                    def scores_col(b, i):
                        n = i * 2 + b
                        pe.wait_ge(max_read.sem, max_read.done(n))
                        for t in range(BT):
                            ins = pe.matmul(psA[b][:, t:t + 1], hT[b][:, t * P:(t + 1) * P], w2_col[:],
                                            start=True, stop=True)
                        ins.then_inc(score_cols.sem, 1)

                    def cumulate(b, i):
                        n = i * 2 + b
                        pe.wait_ge(wctx_ready.sem, wctx_ready.done(n))
                        pe.wait_ge(pre_ready.sem, pre_ready.free(n, 1))
                        for s in range(BT):
                            m = upto if s == 0 else ones
                            pe.matmul(psC[:, s:, :], m[:], wctx[b][:, 0:BT - s, :], start=(s == 0), stop=(s == BT - 1))
                        for s in range(BT):
                            m = upto if s == 0 else ones
                            ins = pe.matmul(psA[b][:, DEN + s:DEN + BT], m[:], e4[b][:, 0:BT - s], start=(s == 0), stop=(s == BT - 1))
                        ins.then_inc(cum_psum.sem, 1)

                    def turn_w(k, r):
                        if k == 0:
                            pe.wait_ge(stage_in, r * 32 + 32)
                            pe.wait_ge(wlo_ready.sem, wlo_ready.free(r, 1))
                        else:
                            pe.wait_ge(wlo_ready.sem, wlo_ready.done(r, k - 1))
                        for cc in range(FC):
                            ins = pe.transpose(psN[:, cc * P:(cc + 1) * P],
                                               stage[:, k // 2, k % 2, cc * P:(cc + 1) * P], ident[:])
                        ins.then_inc(wT_psum.sem, 1)

                    def turn_xn(h, r):
                        if h == 0:
                            pe.wait_ge(xn_ready.sem, xn_ready.done(r))
                            pe.wait_ge(b2_ready.sem, b2_ready.free(r, 1))
                            if not at(r, PAIRS - 1):
                                pe.wait_ge(xproj_ready.sem, xproj_ready.done(r * 2 + 3))
                        else:
                            pe.wait_ge(xnT_ready.sem, xnT_ready.done(r, 0))
                        for t in range(BT):
                            ins = pe.transpose(psD[:, t * P:(t + 1) * P], normed[:, h * BT + t, :], ident[:])
                        ins.then_inc(xnT_psum.sem, 1)

                    def route_logits(h, r):
                        if h == 0:
                            pe.wait_ge(xnT_ready.sem, xnT_ready.done(r))
                        else:
                            pe.wait_ge(logitsT_ready.sem, logitsT_ready.done(r, 0))
                        pe.matmul(psD[0:E, :], LW[:], xnT[h][:], start=True, stop=False)
                        pe.matmul(psD[0:E, :], neg1[:], xnS[h][:], start=False, stop=True).then_inc(logitsT_psum.sem, 1)

                    def turn_logits(r):
                        pe.wait_ge(logitsT_ready.sem, logitsT_ready.done(r))
                        pe.wait_ge(wselT_ready.sem, wselT_ready.free(r, 1))
                        apart(pe)
                        for j in range(PT):
                            ins = pe.transpose(psL[:, j * E:(j + 1) * E], logitsT[:, j * P:(j + 1) * P], ident[0:E, 0:E])
                        ins.then_inc(logits_psum.sem, 1)

                    def ranks(r):
                        pe.wait_ge(chosen_ready.sem, chosen_ready.done(r))
                        o = psL[:, 0:PT * E]
                        pe.matmul(o, before16[:], chosen16[:].rearrange("p j e -> p (j e)"), start=True, stop=False)
                        for s in range(1, PT):
                            pe.matmul(psL[:, s * E:PT * E], ones16[:], chosen16[:, 0:PT - s, :].rearrange("p j e -> p (j e)"),
                                      start=False, stop=False)
                        pe.matmul(o.rearrange("p (j e) -> p j e", e=E), ones16[:],
                                  count16[:].unsqueeze(1).to_broadcast([P, PT, E]), start=False, stop=True)\
                            .then_inc(rank_psum.sem, 1)

                    def turn_wsel(r):
                        pe.wait_ge(wsel_ready.sem, wsel_ready.done(r))
                        pe.wait_ge(rows_ready.sem, rows_ready.done(r))
                        pe.transpose(psL[:, 0:P], wsel[:].rearrange("p j e -> p (j e)"), ident[:]).then_inc(wselT_psum.sem, 1)

                    def b2_rows(h, r):
                        if h == 0:
                            if not (isinstance(r, int) and r >= PAIRS - 2):
                                pe.wait_ge(xproj_ready.sem, xproj_ready.done(r * 2 + 5))
                            pe.wait_ge(wselT_ready.sem, wselT_ready.done(r))
                        else:
                            pe.wait_ge(b2_ready.sem, b2_ready.done(r, 0))
                        pe.matmul(psD[:], wselT[:], b2_sel[:, h * BT:(h + 1) * BT, :].rearrange("p j d -> p (j d)"),
                                  start=True, stop=True).then_inc(b2_psum.sem, 1)

                    def step(x, i, n, c, u):
                        if c is not None:
                            turn_xn(0, c)
                        if i is not None:
                            turn_x(0, i)
                            turn_x(1, i)
                        if c is not None:
                            turn_xn(1, c)
                        if i is not None:
                            hidden(0, i)
                            hidden(1, i)
                        if c is not None:
                            route_logits(0, c)
                        if i is not None:
                            scores_row(0, i)
                            scores_row(1, i)
                        if c is not None:
                            route_logits(1, c)
                        if i is not None:
                            scores_col(0, i)
                            project_ctx(0, i)
                            project_ctx(1, i)
                            scores_col(1, i)
                        if c is not None:
                            turn_logits(c)
                            turn_w(0, c)
                        if i is not None:
                            project_x(0, i)
                        if c is not None:
                            turn_w(1, c)
                        if i is not None:
                            project_x(1, i)
                        if c is not None:
                            ranks(c)
                        if i is not None:
                            cumulate(0, i)
                        if c is not None:
                            turn_w(2, c)
                            turn_wsel(c)
                        if i is not None:
                            cumulate(1, i)
                        if c is not None:
                            b2_rows(0, c)
                            turn_w(3, c)
                            b2_rows(1, c)

                    steps(pe, step)

                    table = psC[:].rearrange("p (a b) d -> p a (b d)", a=2)
                    pe.wait_ge(rows_ready.sem, rows_ready.done(PAIRS - 1))
                    pe.wait_ge(pre_ready.sem, pre_ready.done(NB - 1))
                    pe.matmul(psA[0][:, 0:E], ones16[:], count16[:], start=True, stop=True).then_inc(tab_count, 1)
                    pe.wait_ge(tab_spread, 1)
                    for a in range(2):
                        pe.matmul(table[:, a, 0:P], spread[:, a, 0, :], ident[:], start=True, stop=True)
                        ins = pe.matmul(table[:, a, P:TILES], spread[:, a, 1, :], ident[:, 0:TILES - P], start=True, stop=True)
                    ins.then_inc(tab_rows, 1)

                @block.scalar
                def _(act):
                    act.sem_inc(xproj_ready.sem, xproj_ready.start)
                    act.sem_inc(wctx_ready.sem, wctx_ready.start)
                    act.sem_inc(e_ready.sem, e_ready.start)
                    act.sem_inc(attn_ready.sem, attn_ready.start)
                    act.sem_inc(wselT_ready.sem, wselT_ready.start)
                    act.sem_inc(b2_ready.sem, b2_ready.start)

                    def norm1(b, i):
                        n = i * 2 + b
                        act.wait_ge(xT_psum.sem, xT_psum.free(n, 2))
                        if at(i, FIRST // PT):
                            act.wait_ge(ln1_ready, 2)
                        apart(act)
                        for t in range(BT):
                            j = i * PT + (b * BT + t)
                            ins = act.activation(xn1[b][:, t, :], X[:, bass.ds(j, 1), :].rearrange("p a d -> p (a d)"),
                                                 ACT.Identity, bias=nmr1[:, bass.ds(j, 1)], scale=rstd1[:, bass.ds(j, 1)])
                        ins.then_inc(xn1_ready.sem, 1)

                    def copy_xT(b, i):
                        n = i * 2 + b
                        act.wait_ge(xT_psum.sem, xT_psum.done(n))
                        act.wait_ge(xproj_psum.sem, xproj_psum.free(n, 2))
                        act.activation(xT[b][:], psA[b][:], ACT.Copy).then_inc(xT_ready.sem, 1)

                    def tanh_h(b, i):
                        n = i * 2 + b
                        act.wait_ge(h_psum.sem, h_psum.done(n))
                        act.wait_ge(e_ready.sem, e_ready.free(n, 2))
                        act.activation(hT[b][:], psA[b][:], ACT.Tanh, bias=b1_col[:]).then_inc(hT_ready.sem, 1)

                    def copy_xproj(b, i):
                        n = i * 2 + b
                        act.wait_ge(xproj_psum.sem, xproj_psum.done(n))
                        act.wait_ge(pre_ready.sem, pre_ready.free(n, 2))
                        act.activation(xproj[b][:].rearrange("p t d -> p (t d)"), psD[:], ACT.Copy).then_inc(xproj_ready.sem, 1)

                    def exp_scores(b, i):
                        n = i * 2 + b
                        act.wait_ge(score_cols.sem, score_cols.done(n))
                        act.wait_ge(negmax_ready.sem, negmax_ready.done(n))
                        act.wait_ge(cum_psum.sem, cum_psum.free(n, 2))
                        act.activation(e4[b][:], psA[b][:, 0:BT], ACT.Exp, bias=mx[b][:, 2:3]).then_inc(e_ready.sem, 1)

                    def weigh(b, i):
                        n = i * 2 + b
                        act.wait_ge(e_ready.sem, e_ready.done(n))
                        act.wait_ge(zctx_psum.sem, zctx_psum.done(n))
                        act.wait_ge(cum_psum.sem, cum_psum.free(n, 2))
                        for t in range(BT):
                            ins = act.activation(wctx[b][:, t, :], psZ[b][:, t, :], ACT.Copy, scale=e4[b][:, t:t + 1])
                        ins.then_inc(wctx_ready.sem, 1)

                    def tanh_out(b, i):
                        n = i * 2 + b
                        act.wait_ge(pre_ready.sem, pre_ready.done(n))
                        apart(act)
                        act.activation(R[:, bass.ds(i * PT + b * BT, BT), :], pre[b][:], ACT.Tanh).then_inc(attn_ready.sem, 1)

                    def norm2(r):
                        act.wait_ge(ln2_ready.sem, ln2_ready.done(r))
                        act.wait_ge(split_ready.sem, split_ready.free(r, 1))
                        act.wait_ge(xnT_psum.sem, xnT_psum.free(r, 1))
                        apart(act)
                        for j in range(PT):
                            ins = act.activation(normed[:, j, :], R[:, bass.ds(r * PT + j, 1), :].rearrange("p a d -> p (a d)"),
                                                 ACT.Identity, bias=ln2[:, 1, j:j + 1], scale=ln2[:, 0, j:j + 1])
                        ins.then_inc(ln2_applied.sem, 1)

                    def norm3(r):
                        act.wait_ge(ln3_ready.sem, ln3_ready.done(r))
                        apart(act)
                        for j in range(PT):
                            ins = act.activation(normed[:, j, :], X[:, bass.ds(r * PT + j, 1), :].rearrange("p a d -> p (a d)"),
                                                 ACT.Identity, bias=ln3[:, 1, j:j + 1], scale=ln3[:, 0, j:j + 1])
                        ins.then_inc(xn_ready.sem, 1)

                    def high_xn(r, u):
                        act.wait_ge(xn_ready.sem, xn_ready.done(r))
                        act.wait_ge(rows_sent.sem, rows_sent.free(r, 2))
                        act.activation(rows16[u][:, :, HI:HI + D], normed[:], ACT.Copy).then_inc(hi_ready.sem, 1)

                    def squares(groups):
                        for m in groups:
                            act.wait_ge(raw_in[m // 4], 32)
                            for a in range(2):
                                flat = w_raw[a][m // 4][:, m % 4 * 2:m % 4 * 2 + 2].rearrange("p e f -> p (e f)")
                                ins = act.activation(flat, flat, ACT.Square, accum_out=group_sq[:, a, m:m + 1])
                            ins.then_inc(squared, 1)

                    def split_w(k, r):
                        if k == 0:
                            act.wait_ge(setup_ready, 1)
                        act.wait_ge(wT_psum.sem, wT_psum.done(r, k))
                        w = (W1H if k < 2 else W2H)[:, bass.ds(r * 2 + k % 2, 1), :].rearrange("p a f -> p (a f)")
                        apart(act)
                        act.activation(w, psN[:], ACT.Copy, scale=scales[:, k // 2:k // 2 + 1]).then_inc(whi_ready.sem, 1)

                    def copy_xnT(h, r):
                        act.wait_ge(xnT_psum.sem, xnT_psum.done(r, h))
                        act.wait_ge(logitsT_psum.sem, logitsT_psum.free(r, 1))
                        act.activation(xnT[h][:], psD[:], ACT.Copy)
                        act.activation(xnS[h][:], psD[:], ACT.Square).then_inc(xnT_ready.sem, 1)

                    def copy_logitsT(h, r):
                        act.wait_ge(logitsT_psum.sem, logitsT_psum.done(r, h))
                        act.wait_ge(logits_psum.sem, logits_psum.free(r, 1))
                        act.activation(logitsT[:, h * T:(h + 1) * T], psD[0:E, :], ACT.Identity, bias=key_bias[:])\
                            .then_inc(logitsT_ready.sem, 1)

                    def exp_gaps(r):
                        act.wait_ge(gaps_ready.sem, gaps_ready.done(r))
                        act.activation(gap4[:], gap4[:], ACT.Exp)
                        act.activation(gap16[:], gap16[:], ACT.Exp).then_inc(exps_ready.sem, 1)

                    def copy_wselT(r):
                        act.wait_ge(wselT_psum.sem, wselT_psum.done(r))
                        act.activation(wselT[:], psL[:, 0:P], ACT.Copy).then_inc(wselT_ready.sem, 1)

                    def copy_b2(h, r):
                        act.wait_ge(b2_psum.sem, b2_psum.done(r, h))
                        apart(act)
                        act.activation(R[:, bass.ds(r * PT + h * BT, BT), :].rearrange("p j d -> p (j d)"),
                                       psD[:], ACT.Copy).then_inc(b2_ready.sem, 1)

                    def step(x, i, n, c, u):
                        if c is not None:
                            copy_xnT(0, c)
                        if i is not None:
                            copy_xT(0, i)
                            copy_xT(1, i)
                        if c is not None:
                            copy_xnT(1, c)
                        if i is not None:
                            tanh_h(0, i)
                            tanh_h(1, i)
                        if n is not None:
                            norm2(n)
                        if c is not None:
                            copy_logitsT(0, c)
                            copy_logitsT(1, c)
                        if i is not None:
                            exp_scores(0, i)
                            weigh(0, i)
                            exp_scores(1, i)
                            weigh(1, i)
                        if c is not None:
                            split_w(0, c)
                        if i is not None:
                            copy_xproj(0, i)
                        if n is not None:
                            norm3(n)
                        if c is not None:
                            split_w(1, c)
                        if i is not None:
                            copy_xproj(1, i)
                        if at(i, 0):
                            squares(range(0, 2))
                        if c is not None:
                            exp_gaps(c)
                            split_w(2, c)
                        if at(i, 1):
                            squares(range(4, 7))
                        if i is not None:
                            tanh_out(0, i)
                        if c is not None:
                            copy_wselT(c)
                        if x is not None:
                            norm1(0, x)
                        if at(i, 0):
                            squares(range(2, 4))
                        if n is not None:
                            high_xn(n, 1 - u)
                        if at(i, 1):
                            squares(range(7, 8))
                        if c is not None:
                            copy_b2(0, c)
                        if i is not None:
                            tanh_out(1, i)
                        if c is not None:
                            split_w(3, c)
                            copy_b2(1, c)
                        if x is not None:
                            norm1(1, x)

                    steps(act, step)

                    act.wait_ge(pads_at, 1)
                    pad(act, range(E // 2, E))

                @block.vector
                def _(v):
                    v.memset(rows[0][:], 0.0)
                    v.memset(rows[1][:], 0.0).then_inc(rows_clear, 1)
                    v.wait_ge(rows_clear, 1)
                    v.sem_inc(pre_ready.sem, pre_ready.start)
                    v.sem_inc(split_ready.sem, split_ready.start)
                    v.sem_inc(wlo_ready.sem, wlo_ready.start)
                    attn_at, norm_at, route_at = [None], [None], [None]
                    rest_chain = Chain(rest_steps, 0, 0)
                    rest = onehot[:].rearrange("p j k e -> p (j k e)")[:, 0:(NT - FIRST) * 6].rearrange("p (t s) -> p t s", s=6)
                    rest_scr = picked[:].rearrange("p j k e -> p (j k e)")[:, 0:(NT - FIRST) * 6].rearrange("p (s t) -> p s t", s=6)
                    ATTN = 4

                    def row_max(b, i):
                        n = i * 2 + b
                        if b == 0:
                            attn_at[0] = Chain(attn_steps, i * ATTN, ATTN)
                        c = attn_at[0]
                        v.wait_ge(score_rows.sem, score_rows.done(n))
                        v.wait_ge(e_ready.sem, e_ready.free(n, 2))
                        v.tensor_reduce(mx[b][:, 0:1], psA[b][:], AX.X, ALU.max).then_inc(max_read.sem, 1)
                        v.wait_ge(max_read.sem, max_read.done(n))
                        v.tensor_tensor(mx[b][:, 1:2], mx[b][:, 0:1], b2_col[:], ALU.add).then_inc(c.sem, c.step())
                        v.wait_ge(c.sem, c.now())
                        v.tensor_tensor(mx[b][:, 2:3], b2_col[:], mx[b][:, 1:2], ALU.subtract).then_inc(negmax_ready.sem, 1)

                    def combine(b, i):
                        n = i * 2 + b
                        c = attn_at[0]
                        v.wait_ge(cum_psum.sem, cum_psum.done(n))
                        v.reciprocal(rden[b][:], psA[b][:, DEN:DEN + BT]).then_inc(c.sem, c.step())
                        v.wait_ge(c.sem, c.now())
                        v.wait_ge(xproj_ready.sem, xproj_ready.done(n))
                        v.wait_ge(attn_ready.sem, attn_ready.free(n, 2))
                        for t in range(BT):
                            ins = v.scalar_tensor_tensor(pre[b][:, t, :], psC[:, t, :], rden[b][:, t:t + 1],
                                                         xproj[b][:, t, :], ALU.mult, ALU.add)
                        ins.then_inc(pre_ready.sem, 1)
                        if b == 1:
                            c.end()

                    def stats2(r):
                        c = norm_at[0] = Chain(norms_steps, r * (2 * NORM_STEPS + 1), 2 * NORM_STEPS + 1)
                        v.wait_ge(attn_ready.sem, attn_ready.done(r * 2 + 1))
                        apart(v)
                        for j in range(PT):
                            ins = v.bn_stats(stats[:, j, :], R[:, bass.ds(r * PT + j, 1), :].rearrange("p a d -> p (a d)"))
                        ins.then_inc(c.sem, c.step())
                        norm_steps(v, c, stats, ln2[:, 0, :], ln2[:, 1, :], scr, ln2_ready.sem)

                    def stats3(r):
                        c = norm_at[0]
                        v.wait_ge(ln2_applied.sem, ln2_applied.done(r))
                        x2 = X[:, bass.ds(r * PT, PT), :]
                        v.tensor_tensor(x2, x2, normed[:], ALU.add).then_inc(c.sem, c.step())
                        v.wait_ge(c.sem, c.now())
                        apart(v)
                        for j in range(PT):
                            ins = v.bn_stats(stats[:, j, :], X[:, bass.ds(r * PT + j, 1), :].rearrange("p a d -> p (a d)"))
                        ins.then_inc(c.sem, c.step())
                        norm_steps(v, c, stats, ln3[:, 0, :], ln3[:, 1, :], scr, ln3_ready.sem)

                    def split_w(k, r):
                        v.wait_ge(whi_ready.sem, whi_ready.done(r, k))
                        h, l = (W1H, W1L) if k < 2 else (W2H, W2L)
                        at = bass.ds(r * 2 + k % 2, 1)
                        v.scalar_tensor_tensor(l[:, at, :].rearrange("p a f -> p (a f)"), psN[:], scales[:, k // 2:k // 2 + 1],
                                               h[:, at, :].rearrange("p a f -> p (a f)"), ALU.mult, ALU.subtract)\
                            .then_inc(wlo_ready.sem, 1)

                    def split_xn(r, u):
                        c = norm_at[0]
                        v.wait_ge(hi_ready.sem, hi_ready.done(r))
                        v.tensor_tensor(rows16[u][:, :, LO:LO + D], normed[:], rows16[u][:, :, HI:HI + D], ALU.subtract)\
                            .then_inc(split_ready.sem, 1)
                        c.end()

                    def choose(r, u):
                        c = route_at[0] = Chain(route_steps, r * ROUTE_STEPS, ROUTE_STEPS)
                        v.wait_ge(logits_psum.sem, logits_psum.done(r))
                        v.tensor_copy(logits[:].rearrange("p j e -> p (j e)"), psL[:, 0:PT * E]).then_inc(c.sem, c.step())
                        v.wait_ge(c.sem, c.now())
                        apart(v)
                        for j in range(PT):
                            ins = v.max(top[:, j, :], logits[:, j, :])
                        ins.then_inc(c.sem, c.step())
                        v.wait_ge(c.sem, c.now())
                        apart(v)
                        for j in range(PT):
                            ins = v.max_index(top_e[:, j, :], top[:, j, :], logits[:, j, :])
                        ins.then_inc(c.sem, c.step())
                        best = top[:, :, 0:1]
                        v.tensor_tensor(gap4[:], top[:, :, 0:K], best.to_broadcast([P, PT, K]), ALU.subtract).then_inc(c.sem, c.step())
                        v.tensor_tensor(gap16[:], logits[:], best.to_broadcast([P, PT, E]), ALU.subtract).then_inc(gaps_ready.sem, 1)
                        v.wait_ge(c.sem, c.now())
                        expert = rows[u][:, :, EXPERT:EXPERT + K]
                        v.tensor_copy(expert, top_e[:, :, 0:K]).then_inc(c.sem, c.step())
                        v.tensor_copy(rows[u][:, :, EXPERT + K:DEST], top_e[:, :, 0:K]).then_inc(c.sem, c.step())
                        v.tensor_copy(rows[u][:, :, DEST:DEST + K], dest[:]).then_inc(c.sem, c.step())
                        v.wait_ge(c.sem, c.now())
                        v.tensor_tensor(onehot[:], iota_e[:].unsqueeze(1).unsqueeze(1).to_broadcast([P, PT, K, E]),
                                        expert.unsqueeze(3).to_broadcast([P, PT, K, E]), ALU.is_equal).then_inc(c.sem, c.step())
                        v.tensor_scalar(dest[:], dest[:], float(PT * P * K), None, ALU.add).then_inc(c.sem, c.step())
                        v.wait_ge(c.sem, c.now())
                        v.tensor_reduce(chosen[:], onehot[:].rearrange("p j k e -> p j e k"), AX.X, ALU.add).then_inc(c.sem, c.step())
                        v.wait_ge(c.sem, c.now())
                        v.tensor_copy(chosen16[:], chosen[:]).then_inc(chosen_ready.sem, 1)

                    def weights(r, u):
                        c = route_at[0]
                        v.wait_ge(exps_ready.sem, exps_ready.done(r))
                        total, inv, inv_out = rsum[:, 0, :], rsum[:, 1, :], rsum[:, 2, :]
                        v.tensor_reduce(total, gap4[:], AX.X, ALU.add).then_inc(c.sem, c.step())
                        v.tensor_tensor(wsel[:], gap16[:], chosen[:], ALU.mult).then_inc(c.sem, c.step())
                        v.wait_ge(c.sem, c.now())
                        v.reciprocal(inv, total).then_inc(c.sem, c.step())
                        v.wait_ge(c.sem, c.now())
                        v.tensor_scalar(inv_out, inv, unscale[:, 3:4], None, ALU.mult).then_inc(c.sem, c.step())
                        v.tensor_tensor(wsel[:], wsel[:], inv.unsqueeze(2).to_broadcast([P, PT, E]), ALU.mult).then_inc(wsel_ready.sem, 1)
                        v.wait_ge(c.sem, c.now())
                        v.tensor_tensor(rows[u][:, :, WEIGHT:WEIGHT + K], gap4[:],
                                        inv_out.unsqueeze(2).to_broadcast([P, PT, K]), ALU.mult).then_inc(c.sem, c.step())

                    def places(r, u):
                        c = route_at[0]
                        v.wait_ge(rank_psum.sem, rank_psum.done(r))
                        v.tensor_tensor(slot[:], psL[:, 0:PT * E].rearrange("p (j e) -> p j e", e=E),
                                        region_e[:].unsqueeze(1).to_broadcast([P, PT, E]), ALU.add).then_inc(c.sem, c.step())
                        v.tensor_reduce(pair_count[:], chosen[:].rearrange("p j e -> p e j"), AX.X, ALU.add).then_inc(c.sem, c.step())
                        v.wait_ge(c.sem, c.now())
                        v.tensor_tensor(picked[:], onehot[:], slot[:].unsqueeze(2).to_broadcast([P, PT, K, E]), ALU.mult).then_inc(c.sem, c.step())
                        v.tensor_tensor(count[:], count[:], pair_count[:], ALU.add).then_inc(c.sem, c.step())
                        v.wait_ge(c.sem, c.now())
                        v.tensor_reduce(slot4[:], picked[:], AX.X, ALU.add).then_inc(c.sem, c.step())
                        v.tensor_copy(count16[:], count[:]).then_inc(c.sem, c.step())
                        v.wait_ge(c.sem, c.now())
                        v.tensor_copy(place[u][:], slot4[:].rearrange("p j k -> p (j k)")).then_inc(rows_ready.sem, 1)
                        c.end()

                    def rest_stats(q):
                        v.wait_ge(x_in[q], 16)
                        for t in range(q * FIRST, (q + 1) * FIRST):
                            ins = v.bn_stats(rest[:, t - FIRST, :], X[:, t, :])
                        ins.then_inc(rest_steps, rest_chain.step())

                    def rest_norm():
                        norm_steps(v, rest_chain, rest, rstd1[:, FIRST:], nmr1[:, FIRST:], rest_scr, ln1_ready)

                    def weight_bounds():
                        c = rest_chain
                        v.wait_ge(squared, E // 2)
                        v.tensor_tensor(fb1_sq[:], b1T[:], b1T[:], ALU.mult).then_inc(c.sem, c.step())
                        v.tensor_reduce(bound[:, 0:2], group_sq[:], AX.X, ALU.max).then_inc(c.sem, c.step())
                        v.wait_ge(c.sem, c.now())
                        v.tensor_reduce(bound[:, 2:3], fb1_sq[:], AX.X, ALU.max).then_inc(c.sem, c.step())
                        v.wait_ge(c.sem, c.now())
                        v.tensor_scalar(bound[:, 2:3], bound[:, 2:3], 2.0, None, ALU.mult).then_inc(bounds_in, 1)
                        v.wait_ge(bounds_all, 1)
                        v.scalar_tensor_tensor(bound_all[:, 2:3], bound_all[:, 0:1], 2.0 * LN_BOUND_SQ,
                                               bound_all[:, 2:3], ALU.mult, ALU.add).then_inc(c.sem, c.step())
                        v.wait_ge(c.sem, c.now())
                        v.tensor_single_scalar(sbits[:], bound_all[:].bitcast(I32), 23, ALU.logical_shift_right).then_inc(c.sem, c.step())
                        v.wait_ge(c.sem, c.now())
                        v.tensor_scalar(sbits[:], sbits[:], 1.0, None, ALU.add).then_inc(c.sem, c.step())
                        v.wait_ge(c.sem, c.now())
                        v.tensor_single_scalar(sbits[:], sbits[:], 1, ALU.logical_shift_right).then_inc(c.sem, c.step())
                        v.wait_ge(c.sem, c.now())
                        v.tensor_scalar(sbits[:], sbits[:], -1.0, 205.0, ALU.mult, ALU.add).then_inc(c.sem, c.step())
                        v.wait_ge(c.sem, c.now())
                        v.tensor_single_scalar(scales[:].bitcast(I32), sbits[:], 23, ALU.logical_shift_left).then_inc(c.sem, c.step())
                        v.wait_ge(c.sem, c.now())
                        v.reciprocal(unscale[:, 0:3], scales[:]).then_inc(c.sem, c.step())
                        v.wait_ge(c.sem, c.now())
                        v.tensor_tensor(unscale[:, 3:4], unscale[:, 1:2], unscale[:, 2:3], ALU.mult).then_inc(setup_ready, 1)

                    def step(x, i, n, c, u):
                        if n is not None:
                            stats2(n)
                        if i is not None:
                            row_max(0, i)
                            row_max(1, i)
                        if at(i, 0):
                            rest_stats(2)
                            rest_stats(1)
                        if n is not None:
                            stats3(n)
                        if c is not None:
                            split_w(0, c)
                            choose(c, u)
                            split_w(1, c)
                            weights(c, u)
                            places(c, u)
                        if i is not None:
                            combine(0, i)
                        if c is not None:
                            split_w(2, c)
                        if at(i, 0):
                            rest_stats(3)
                        if i is not None:
                            combine(1, i)
                        if at(i, 0):
                            rest_norm()
                        if n is not None:
                            split_xn(n, 1 - u)
                        if c is not None:
                            split_w(3, c)
                        if at(i, 1):
                            weight_bounds()

                    steps(v, step)

                    table = psC[:].rearrange("p (a b) d -> p a (b d)", a=2)
                    c = Chain(tab_c, 0, 0)
                    v.memset(blank, 0.0).then_inc(c.sem, c.step())
                    v.memset(row_e, 0.0).then_inc(c.sem, c.step())
                    v.memset(one_e[:], 1.0).then_inc(c.sem, c.step())
                    v.wait_ge(c.sem, c.now())
                    v.memset(blank[:, :, EXPERT:DEST], -1.0).then_inc(c.sem, c.step())
                    v.wait_ge(tab_count, 1)
                    v.wait_ge(tab_iota, 2)
                    v.tensor_copy(n_e[:], psA[0][:, 0:E]).then_inc(c.sem, c.step())
                    v.tensor_copy(tile_n[:], tile_i[:, 0:C]).then_inc(c.sem, c.step())
                    v.tensor_copy(pad_f[:], tile_i[0:1, C:]).then_inc(c.sem, c.step())
                    v.wait_ge(c.sem, c.now())
                    v.scalar_tensor_tensor(pad_f[:], pad_f[:], 256.0, n_e[0:1, :], ALU.mult, ALU.add).then_inc(c.sem, c.step())
                    v.tensor_scalar(tiles_i[:], n_e[:], float(SLOTS - 1), None, ALU.add).then_inc(c.sem, c.step())
                    v.wait_ge(c.sem, c.now())
                    v.tensor_copy(pad_at[:], pad_f[:]).then_inc(pads_at, 1)
                    v.tensor_single_scalar(tiles_i[:], tiles_i[:], 8, ALU.logical_shift_right).then_inc(c.sem, c.step())
                    v.wait_ge(c.sem, c.now())
                    v.tensor_copy(tiles_f[:], tiles_i[:]).then_inc(c.sem, c.step())
                    v.wait_ge(c.sem, c.now())
                    v.tensor_tensor_scan(end_e[:], one_e[:], tiles_f[:], 0.0, ALU.mult, ALU.add).then_inc(c.sem, c.step())
                    v.wait_ge(c.sem, c.now())
                    v.tensor_tensor(past[:], tile_n[:].unsqueeze(2).to_broadcast([P, C, E]),
                                    end_e[:].unsqueeze(1).to_broadcast([P, C, E]), ALU.is_ge).then_inc(c.sem, c.step())
                    v.wait_ge(c.sem, c.now())
                    v.tensor_tensor(past_n[:], past[:], tiles_f[:].unsqueeze(1).to_broadcast([P, C, E]), ALU.mult).then_inc(c.sem, c.step())
                    v.tensor_reduce(before[:, 0, :], past[:], AX.X, ALU.add).then_inc(c.sem, c.step())
                    v.wait_ge(c.sem, c.now())
                    v.tensor_reduce(before[:, 1, :], past_n[:], AX.X, ALU.add).then_inc(c.sem, c.step())
                    v.tensor_scalar(cols[:, 0, :], before[:, 0, :], float(E - 1), None, ALU.min).then_inc(c.sem, c.step())
                    v.wait_ge(c.sem, c.now())
                    v.tensor_tensor(before[:, 1, :], tile_n[:], before[:, 1, :], ALU.subtract).then_inc(c.sem, c.step())
                    v.tensor_scalar(cols[:, 1, :], before[:, 0, :], float(REGION), None, ALU.mult).then_inc(c.sem, c.step())
                    v.wait_ge(c.sem, c.now())
                    v.scalar_tensor_tensor(cols[:, 1, :], before[:, 1, :], float(SLOTS), cols[:, 1, :], ALU.mult, ALU.add).then_inc(c.sem, c.step())
                    v.wait_ge(c.sem, c.now())
                    v.tensor_scalar(cols[:, 1, :], cols[:, 1, :], float(E * REGION), None, ALU.min).then_inc(c.sem, c.step())
                    v.wait_ge(c.sem, c.now())
                    for a in range(2):
                        for b in range(C):
                            ins = v.tensor_scalar(spread[:, a, b, :], ones[:], cols[:, a, b:b + 1], None, ALU.mult)
                    ins.then_inc(tab_spread, 1)
                    v.wait_ge(tab_rows, 1)
                    v.tensor_copy(tile_e[:], table[:, 0, 0:TILES])
                    v.tensor_copy(tile_tab[:], table[0:1, :, 0:TILES])
                    v.tensor_copy(row_e[:, 0:TILES // GROUP, :].rearrange("a g q -> a (g q)"), table[0:1, 0, 0:TILES])\
                        .then_inc(c.sem, c.step())
                    v.wait_ge(c.sem, c.now())
                    v.tensor_copy(packed[:], row_e[:, 0:TILES // GROUP, 0]).then_inc(c.sem, c.step())
                    for k in range(1, GROUP + 2):
                        g, q = divmod(k, GROUP)
                        v.wait_ge(c.sem, c.now())
                        v.scalar_tensor_tensor(packed[:], row_e[:, g:g + TILES // GROUP, q], float(16 ** k), packed[:],
                                               ALU.mult, ALU.add).then_inc(c.sem, c.step())
                    v.wait_ge(c.sem, c.now())
                    v.tensor_copy(turn_experts[:], packed[:]).then_inc(c.sem, c.step())

                @block.gpsimd
                def _(pool):
                    pool.iota(tile_i[:, 0:C], [[P, C]], base=0, channel_multiplier=1).then_inc(tab_iota, 1)
                    pool.iota(tile_i[:, C:], [[REGION // 256, E]], base=0, channel_multiplier=0).then_inc(tab_iota, 1)
                    pool.sem_inc(rows_sent.sem, rows_sent.start)

                    pool.wait_ge(bounds_in, 1)
                    pool.partition_all_reduce(bound_all[:], bound[:], P, bass.bass_isa.ReduceOp.max).then_inc(bounds_all, 1)

                    def send(r, u, before):
                        pool.wait_ge(rows_ready.sem, rows_ready.done(r))
                        apart(pool)
                        for j in range(PT):
                            if j == 1 and before is not None:
                                landed(before, 1 - u)
                            for k in range(K):
                                pool.indirect_dma_start(
                                    dispatch[:, :], bass.IndirectOffsetOnAxis(ap=place[u][:, j * K + k:j * K + k + 1], axis=0),
                                    rows[u][:, j, :], None).then_inc(scattered[u].sem, 16)

                    def landed(use, u):
                        pool.wait_ge(scattered[u].sem, scattered[u].done(use))
                        pool.sem_inc(rows_sent.sem, 1)

                    send(0, 0, None)
                    with pool.Fori(0, PAIRS // 2 - 1) as h:
                        send(h * 2 + 1, 1, h)
                        send(h * 2 + 2, 0, h)
                    send(PAIRS - 1, 1, PAIRS // 2 - 1)
                    landed(PAIRS // 2 - 1, 1)

        with ExitStack() as two:
            def s2(name, shape, dt=F32):
                return sb(name, shape, dt, two)

            rows2 = [s2(f"rows2_{q}", [P, 2, ROW]) for q in range(GROUP)]
            rows2h = [r[:].bitcast(F16) for r in rows2]
            meta = [s2(f"meta{q}", [P, 2 * 2]) for q in range(GROUP)]
            back = [s2(f"back{q}", [P, 2], U32) for q in range(GROUP)]
            match = [s2(f"match{q}", [P, 2, 2 * K]) for q in range(GROUP)]
            xT16 = [s2(f"xT16_{u}", [P, 2, SLOTS], F16) for u in range(2)]
            act_h = [s2(f"act_h{u}", [P, FC, SLOTS]) for u in range(2)]
            h_hi = [s2(f"h_hi{u}", [P, FC, SLOTS], F16) for u in range(2)]
            h_lo = [s2(f"h_lo{u}", [P, FC, SLOTS], F16) for u in range(2)]
            y = [s2(f"y{q}", [P, 2, D]) for q in range(GROUP)]
            psX = [pb(f"psX{u}", [P, 2, SLOTS], F16, two) for u in range(2)]
            psU = [pb(f"psU{u}", [P, FC, SLOTS], F32, two) for u in range(2)]
            psY = [pb(f"psY{s}", [P, 512], F32, two) for s in range(2)]

            rows_in = [sem(f"rows_in{q}") for q in range(GROUP)]
            turned = Signal(sem("turned"), credit=GROUP)
            xT16_ready = Signal(sem("xT16_ready"), credit=2)
            match_ready = Signal(sem("match_ready"), credit=GROUP)
            up_psum = Signal(sem("up_psum"), credit=2, per=2)
            gelu_ready = Signal(sem("gelu_ready"), credit=2, per=2)
            h_ready = Signal(sem("h_ready"), credit=2, per=2)
            down_psum = Signal(sem("down_psum"), credit=2)
            meta_ready = Signal(sem("meta_ready"), credit=1)
            y_ready = Signal(sem("y_ready"), credit=1)
            returned = [Signal(sem(f"returned{q}"), per=32) for q in range(GROUP)]
            y_sent = Signal(sem("y_sent"), credit=GROUP)
            tile_steps = sem("tile_steps")
            TSTEPS = 3
            LAST = TILES // TURN - 1

            def tile(t, k):
                return t * TURN + k, t * (TURN // GROUP) + k // GROUP, k % GROUP

            def experts(eng, word):
                both = eng.value_load(turn_experts[0:1, bass.ds(word, 1)], min_val=0, max_val=16 ** (GROUP + 2) - 1)
                return [eng.snap(both // 16 ** q % 16, min_val=0, max_val=E - 1) for q in range(GROUP + 2)]

            with nc.Block() as block:
                @block.sync
                def _(sp):
                    def load(n, h, q):
                        sp.wait_ge(turned.sem, turned.free(n, GROUP))
                        sp.wait_ge(match_ready.sem, match_ready.free(n, GROUP))
                        at = sp.value_load(tile_tab[0:1, 1, bass.ds(n, 1)], min_val=0, max_val=E * REGION)
                        sp.dma_start(rows2[q][:], dispatch[bass.ds(at, SLOTS), :].rearrange("(h p) w -> p h w", p=P))\
                          .then_inc(rows_in[q], 16)
                    with sp.Fori(0, TILES // TURN) as t:
                        for k in range(TURN):
                            load(*tile(t, k))

                @block.tensor
                def _(pe):
                    pe.sem_inc(turned.sem, turned.start)
                    pe.sem_inc(up_psum.sem, up_psum.start)
                    pe.sem_inc(down_psum.sem, down_psum.start)

                    def turn(n, h, q):
                        u = q % 2
                        pe.wait_ge(rows_in[q], h * 16 + 16)
                        pe.wait_ge(xT16_ready.sem, xT16_ready.free(n, 2))
                        for part in range(2):
                            for s in range(2):
                                ins = pe.transpose(psX[u][:, part, s * P:(s + 1) * P], rows2h[q][:, s, part * D:(part + 1) * D],
                                                   ident16[:])
                        ins.then_inc(turned.sem, 1)

                    def expert(n):
                        return pe.value_load(tile_tab[0:1, 0, bass.ds(n, 1)], min_val=0, max_val=E - 1)

                    def up(n, h, q, e):
                        u = q % 2
                        pe.wait_ge(xT16_ready.sem, xT16_ready.done(n))
                        hi, lo = xT16[u][:, 0, :], xT16[u][:, 1, :]
                        for cc in range(FC):
                            if cc % 2 == 0:
                                pe.wait_ge(gelu_ready.sem, gelu_ready.free(n, 2, cc // 2))
                            wh = W1H[:, bass.ds(e, 1), cc * P:(cc + 1) * P].rearrange("p a f -> p (a f)")
                            wl = W1L[:, bass.ds(e, 1), cc * P:(cc + 1) * P].rearrange("p a f -> p (a f)")
                            pe.matmul(psU[u][:, cc, :], wh, hi, start=True, stop=False)
                            pe.matmul(psU[u][:, cc, :], wh, lo, start=False, stop=False)
                            ins = pe.matmul(psU[u][:, cc, :], wl, hi, start=False, stop=True)
                            if cc % 2:
                                ins.then_inc(up_psum.sem, 1)

                    def down(n, h, q, e):
                        u = q % 2
                        pe.wait_ge(y_ready.sem, y_ready.free(n, 1))
                        for cc in range(FC):
                            if cc % 2 == 0:
                                pe.wait_ge(h_ready.sem, h_ready.done(n, cc // 2))
                            wh = W2H[:, bass.ds(e, 1), cc * P:(cc + 1) * P].rearrange("p a f -> p (a f)")
                            wl = W2L[:, bass.ds(e, 1), cc * P:(cc + 1) * P].rearrange("p a f -> p (a f)")
                            rows_of = [slice(s * P, (s + 1) * P) for s in range(2)]
                            for s in range(2):
                                pe.matmul(psY[s][:, 0:D], h_hi[u][:, cc, rows_of[s]], wh, start=(cc == 0), stop=False)
                            for s in range(2):
                                pe.matmul(psY[s][:, 0:D], h_hi[u][:, cc, rows_of[s]], wl, start=False, stop=False)
                            for s in range(2):
                                ins = pe.matmul(psY[s][:, 0:D], h_lo[u][:, cc, rows_of[s]], wh, start=False, stop=(cc == FC - 1))
                        ins.then_inc(down_psum.sem, 1)

                    turn(*tile(0, 0))
                    turn(*tile(0, 1))
                    up(*tile(0, 0), expert(0))
                    turn(*tile(0, 2))
                    up(*tile(0, 1), expert(1))
                    with pe.Fori(0, LAST) as t:
                        for k in range(TURN):
                            if k % GROUP == 0:
                                e = experts(pe, t * (TURN // GROUP) + k // GROUP)
                            turn(*tile(t, k + 3))
                            up(*tile(t, k + 2), e[k % GROUP + 2])
                            down(*tile(t, k), e[k % GROUP])
                    for k in range(TURN):
                        if k + 3 < TURN:
                            turn(*tile(LAST, k + 3))
                        if k + 2 < TURN:
                            up(*tile(LAST, k + 2), expert(LAST * TURN + k + 2))
                        down(*tile(LAST, k), expert(LAST * TURN + k))

                @block.scalar
                def _(act):
                    act.sem_inc(xT16_ready.sem, xT16_ready.start)
                    act.sem_inc(gelu_ready.sem, gelu_ready.start)
                    act.sem_inc(y_ready.sem, y_ready.start)

                    def expert(n):
                        return act.value_load(tile_tab[0:1, 0, bass.ds(n, 1)], min_val=0, max_val=E - 1)

                    def gelu(n, h, q, e):
                        u = q % 2
                        for part in range(2):
                            act.wait_ge(up_psum.sem, up_psum.done(n, part))
                            act.wait_ge(h_ready.sem, h_ready.free(n, 2, part))
                            apart(act)
                            for cc in range(2 * part, 2 * part + 2):
                                ins = act.activation(act_h[u][:, cc, :], psU[u][:, cc, :], ACT.Gelu,
                                                     bias=b1T[:, bass.ds(e * FC + cc, 1)], scale=unscale[:, 0:1])
                            ins.then_inc(gelu_ready.sem, 1)

                    def copy_rows(n, h, q):
                        u = q % 2
                        act.wait_ge(turned.sem, turned.done(n))
                        act.wait_ge(up_psum.sem, up_psum.free(n, 2))
                        act.activation(xT16[u][:].bitcast(F32), psX[u][:].bitcast(F32), ACT.Copy).then_inc(xT16_ready.sem, 1)

                    def weigh(n, h, q):
                        u = q % 2
                        act.wait_ge(down_psum.sem, down_psum.done(n))
                        act.wait_ge(meta_ready.sem, meta_ready.done(n))
                        act.wait_ge(y_sent.sem, y_sent.free(n, GROUP))
                        for s in range(2):
                            ins = act.activation(y[q][:, s, :], psY[s][:, 0:D], ACT.Copy, scale=meta[q][:, 2 * s + 1:2 * s + 2])
                        ins.then_inc(y_ready.sem, 1)

                    copy_rows(*tile(0, 0))
                    copy_rows(*tile(0, 1))
                    gelu(*tile(0, 0), expert(0))
                    copy_rows(*tile(0, 2))
                    gelu(*tile(0, 1), expert(1))
                    with act.Fori(0, LAST) as t:
                        for k in range(TURN):
                            if k % GROUP == 0:
                                e = experts(act, t * (TURN // GROUP) + k // GROUP)
                            copy_rows(*tile(t, k + 3))
                            gelu(*tile(t, k + 2), e[k % GROUP + 2])
                            weigh(*tile(t, k))
                    for k in range(TURN):
                        if k + 3 < TURN:
                            copy_rows(*tile(LAST, k + 3))
                        if k + 2 < TURN:
                            gelu(*tile(LAST, k + 2), expert(LAST * TURN + k + 2))
                        weigh(*tile(LAST, k))

                @block.vector
                def _(v):
                    v.sem_inc(match_ready.sem, match_ready.start)
                    v.sem_inc(h_ready.sem, h_ready.start)
                    v.sem_inc(meta_ready.sem, meta_ready.start)

                    def split(n, h, q, c):
                        u = q % 2
                        v.wait_ge(down_psum.sem, down_psum.free(n, 2))
                        for part in range(2):
                            v.wait_ge(gelu_ready.sem, gelu_ready.done(n, part))
                            s = slice(2 * part, 2 * part + 2)
                            v.tensor_scalar(h_hi[u][:, s, :], act_h[u][:, s, :], scales[:, 2:3], None, ALU.mult).then_inc(c.sem, c.step())
                            v.wait_ge(c.sem, c.now())
                            v.scalar_tensor_tensor(h_lo[u][:, s, :], act_h[u][:, s, :], scales[:, 2:3], h_hi[u][:, s, :],
                                                   ALU.mult, ALU.subtract).then_inc(h_ready.sem, 1)

                    def head(n, h, q):
                        v.wait_ge(rows_in[q], h * 16 + 16)
                        v.scalar_tensor_tensor(match[q][:], rows2[q][:, :, EXPERT:DEST], tile_e[:, bass.ds(n, 1)],
                                               rows2[q][:, :, DEST:WEIGHT + K], ALU.is_equal, ALU.mult)\
                            .then_inc(match_ready.sem, 1)

                    def choice(n, q, c):
                        v.wait_ge(y_sent.sem, y_sent.free(n, GROUP))
                        v.wait_ge(match_ready.sem, match_ready.done(n))
                        v.tensor_reduce(meta[q][:], match[q][:].rearrange("p s (a k) -> p (s a) k", k=K), AX.X, ALU.add).then_inc(c.sem, c.step())
                        v.wait_ge(c.sem, c.now())
                        v.tensor_scalar(back[q][:], meta[q][:, 0:4:2], float(NO_ROW), None, ALU.add).then_inc(meta_ready.sem, 1)

                    def split_and_choose(n, h, q):
                        c = Chain(tile_steps, n * TSTEPS, TSTEPS)
                        split(n, h, q, c)
                        choice(n, q, c)
                        c.end()

                    head(*tile(0, 0))
                    head(*tile(0, 1))
                    with v.Fori(0, LAST) as t:
                        for k in range(TURN):
                            head(*tile(t, k + 2))
                            split_and_choose(*tile(t, k))
                    for k in range(TURN):
                        if k + 2 < TURN:
                            head(*tile(LAST, k + 2))
                        split_and_choose(*tile(LAST, k))

                @block.gpsimd
                def _(pool):
                    pool.sem_inc(y_sent.sem, y_sent.start)
                    last_row = pool.alloc_register("last_row")
                    pool.reg_mov(last_row, TOKENS * K - 1)
                    limit = pool.snap(last_row)

                    def send(n, h, q):
                        pool.wait_ge(y_ready.sem, y_ready.done(n))
                        apart(pool)
                        for s in range(2):
                            pool.indirect_dma_start(
                                expert_out[:, :], bass.IndirectOffsetOnAxis(ap=back[q][:, s:s + 1], axis=0),
                                y[q][:, s, :], None, bounds_check=limit, oob_is_err=False).then_inc(returned[q].sem, 16)

                    def landed(n, h, q):
                        pool.wait_ge(returned[q].sem, returned[q].done(h))
                        pool.sem_inc(y_sent.sem, 1)

                    for k in range(3):
                        send(*tile(0, k))
                    with pool.Fori(0, LAST) as t:
                        for k in range(TURN):
                            send(*tile(t, k + 3))
                            landed(*tile(t, k))
                    for k in range(TURN):
                        if k + 3 < TURN:
                            send(*tile(LAST, k + 3))
                        landed(*tile(LAST, k))

        with ExitStack() as three:
            def s3(name, shape, dt=F32):
                return sb(name, shape, dt, three)

            picks = [s3(f"picks{q}", [P, BT, K, D]) for q in range(4)]
            z = [s3(f"z{u}", [P, PT, D]) for u in range(2)]
            zn = [s3(f"zn{u}", [P, PT, D]) for u in range(2)]
            zo = [s3(f"zo{u}", [P, PT, D]) for u in range(2)]
            zstats = s3("zstats", [P, PT, 6])
            zscr = s3("zscr", [P, 6, PT])
            ln4 = [s3(f"ln4_{u}", [P, 2, PT]) for u in range(2)]
            psS = [pb(f"psS{q}", [P, BT, D], F32, three) for q in range(4)]

            picks_in = [sem(f"picks_in{q}") for q in range(4)]
            sum_psum = Signal(sem("sum_psum"), credit=4)
            z_ready = Signal(sem("z_ready"), credit=4)
            ln4_ready = Signal(sem("ln4_ready"))
            zn_ready = Signal(sem("zn_ready"), credit=2, per=2)
            zo_ready = Signal(sem("zo_ready"), credit=2, per=2)
            stored = [Signal(sem(f"stored{u}"), credit=1, per=32) for u in range(2)]
            z_steps = sem("z_steps")
            expert_tiles = expert_out[:, :].rearrange("(j p k) d -> p j k d", p=P, k=K)

            with nc.Block() as block:
                @block.sync
                def _(sp):
                    with sp.Fori(0, NB // 4) as h:
                        for q in range(4):
                            sp.wait_ge(sum_psum.sem, sum_psum.free(h * 4 + q, 4))
                            sp.dma_start(picks[q][:], expert_tiles[:, bass.ds(h * NB + q * BT, BT)]).then_inc(picks_in[q], 16)

                @block.tensor
                def _(pe):
                    pe.sem_inc(sum_psum.sem, sum_psum.start)
                    with pe.Fori(0, NB // 4) as h:
                        for q in range(4):
                            pe.wait_ge(picks_in[q], h * 16 + 16)
                            pe.wait_ge(z_ready.sem, z_ready.free(h * 4 + q, 4))
                            for k in range(K):
                                ins = pe.matmul(psS[q][:], ident[:], picks[q][:, :, k, :], start=(k == 0), stop=(k == K - 1))
                            ins.then_inc(sum_psum.sem, 1)

                @block.vector
                def _(v):
                    v.sem_inc(z_ready.sem, z_ready.start)
                    STEPS = NORM_STEPS
                    with v.Fori(0, PAIRS // 2) as h:
                        for u in range(2):
                            i = h * 2 + u
                            c = Chain(z_steps, i * STEPS, STEPS)
                            v.wait_ge(zn_ready.sem, zn_ready.free(i, 2))
                            for b in range(2):
                                q = 2 * u + b
                                v.wait_ge(sum_psum.sem, sum_psum.done(i * 2 + b))
                                v.tensor_tensor(z[u][:, b * BT:(b + 1) * BT, :], psS[q][:],
                                                R[:, bass.ds(i * PT + b * BT, BT), :], ALU.add).then_inc(z_ready.sem, 1)
                                v.wait_ge(z_ready.sem, z_ready.done(i * 2 + b))
                                for j in range(b * BT, (b + 1) * BT):
                                    ins = v.bn_stats(zstats[:, j, :], z[u][:, j, :])
                            ins.then_inc(c.sem, c.step())
                            norm_steps(v, c, zstats, ln4[u][:, 0, :], ln4[u][:, 1, :], zscr, ln4_ready.sem)
                            c.end()

                @block.scalar
                def _(act):
                    act.sem_inc(zn_ready.sem, zn_ready.start)
                    with act.Fori(0, PAIRS // 2) as h:
                        for u in range(2):
                            i = h * 2 + u
                            act.wait_ge(ln4_ready.sem, ln4_ready.done(i))
                            act.wait_ge(zo_ready.sem, zo_ready.free(i, 2))
                            for b in range(2):
                                for j in range(b * BT, (b + 1) * BT):
                                    ins = act.activation(zn[u][:, j, :], z[u][:, j, :], ACT.Identity,
                                                         bias=ln4[u][:, 1, j:j + 1], scale=ln4[u][:, 0, j:j + 1])
                                ins.then_inc(zn_ready.sem, 1)
                            for b in range(2):
                                act.wait_ge(zo_ready.sem, zo_ready.done(i, b))
                                act.dma_start(out_tiles[:, bass.ds(i * PT + b * BT, BT), :], zo[u][:, b * BT:(b + 1) * BT, :])\
                                   .then_inc(stored[u].sem, 16)
                    for u in range(2):
                        act.wait_ge(stored[u].sem, stored[u].done(PAIRS // 2 - 1))

                @block.gpsimd
                def _(pool):
                    pool.sem_inc(zo_ready.sem, zo_ready.start)
                    for u in range(2):
                        pool.sem_inc(stored[u].sem, stored[u].start)
                    with pool.Fori(0, PAIRS // 2) as h:
                        for u in range(2):
                            i = h * 2 + u
                            pool.wait_ge(stored[u].sem, stored[u].free(h, 1))
                            for b in range(2):
                                pool.wait_ge(zn_ready.sem, zn_ready.done(i, b))
                                half = slice(b * BT, (b + 1) * BT)
                                pool.tensor_tensor(zo[u][:, half, :], zn[u][:, half, :], X[:, bass.ds(i * PT + b * BT, BT), :],
                                                   ALU.add).then_inc(zo_ready.sem, 1)



_INS = ['L0_attn_x', 'L0_attn_W1', 'L0_attn_b1', 'L0_attn_w2', 'L0_attn_b2', 'L0_attn_Wc', 'L0_attn_bc', 'L0_ffn_keys',
        'L0_ffn_w1', 'L0_ffn_b1', 'L0_ffn_w2', 'L0_ffn_b2', 'L0_ffn_rw', 'L0_ffn_rb']
_OUTS = [((NB, T, D), 'float32')]


def kernel(**inputs):
    import numpy as _np
    import concourse.bacc as _bacc
    from concourse import mybir as _mybir
    from concourse.bass_utils import run_bass_kernel_spmd as _run

    nc = _bacc.Bacc("TRN2", target_bir_lowering=False, num_devices=1)
    arrays, args = {}, []
    for name in _INS:
        a = _np.ascontiguousarray(inputs[name])
        arrays[f"in_{name}_dram"] = a
        args.append(nc.dram_tensor(f"in_{name}_dram", a.shape, _mybir.dt.from_np(a.dtype), kind="ExternalInput").ap())
    for i, (shape, dtype) in enumerate(_OUTS):
        dt = _mybir.dt.from_np(_np.dtype(dtype))
        args.append(nc.dram_tensor(f"out_{i}_dram", shape, dt, kind="ExternalOutput").ap())
    build(nc, *args)
    r = _run(nc, [arrays], core_ids=[0])
    got = tuple(r.results[0][f"out_{i}_dram"] for i in range(len(_OUTS)))
    return got[0]
```
